# Optimizing a Trainium2 kernel written in Bass

```python
import numpy as np
import jax
import jax.numpy as jnp

def _softmax(x, axis=-1):
    return jax.nn.softmax(x, axis=axis)

def _gelu(x):
    return jax.nn.gelu(x, approximate=True)

def _silu(x):
    return jax.nn.silu(x)

def _sigmoid(x):
    return jax.nn.sigmoid(x)

def _layernorm(x, axis=-1, eps=1e-05):
    m = jnp.mean(x, axis=axis, keepdims=True)
    v = jnp.var(x, axis=axis, keepdims=True)
    return (x - m) / jnp.sqrt(v + eps)

def _scatter_add(tgt, idx, src, axis=0):
    return tgt.at[idx].add(src)

def _segment_sum(src, seg, n):
    return jax.ops.segment_sum(src, seg, n)
kernel_name = 'mk_adaln_attn_ffn_d2_seqx_r8_06bd6d'

def setup_inputs(seed: int=0):
    np.random.seed(seed)
    _w = jnp.asarray

    def _rec_inputs():
        import jax
        import jax.numpy as jnp
        _rk = jax.random.key(seed)
        x = -0.000125 + 0.9999 * jax.random.normal(jax.random.fold_in(_rk, 1), (128, 32, 128), jnp.float32)
        _lenS = 32 - jax.random.randint(jax.random.fold_in(_rk, 7), (128,), 0, max(1, 32 // 4) + 1, jnp.int32)
        _lenS2 = 32 - jax.random.randint(jax.random.fold_in(_rk, 8), (128,), 0, max(1, 32 // 4) + 1, jnp.int32)
        cond_512 = 0.0061147 + 1.02565 * jax.random.normal(jax.random.fold_in(_rk, 11), (128, 64), jnp.float32)
        return (x, cond_512)
    x, cond_512 = _rec_inputs()

    def _L0_cond_setup():
        import jax, jax.numpy as jnp
        import numpy as np
        B, S, D, H, C = (8, 512, 128, 32, 64)
        INIT_RANGE = 0.01
        key = jax.random.key(seed)
        ks = jax.random.split(key, 6)
        return {'hidden_states': jax.random.normal(ks[0], (B, S, D), dtype=jnp.float32), 'conditions': jax.random.normal(ks[1], (B, C), dtype=jnp.float32), 'down_project': jax.random.normal(ks[2], (D, H), dtype=jnp.float32) * INIT_RANGE, 'down_gamma': jax.random.normal(ks[3], (C, H), dtype=jnp.float32), 'down_beta': jnp.zeros((C, H), dtype=jnp.float32), 'up_project': jax.random.normal(ks[4], (H, D), dtype=jnp.float32) * INIT_RANGE, 'up_gamma': jax.random.normal(ks[5], (C, D), dtype=jnp.float32), 'up_beta': jnp.zeros((C, D), dtype=jnp.float32)}
    _L0_cond_all = _L0_cond_setup()
    _L0_cond_in = {k: v for k, v in _L0_cond_all.items() if k in ('down_project', 'down_gamma', 'down_beta', 'up_project', 'up_gamma', 'up_beta')}
    del _L0_cond_all

    def _L0_attn_setup():
        import jax, jax.numpy as jnp
        import numpy as np
        B, N, D = (4, 256, 128)
        H, HD = (16, 64)
        MAX_SEQ = 512
        INNER = H * HD

        def _rope_tables(n, head_dim):
            inv_freq = 1.0 / 10000.0 ** (jnp.arange(0, head_dim, 2, dtype=jnp.float32) / head_dim)
            pos = jnp.arange(n, dtype=jnp.float32)
            ang = pos[:, None] * inv_freq[None, :]
            return (jnp.sin(ang), jnp.cos(ang))
        key = jax.random.key(seed)
        ks = jax.random.split(key, 5)
        s = 0.02
        return {'x': jax.random.normal(ks[0], (B, N, D), dtype=jnp.float32), 'ln_gamma': jnp.ones((D,), jnp.float32), 'ln_beta': jnp.zeros((D,), jnp.float32), 'w_qkv': jax.random.normal(ks[1], (D, 3 * INNER), dtype=jnp.float32) * s, 'w_out': jax.random.normal(ks[2], (INNER, D), dtype=jnp.float32) * s, 'b_out': jnp.zeros((D,), jnp.float32)}
    _L0_attn_all = _L0_attn_setup()
    _L0_attn_in = {k: v for k, v in _L0_attn_all.items() if k in ('ln_gamma', 'ln_beta', 'w_qkv', 'w_out', 'b_out')}
    del _L0_attn_all

    def _L0_cond2_setup():
        import jax, jax.numpy as jnp
        import numpy as np
        W_DIM = 64
        CLAMP = 256.0
        key = jax.random.key(seed)
        ks = jax.random.split(key, 6)
        B, L, C = (8, 1024, 128)
        return {'x': jax.random.normal(ks[0], (B, L, C), dtype=jnp.float32), 'w': jax.random.normal(ks[1], (B, W_DIM), dtype=jnp.float32), 'weight': jax.random.normal(ks[2], (C, C), dtype=jnp.float32), 'bias': jax.random.normal(ks[3], (C,), dtype=jnp.float32), 'affine_w': jax.random.normal(ks[4], (C, W_DIM), dtype=jnp.float32), 'affine_b': jnp.ones((C,), dtype=jnp.float32)}
    _L0_cond2_all = _L0_cond2_setup()
    _L0_cond2_in = {k: v for k, v in _L0_cond2_all.items() if k in ('weight', 'bias', 'affine_w', 'affine_b')}
    del _L0_cond2_all

    def _L0_ffn_setup():
        import jax, jax.numpy as jnp
        import numpy as np
        D_MODEL = 128
        NUM_EXPERTS = 8
        HIDDEN = 256
        TOP_K = 2
        SHARED_HIDDEN = 256
        BATCH, SEQ = (4, 256)
        key = jax.random.key(seed)
        ks = jax.random.split(key, 8)
        s = 1.0 / np.sqrt(D_MODEL)
        sh = 1.0 / np.sqrt(HIDDEN)
        return {'x': jax.random.normal(ks[0], (BATCH, SEQ, D_MODEL), dtype=jnp.float32), 'w_router': jax.random.normal(ks[1], (D_MODEL, NUM_EXPERTS), dtype=jnp.float32) * s, 'w1': jax.random.normal(ks[2], (NUM_EXPERTS, D_MODEL, HIDDEN), dtype=jnp.float32) * s, 'w3': jax.random.normal(ks[3], (NUM_EXPERTS, D_MODEL, HIDDEN), dtype=jnp.float32) * s, 'w2': jax.random.normal(ks[4], (NUM_EXPERTS, HIDDEN, D_MODEL), dtype=jnp.float32) * sh, 'ws1': jax.random.normal(ks[5], (D_MODEL, SHARED_HIDDEN), dtype=jnp.float32) * s, 'ws3': jax.random.normal(ks[6], (D_MODEL, SHARED_HIDDEN), dtype=jnp.float32) * s, 'ws2': jax.random.normal(ks[7], (SHARED_HIDDEN, D_MODEL), dtype=jnp.float32) * sh}
    _L0_ffn_all = _L0_ffn_setup()
    _L0_ffn_in = {k: v for k, v in _L0_ffn_all.items() if k in ('w_router', 'w1', 'w3', 'w2', 'ws1', 'ws3', 'ws2')}
    del _L0_ffn_all

    def _L1_cond_setup():
        import jax, jax.numpy as jnp
        import numpy as np
        import math
        HEAD_NUM = 16
        EPS = 1e-08

        def modulated_linear(x, s, aff_w, aff_b, w, b):
            style = s @ aff_w.T + aff_b
            w_mod = w[None, :, :] * style[:, None, :]
            demod = jax.lax.rsqrt(jnp.sum(w_mod * w_mod, axis=2) + EPS)
            w_mod = w_mod * demod[:, :, None]
            return jnp.einsum('bni,boi->bno', x, w_mod) + b
        key = jax.random.key(seed)
        ks = jax.random.split(key, 6)
        B, N, F, S = (8, 128, 128, 64)
        return {'x': jax.random.normal(ks[0], (B, N, F), dtype=jnp.float32), 's': jax.random.normal(ks[1], (B, S), dtype=jnp.float32), 'k_aff_w': jax.random.normal(ks[2], (F, S), dtype=jnp.float32) * 0.02, 'k_aff_b': jnp.ones((F,), dtype=jnp.float32), 'k_w': jax.random.normal(ks[3], (F, F), dtype=jnp.float32) * 0.02, 'k_b': jnp.zeros((F,), dtype=jnp.float32), 'o_aff_w': jax.random.normal(ks[4], (F, S), dtype=jnp.float32) * 0.02, 'o_aff_b': jnp.ones((F,), dtype=jnp.float32), 'o_w': jax.random.normal(ks[5], (F, F), dtype=jnp.float32) * 0.02, 'o_b': jnp.zeros((F,), dtype=jnp.float32)}
    _L1_cond_all = _L1_cond_setup()
    _L1_cond_in = {k: v for k, v in _L1_cond_all.items() if k in ('k_aff_w', 'k_aff_b', 'k_w', 'k_b', 'o_aff_w', 'o_aff_b', 'o_w', 'o_b')}
    del _L1_cond_all

    def _L1_attn_setup():
        import jax, jax.numpy as jnp
        import numpy as np
        import math
        B, N, D = (2, 256, 128)
        H = 16
        DH = D // H
        CG_ITERS = 30
        THRESHOLD = 0.99
        LAMBDA_INIT = 1.0
        LAMBDA_LOWER = 0.25
        NORM_EPS = 1e-05

        def l2norm(x, eps=1e-06):
            return x * jax.lax.rsqrt(jnp.sum(x * x, axis=-1, keepdims=True) + eps)

        def cg_solve(A, rhs, n_iters):
            x0 = jnp.zeros_like(rhs)
            rs0 = jnp.sum(rhs * rhs, axis=-1)

            def step(carry, _):
                x, r, p, rs = carry
                Ap = jnp.einsum('bhij,bhj->bhi', A, p)
                alpha = rs / (jnp.sum(p * Ap, axis=-1) + 1e-12)
                x = x + alpha[..., None] * p
                r = r - alpha[..., None] * Ap
                rs_new = jnp.sum(r * r, axis=-1)
                p = r + (rs_new / (rs + 1e-12))[..., None] * p
                return ((x, r, p, rs_new), None)
            (x, _, _, _), _ = jax.lax.scan(step, (x0, rhs, rhs, rs0), None, length=n_iters)
            return x
        key = jax.random.key(seed)
        ks = jax.random.split(key, 10)
        std = 0.02
        inp = {'x': jax.random.normal(ks[0], (B, N, D), dtype=jnp.float32), 'Wq': jax.random.normal(ks[1], (D, D), dtype=jnp.float32) * std, 'Wk': jax.random.normal(ks[2], (D, D), dtype=jnp.float32) * std, 'Wv': jax.random.normal(ks[3], (D, D), dtype=jnp.float32) * std, 'Wf': jax.random.normal(ks[4], (D, H), dtype=jnp.float32) * std, 'Wbet': jax.random.normal(ks[5], (D, H), dtype=jnp.float32) * std, 'Wo': jax.random.normal(ks[6], (D, D), dtype=jnp.float32) * std, 'delta': jnp.full((H,), math.log(THRESHOLD / (1.0 - THRESHOLD)), dtype=jnp.float32), 'lamb_params': jnp.full((D,), math.log(math.exp(math.exp(LAMBDA_INIT - LAMBDA_LOWER)) - 1.0), dtype=jnp.float32), 'norm_weight': jnp.ones((D,), dtype=jnp.float32), 'gate_w1': jax.random.normal(ks[7], (D, DH), dtype=jnp.float32) * std, 'gate_w2': jax.random.normal(ks[8], (DH, D), dtype=jnp.float32) * std}
        return inp
    _L1_attn_all = _L1_attn_setup()
    _L1_attn_in = {k: v for k, v in _L1_attn_all.items() if k in ('Wq', 'Wk', 'Wv', 'Wf', 'Wbet', 'Wo', 'delta', 'lamb_params', 'norm_weight', 'gate_w1', 'gate_w2')}
    del _L1_attn_all

    def _L1_cond2_setup():
        import jax, jax.numpy as jnp
        import numpy as np
        IN_DIM = 128
        OUT_DIM = 128
        MU_DIM = 64
        K = 30
        key = jax.random.key(seed)
        k1, k2, k3, k4, k5 = jax.random.split(key, 5)
        B, S = (16, 256)
        x = jax.random.normal(k1, (B, S, IN_DIM), dtype=jnp.float32)
        mu = jax.random.normal(k2, (B, MU_DIM), dtype=jnp.float32)
        W_dec = jax.random.normal(k3, (MU_DIM, (IN_DIM + 1) * K), dtype=jnp.float32) / np.sqrt(MU_DIM)
        b_dec = jax.random.normal(k4, ((IN_DIM + 1) * K,), dtype=jnp.float32) * 0.01
        V = jax.random.normal(k5, (K, OUT_DIM), dtype=jnp.float32) / np.sqrt(K)
        return {'x': x, 'mu': mu, 'W_dec': W_dec, 'b_dec': b_dec, 'V': V}
    _L1_cond2_all = _L1_cond2_setup()
    _L1_cond2_in = {k: v for k, v in _L1_cond2_all.items() if k in ('W_dec', 'b_dec', 'V')}
    del _L1_cond2_all

    def _L1_ffn_setup():
        import jax, jax.numpy as jnp
        import numpy as np
        DIM = 128
        HIDDEN = 256
        N_EXPERTS = 8
        TOP_K = 2
        EPS = 1e-06

        def rms_norm(x, scale, eps=EPS):
            ms = jnp.mean(jnp.square(x.astype(jnp.float32)), axis=-1, keepdims=True)
            s = scale.astype(jnp.float32) * jax.lax.rsqrt(ms + eps)
            return x * s.astype(x.dtype)

        def moe_linear(xf, ids, W):
            E = W.shape[0]
            out = jnp.zeros((xf.shape[0], W.shape[1]), dtype=xf.dtype)
            for e in range(E):
                out = out + jnp.where((ids == e)[:, None], xf @ W[e].T, 0.0)
            return out
        key = jax.random.key(seed)
        k1, k2, k3, k4 = jax.random.split(key, 4)
        x = jax.random.normal(k1, (4, 512, DIM), dtype=jnp.float32)
        norm_scale = jnp.ones((DIM,), dtype=jnp.float32)
        w_router = jax.random.normal(k2, (N_EXPERTS, DIM), dtype=jnp.float32) / np.sqrt(DIM)
        lim_up = np.sqrt(6.0 / (DIM + 2 * HIDDEN))
        w_up = jax.random.uniform(k3, (N_EXPERTS, 2 * HIDDEN, DIM), dtype=jnp.float32, minval=-lim_up, maxval=lim_up)
        lim_dn = np.sqrt(6.0 / (HIDDEN + DIM))
        w_down = jax.random.uniform(k4, (N_EXPERTS, DIM, HIDDEN), dtype=jnp.float32, minval=-lim_dn, maxval=lim_dn)
        return {'x': x, 'norm_scale': norm_scale, 'w_router': w_router, 'w_up': w_up, 'w_down': w_down}
    _L1_ffn_all = _L1_ffn_setup()
    _L1_ffn_in = {k: v for k, v in _L1_ffn_all.items() if k in ('norm_scale', 'w_router', 'w_up', 'w_down')}
    del _L1_ffn_all
    return {'x': x, 'cond_512': cond_512, 'L0_cond_down_project': _L0_cond_in['down_project'], 'L0_cond_down_gamma': _L0_cond_in['down_gamma'], 'L0_cond_down_beta': _L0_cond_in['down_beta'], 'L0_cond_up_project': _L0_cond_in['up_project'], 'L0_cond_up_gamma': _L0_cond_in['up_gamma'], 'L0_cond_up_beta': _L0_cond_in['up_beta'], 'L0_attn_ln_gamma': _L0_attn_in['ln_gamma'], 'L0_attn_ln_beta': _L0_attn_in['ln_beta'], 'L0_attn_w_qkv': _L0_attn_in['w_qkv'], 'L0_attn_w_out': _L0_attn_in['w_out'], 'L0_attn_b_out': _L0_attn_in['b_out'], 'L0_cond2_weight': _L0_cond2_in['weight'], 'L0_cond2_bias': _L0_cond2_in['bias'], 'L0_cond2_affine_w': _L0_cond2_in['affine_w'], 'L0_cond2_affine_b': _L0_cond2_in['affine_b'], 'L0_ffn_w_router': _L0_ffn_in['w_router'], 'L0_ffn_w1': _L0_ffn_in['w1'], 'L0_ffn_w3': _L0_ffn_in['w3'], 'L0_ffn_w2': _L0_ffn_in['w2'], 'L0_ffn_ws1': _L0_ffn_in['ws1'], 'L0_ffn_ws3': _L0_ffn_in['ws3'], 'L0_ffn_ws2': _L0_ffn_in['ws2'], 'L1_cond_k_aff_w': _L1_cond_in['k_aff_w'], 'L1_cond_k_aff_b': _L1_cond_in['k_aff_b'], 'L1_cond_k_w': _L1_cond_in['k_w'], 'L1_cond_k_b': _L1_cond_in['k_b'], 'L1_cond_o_aff_w': _L1_cond_in['o_aff_w'], 'L1_cond_o_aff_b': _L1_cond_in['o_aff_b'], 'L1_cond_o_w': _L1_cond_in['o_w'], 'L1_cond_o_b': _L1_cond_in['o_b'], 'L1_attn_Wq': _L1_attn_in['Wq'], 'L1_attn_Wk': _L1_attn_in['Wk'], 'L1_attn_Wv': _L1_attn_in['Wv'], 'L1_attn_Wf': _L1_attn_in['Wf'], 'L1_attn_Wbet': _L1_attn_in['Wbet'], 'L1_attn_Wo': _L1_attn_in['Wo'], 'L1_attn_delta': _L1_attn_in['delta'], 'L1_attn_lamb_params': _L1_attn_in['lamb_params'], 'L1_attn_norm_weight': _L1_attn_in['norm_weight'], 'L1_attn_gate_w1': _L1_attn_in['gate_w1'], 'L1_attn_gate_w2': _L1_attn_in['gate_w2'], 'L1_cond2_W_dec': _L1_cond2_in['W_dec'], 'L1_cond2_b_dec': _L1_cond2_in['b_dec'], 'L1_cond2_V': _L1_cond2_in['V'], 'L1_ffn_norm_scale': _L1_ffn_in['norm_scale'], 'L1_ffn_w_router': _L1_ffn_in['w_router'], 'L1_ffn_w_up': _L1_ffn_in['w_up'], 'L1_ffn_w_down': _L1_ffn_in['w_down']}

def reference(x, cond_512, L0_cond_down_project, L0_cond_down_gamma, L0_cond_down_beta, L0_cond_up_project, L0_cond_up_gamma, L0_cond_up_beta, L0_attn_ln_gamma, L0_attn_ln_beta, L0_attn_w_qkv, L0_attn_w_out, L0_attn_b_out, L0_cond2_weight, L0_cond2_bias, L0_cond2_affine_w, L0_cond2_affine_b, L0_ffn_w_router, L0_ffn_w1, L0_ffn_w3, L0_ffn_w2, L0_ffn_ws1, L0_ffn_ws3, L0_ffn_ws2, L1_cond_k_aff_w, L1_cond_k_aff_b, L1_cond_k_w, L1_cond_k_b, L1_cond_o_aff_w, L1_cond_o_aff_b, L1_cond_o_w, L1_cond_o_b, L1_attn_Wq, L1_attn_Wk, L1_attn_Wv, L1_attn_Wf, L1_attn_Wbet, L1_attn_Wo, L1_attn_delta, L1_attn_lamb_params, L1_attn_norm_weight, L1_attn_gate_w1, L1_attn_gate_w2, L1_cond2_W_dec, L1_cond2_b_dec, L1_cond2_V, L1_ffn_norm_scale, L1_ffn_w_router, L1_ffn_w_up, L1_ffn_w_down):
    import jax
    import jax.numpy as jnp

    def _L0_cond_ref(hidden_states, conditions, down_project, down_gamma, down_beta, up_project, up_gamma, up_beta):
        import jax, jax.numpy as jnp
        import numpy as np
        B, S, D, H, C = (8, 512, 128, 32, 64)
        INIT_RANGE = 0.01
        dg = conditions @ down_gamma
        db = conditions @ down_beta
        ug = conditions @ up_gamma
        ub = conditions @ up_beta
        w_down = down_project[None, :, :] * dg[:, None, :] + db[:, None, :]
        down = jnp.einsum('bsd,bdh->bsh', hidden_states, w_down)
        act = jax.nn.relu(down)
        w_up = up_project[None, :, :] * ug[:, None, :] + ub[:, None, :]
        up = jnp.einsum('bsh,bhd->bsd', act, w_up)
        return up + hidden_states

    def _L0_attn_ref(x, ln_gamma, ln_beta, w_qkv, w_out, b_out):
        import jax, jax.numpy as jnp
        import numpy as np
        B, N, D = (4, 256, 128)
        H, HD = (16, 64)
        MAX_SEQ = 512
        INNER = H * HD

        def _rope_tables(n, head_dim):
            inv_freq = 1.0 / 10000.0 ** (jnp.arange(0, head_dim, 2, dtype=jnp.float32) / head_dim)
            pos = jnp.arange(n, dtype=jnp.float32)
            ang = pos[:, None] * inv_freq[None, :]
            return (jnp.sin(ang), jnp.cos(ang))
        b, n, d = x.shape
        mu = jnp.mean(x, axis=-1, keepdims=True)
        var = jnp.var(x, axis=-1, keepdims=True)
        xn = (x - mu) / jnp.sqrt(var + 1e-05) * ln_gamma + ln_beta
        qkv = xn @ w_qkv
        q, k, v = jnp.split(qkv, 3, axis=-1)

        def to_heads(t):
            return t.reshape(b, n, H, HD).transpose(0, 2, 1, 3)
        q, k, v = (to_heads(q), to_heads(k), to_heads(v))
        sin, cos = _rope_tables(n, HD)
        sin = sin[None, None]
        cos = cos[None, None]
        half = HD // 2

        def rotate(t):
            t1, t2 = (t[..., :half], t[..., half:])
            return jnp.concatenate([t1 * cos - t2 * sin, t2 * cos + t1 * sin], axis=-1)
        qr, kr = (rotate(q), rotate(k))
        scale = HD ** (-0.5)
        scores = jnp.einsum('bhid,bhjd->bhij', qr, kr) * scale
        probs = jax.nn.softmax(scores, axis=-1)
        out = jnp.einsum('bhij,bhjd->bhid', probs, v)
        out = out.transpose(0, 2, 1, 3).reshape(b, n, INNER)
        return out @ w_out + b_out

    def _L0_cond2_ref(x, w, weight, bias, affine_w, affine_b):
        import jax, jax.numpy as jnp
        import numpy as np
        W_DIM = 64
        CLAMP = 256.0
        B, L, C = x.shape
        gain = 1.0 / np.sqrt(W_DIM).astype(np.float32)
        styles = w @ (affine_w * gain).T + affine_b
        ws = weight[None, :, :] * styles[:, None, :]
        dcoefs = jax.lax.rsqrt(jnp.sum(ws * ws, axis=2) + 1e-08)
        xm = x * styles[:, None, :]
        y = jnp.einsum('blc,oc->blo', xm, weight)
        y = y * dcoefs[:, None, :]
        y = jnp.clip(y + bias, -CLAMP, CLAMP)
        return y

    def _L0_ffn_ref(x, w_router, w1, w3, w2, ws1, ws3, ws2):
        import jax, jax.numpy as jnp
        import numpy as np
        D_MODEL = 128
        NUM_EXPERTS = 8
        HIDDEN = 256
        TOP_K = 2
        SHARED_HIDDEN = 256
        BATCH, SEQ = (4, 256)
        orig_shape = x.shape
        xf = x.reshape(-1, D_MODEL)
        T = xf.shape[0]
        logits = xf @ w_router
        scores = jax.nn.softmax(logits, axis=-1)
        expert_weights, expert_indices = jax.lax.top_k(scores, TOP_K)
        cw = jnp.zeros((T, NUM_EXPERTS), dtype=xf.dtype)
        cw = cw.at[jnp.arange(T)[:, None], expert_indices].add(expert_weights)
        h = jax.nn.silu(jnp.einsum('td,edh->teh', xf, w1)) * jnp.einsum('td,edh->teh', xf, w3)
        y = jnp.einsum('teh,ehd->ted', h, w2)
        moe_out = jnp.einsum('te,ted->td', cw, y)
        shared = jax.nn.silu(xf @ ws1) * (xf @ ws3) @ ws2
        out = shared / (TOP_K + 1) + moe_out * (TOP_K / (TOP_K + 1))
        return out.reshape(orig_shape)

    def _L1_cond_ref(x, s, k_aff_w, k_aff_b, k_w, k_b, o_aff_w, o_aff_b, o_w, o_b):
        import jax, jax.numpy as jnp
        import numpy as np
        import math
        HEAD_NUM = 16
        EPS = 1e-08

        def modulated_linear(x, s, aff_w, aff_b, w, b):
            style = s @ aff_w.T + aff_b
            w_mod = w[None, :, :] * style[:, None, :]
            demod = jax.lax.rsqrt(jnp.sum(w_mod * w_mod, axis=2) + EPS)
            w_mod = w_mod * demod[:, :, None]
            return jnp.einsum('bni,boi->bno', x, w_mod) + b
        B, N, F = x.shape
        H = HEAD_NUM
        D = F // H
        kx = modulated_linear(x, s, k_aff_w, k_aff_b, k_w, k_b)
        kx = kx.reshape(B, N, H, D)
        q = k = v = kx
        scores = jnp.einsum('bnhd,bnjd->bnhj', q, k) / math.sqrt(D)
        A = jax.nn.softmax(scores, axis=-1)
        out = jnp.einsum('bnhj,bnjd->bnhd', A, v).reshape(B, N, F)
        out = modulated_linear(out, s, o_aff_w, o_aff_b, o_w, o_b)
        return out

    def _L1_attn_ref(x, Wq, Wk, Wv, Wf, Wbet, Wo, delta, lamb_params, norm_weight, gate_w1, gate_w2):
        import jax, jax.numpy as jnp
        import numpy as np
        import math
        B, N, D = (2, 256, 128)
        H = 16
        DH = D // H
        CG_ITERS = 30
        THRESHOLD = 0.99
        LAMBDA_INIT = 1.0
        LAMBDA_LOWER = 0.25
        NORM_EPS = 1e-05

        def l2norm(x, eps=1e-06):
            return x * jax.lax.rsqrt(jnp.sum(x * x, axis=-1, keepdims=True) + eps)

        def cg_solve(A, rhs, n_iters):
            x0 = jnp.zeros_like(rhs)
            rs0 = jnp.sum(rhs * rhs, axis=-1)

            def step(carry, _):
                x, r, p, rs = carry
                Ap = jnp.einsum('bhij,bhj->bhi', A, p)
                alpha = rs / (jnp.sum(p * Ap, axis=-1) + 1e-12)
                x = x + alpha[..., None] * p
                r = r - alpha[..., None] * Ap
                rs_new = jnp.sum(r * r, axis=-1)
                p = r + (rs_new / (rs + 1e-12))[..., None] * p
                return ((x, r, p, rs_new), None)
            (x, _, _, _), _ = jax.lax.scan(step, (x0, rhs, rhs, rs0), None, length=n_iters)
            return x
        b, n, d = x.shape
        h, dh = (H, DH)
        q = (x @ Wq).reshape(b, n, h, dh)
        k = (x @ Wk).reshape(b, n, h, dh)
        v = (x @ Wv).reshape(b, n, h, dh)
        log_f = jax.nn.log_sigmoid(x @ Wf + delta)
        beta = jax.nn.sigmoid(x @ Wbet)
        lamb = (jax.nn.softplus(lamb_params) + LAMBDA_LOWER).reshape(h, dh)
        q = l2norm(q)
        k = l2norm(k)
        diag_lamb = lamb[:, :, None] * jnp.eye(dh, dtype=x.dtype)
        qT = q.transpose(1, 0, 2, 3)
        kT = k.transpose(1, 0, 2, 3)
        vT = v.transpose(1, 0, 2, 3)
        fT = log_f.transpose(1, 0, 2)
        bT = beta.transpose(1, 0, 2)

        def step(carry, inp):
            h_kk, h_kv = carry
            qt, kt, vt, ft, bt = inp
            fexp = jnp.exp(ft)[..., None, None]
            bkt = bt[..., None] * kt
            h_kk = fexp * h_kk + jnp.einsum('bhi,bhj->bhij', bkt, kt)
            h_kv = fexp * h_kv + jnp.einsum('bhi,bhj->bhij', bkt, vt)
            A = h_kk + diag_lamb
            qs = cg_solve(A, qt, CG_ITERS)
            ot = jnp.einsum('bhi,bhij->bhj', qs, h_kv)
            return ((h_kk, h_kv), ot)
        init = (jnp.zeros((b, h, dh, dh), dtype=x.dtype), jnp.zeros((b, h, dh, dh), dtype=x.dtype))
        _, oT = jax.lax.scan(step, init, (qT, kT, vT, fT, bT))
        o = oT.transpose(1, 0, 2, 3)
        gate = jax.nn.sigmoid(x @ gate_w1 @ gate_w2).reshape(b, n, h, dh)
        og = o * gate
        og = og * jax.lax.rsqrt(jnp.mean(og * og, axis=-1, keepdims=True) + NORM_EPS)
        out = og.reshape(b, n, d) * norm_weight
        return out @ Wo

    def _L1_cond2_ref(x, mu, W_dec, b_dec, V):
        import jax, jax.numpy as jnp
        import numpy as np
        IN_DIM = 128
        OUT_DIM = 128
        MU_DIM = 64
        K = 30
        B = mu.shape[0]
        U = (mu @ W_dec + b_dec).reshape(B, IN_DIM + 1, K)
        param = jnp.einsum('bik,kj->bij', U, V)
        weight = param[:, :-1, :]
        bias = param[:, -1, :]
        out = jnp.einsum('bsd,bde->bse', x, weight)
        out = out + bias[:, None, :]
        return out

    def _L1_ffn_ref(x, norm_scale, w_router, w_up, w_down):
        import jax, jax.numpy as jnp
        import numpy as np
        DIM = 128
        HIDDEN = 256
        N_EXPERTS = 8
        TOP_K = 2
        EPS = 1e-06

        def rms_norm(x, scale, eps=EPS):
            ms = jnp.mean(jnp.square(x.astype(jnp.float32)), axis=-1, keepdims=True)
            s = scale.astype(jnp.float32) * jax.lax.rsqrt(ms + eps)
            return x * s.astype(x.dtype)

        def moe_linear(xf, ids, W):
            E = W.shape[0]
            out = jnp.zeros((xf.shape[0], W.shape[1]), dtype=xf.dtype)
            for e in range(E):
                out = out + jnp.where((ids == e)[:, None], xf @ W[e].T, 0.0)
            return out
        B, S, D = x.shape
        skip = x
        xn = rms_norm(x, norm_scale)
        scores = (xn @ w_router.T).astype(jnp.float32)
        scores_topk, idx = jax.lax.top_k(scores, TOP_K)
        weights = jax.nn.softmax(scores_topk, axis=-1)
        xf = jnp.broadcast_to(xn[..., None, :], (B, S, TOP_K, D)).reshape(-1, D)
        ids = idx.reshape(-1)
        up = moe_linear(xf, ids, w_up)
        u, gate = jnp.split(up, 2, axis=-1)
        h = u * jax.nn.silu(gate)
        down = moe_linear(h, ids, w_down)
        down = down.reshape(B, S, TOP_K, D)
        out = jnp.sum(down * weights[..., None].astype(down.dtype), axis=-2)
        return out + skip
    x = x + _L0_attn_ref(_L0_cond_ref(x, cond_512, L0_cond_down_project, L0_cond_down_gamma, L0_cond_down_beta, L0_cond_up_project, L0_cond_up_gamma, L0_cond_up_beta), L0_attn_ln_gamma, L0_attn_ln_beta, L0_attn_w_qkv, L0_attn_w_out, L0_attn_b_out)
    x = x + _L0_ffn_ref(_L0_cond2_ref(x, cond_512, L0_cond2_weight, L0_cond2_bias, L0_cond2_affine_w, L0_cond2_affine_b), L0_ffn_w_router, L0_ffn_w1, L0_ffn_w3, L0_ffn_w2, L0_ffn_ws1, L0_ffn_ws3, L0_ffn_ws2)
    x = x + _L1_attn_ref(_L1_cond_ref(x, cond_512, L1_cond_k_aff_w, L1_cond_k_aff_b, L1_cond_k_w, L1_cond_k_b, L1_cond_o_aff_w, L1_cond_o_aff_b, L1_cond_o_w, L1_cond_o_b), L1_attn_Wq, L1_attn_Wk, L1_attn_Wv, L1_attn_Wf, L1_attn_Wbet, L1_attn_Wo, L1_attn_delta, L1_attn_lamb_params, L1_attn_norm_weight, L1_attn_gate_w1, L1_attn_gate_w2)
    x = x + _L1_ffn_ref(_L1_cond2_ref(x, cond_512, L1_cond2_W_dec, L1_cond2_b_dec, L1_cond2_V), L1_ffn_norm_scale, L1_ffn_w_router, L1_ffn_w_up, L1_ffn_w_down)
    return x

_drawn_inputs = setup_inputs


def setup_inputs(seed=0):
    import zlib

    import numpy as np

    out = dict(_drawn_inputs(seed))
    spreads = {'L0_cond_down_beta': (0.0, 0.511),
     'L0_cond_up_beta': (0.0, 0.1),
     'L0_attn_ln_gamma': (1.0, 0.2),
     'L0_attn_ln_beta': (0.0, 0.286),
     'L0_attn_b_out': (0.0, 0.1),
     'L0_cond2_affine_b': (1.0, 0.2),
     'L1_cond_k_aff_b': (1.0, 0.2),
     'L1_cond_k_b': (0.0, 0.1),
     'L1_cond_o_aff_b': (1.0, 0.2),
     'L1_cond_o_b': (0.0, 0.1),
     'L1_attn_delta': (4.595119953155518, 0.6),
     'L1_attn_lamb_params': (1.9887207746505737, 0.6),
     'L1_attn_norm_weight': (1.0, 0.2),
     'L1_ffn_norm_scale': (1.0, 0.6)}
    factors = {'L0_cond_down_project': 8.0,
     'L0_cond_down_gamma': 8.0,
     'L0_cond_up_project': 5.41,
     'L0_cond_up_gamma': 6.297,
     'L1_attn_Wf': 8.0,
     'L1_attn_Wbet': 3.451,
     'L1_attn_gate_w1': 8.0,
     'L1_attn_gate_w2': 8.0,
     'L1_cond2_b_dec': 5.923,
     'L1_ffn_w_router': 4.334,
     'L1_ffn_w_up': 3.809,
     'L1_ffn_w_down': 3.773}
    for name, (base, spread) in spreads.items():
        noise = np.random.default_rng([zlib.crc32(name.encode()), seed]).standard_normal(out[name].shape)
        drawn = base * np.exp(spread * noise) if base else spread * noise
        out[name] = jnp.asarray(drawn.astype(out[name].dtype))
    for name, factor in factors.items():
        out[name] = (out[name] * factor).astype(out[name].dtype)
    return out
```

```python
from contextlib import ExitStack

import concourse.bass as bass
import numpy as np
from concourse import mybir

F32 = mybir.dt.float32
ALU = mybir.AluOpType
ACT = mybir.ActivationFunctionType
AX = mybir.AxisListType.X

P = 128
B, N, D, C = 128, 32, 128, 64
TOK = B * N
AH = 32
HEADS, HD = 16, 64
HALF = HD // 2
PAIRS = HEADS // 2
INNER = HEADS * HD
GB = P // N
TILES = TOK // P


class Steps:

    def __init__(self, sem, names):
        self.sem, self.names, self.at = sem, names.split(), 0

    def __call__(self, name):
        assert self.names[self.at % len(self.names)] == name, (name, self.names, self.at)
        self.at += 1
        return self.sem

    def done(self, name, t=0):
        return self.sem, t * len(self.names) + (self.names.index(name) + 1)


def wait_if(eng, steps, name, t):
    if not isinstance(t, int) or t >= 0:
        eng.wait_ge(*steps.done(name, t))


def attention_phase(nc, ctx, dram, x1):

    def sb(name, shape):
        return ctx.enter_context(nc.sbuf_tensor("p1_" + name, shape, F32))

    xT = sb("xT", [P, TOK])
    condT = sb("condT", [C, B])
    w_dgb = sb("w_dgb", [C, 2 * AH])
    w_ugb = sb("w_ugb", [C, 2, D])
    w_down = sb("w_down", [P, 2 * AH])
    w_up = sb("w_up", [AH, 2, D])
    fold = sb("fold", [2 * AH, AH])
    ident = sb("ident", [P, P])
    ln_gb = sb("ln_gb", [P, 2])
    b_out = sb("b_out", [P, D])
    x_in = sb("x_in", [P, 2, D])
    xb = sb("xb", [P, 2, D])
    x_out = sb("x_out", [P, 2, D])
    w_qkv = sb("w_qkv", [P, 3 * INNER])
    w_out = sb("w_out", [P, PAIRS, D])
    cos = sb("cos", [P, HD])
    sin = sb("sin", [P, HD])
    dgb = sb("dgb", [2 * AH, B])
    ugb = sb("ugb", [P, 2, B])
    half = sb("half", [P, 1])
    eps = sb("eps", [P, 1])

    gated = sb("gated", [2 * AH, P])
    act = sb("act", [AH, P])
    ups = sb("ups", [P, 2, P])
    hres = sb("hres", [P, P])
    stats = sb("stats", [P, 6])
    mv = sb("mv", [P, 2])
    veps = sb("veps", [P, 1])
    rstd = sb("rstd", [P, 1])
    xn = sb("xn", [P, P])
    xnT = sb("xnT", [P, 2, P])
    rc = sb("rc", [P, 2, INNER])
    rs = sb("rs", [P, 2, INNER])
    rot = sb("rot", [P, 2, INNER])
    qT = sb("qT", [P, PAIRS, P])
    kbd = sb("kbd", [P, PAIRS, GB, 2, N])
    v = sb("v", [P, 2, INNER])
    mx = sb("mx", [P, HEADS])
    sc = sb("sc", [P, HEADS, N])
    ex = sb("ex", [P, HEADS, N])
    sm = sb("sm", [P, HEADS])
    rsm = sb("rsm", [P, HEADS])
    pr = sb("pr", [P, HEADS, N])
    pbd = sb("pbd", [P, HEADS, P])
    oT = sb("oT", [P, PAIRS, P])

    def sem(name):
        return ctx.enter_context(nc.semaphore("p1_" + name))

    loaded = sem("loaded")
    loaded_w = sem("loaded_w")
    LOADS, LOADS_W = 13 * 16, 2 * 16
    zeroed = sem("zeroed")
    ZEROED = 6
    s_pe = Steps(sem("setup_pe"), "gates")
    s_act = Steps(sem("setup_act"), "dgb ugb")
    a_pe = Steps(sem("adapter_pe"), "down fold up sum xnT")
    a_dve = Steps(sem("adapter_dve"), "gated ups hres stats mv xn")
    a_act = Steps(sem("adapter_act"), "act xnT")
    x_read = [sem("x_read_even"), sem("x_read_odd")]
    x_written = [sem("x_written_even"), sem("x_written_odd")]
    e_pool = Steps(sem("bias_pool"), "xb")
    a_pool = Steps(sem("adapter_pool"), "veps rstd")
    b_pe = Steps(sem("qk_pe"), "q k qT kT")
    b_dve = Steps(sem("rope_dve"), "qc qs1 qs2 kc ks1 ks2")
    b_pool = Steps(sem("rope_pool"), "q k")
    b_act = Steps(sem("qk_act"), "qT k0 k1")
    c_pe = Steps(sem("scores_pe"), "scores v")
    c_act = Steps(sem("scores_act"), "v exp")
    c_dve = Steps(sem("softmax_dve"), "max sub sum rsum")
    c_pool = Steps(sem("softmax_pool"), "probs")
    d_dve = Steps(sem("out_dve"), "probsT x1")
    d_pe = Steps(sem("out_pe"), "pv y")
    d_act = Steps(sem("out_act"), "oT")

    ps = ctx.enter_context(nc.psum_tensor("p1_ps", [P, 8, 512], F32))

    def two_banks(k):
        return ps[:, k:k + 2, :].rearrange("p a b -> p (a b)")

    psX, psY, psZ = two_banks(0), two_banks(2), two_banks(4)
    psS, psA = ps[:, 6, :], ps[:, 7, :]

    block = ctx.enter_context(nc.Block())

    def pipeline(stages):

        def turn(t, u, k):
            stages(t, u, k, *(not isinstance(t, int) or 0 <= t + d < TILES for d in (2, 1, 0, -1)))

        return turn

    FIRST, LAST = 2, TILES - 2

    def run(eng, turn):
        for t in range(-2, FIRST):
            turn(t, t % 2, t // 2)
        with eng.Fori(FIRST // 2, LAST // 2) as two:
            turn(two * 2, 0, two)
            turn(two * 2 + 1, 1, two)
        for t in range(LAST, TILES + 1):
            turn(t, t % 2, t // 2)

    @block.sync
    def _(sp):
        for dst, src in ((condT, "condT"), (w_dgb, "dgb"), (w_ugb, "ugb"), (w_down[:, 0:AH], "down"),
                         (w_up[:, 0, :], "up"), (fold, "fold"), (ident, "ident"), (ln_gb, "ln_gb"),
                         (b_out, "b_out"), (cos, "cos"), (sin, "sin")):
            sp.dma_start(dst if dst.__class__ is bass.AP else dst[:], dram[src]).then_inc(loaded, 16)
        for c in range(2):
            sp.dma_start(xT[:, c * TOK // 2:(c + 1) * TOK // 2], dram["xT"][:, c * TOK // 2:(c + 1) * TOK // 2]).then_inc(loaded, 16)
        sp.dma_start(w_qkv[:], dram["w_qkv"]).then_inc(loaded_w, 16)
        sp.dma_start(w_out[:], dram["w_out"]).then_inc(loaded_w, 16)

        def turn(t, u, k, A, Bq, Cs, Do):
            if A:
                wait_if(sp, e_pool, "xb", t)
                sp.dma_start(x_in[:, u, :], dram["x"][bass.ds((t + 2) * P, P), :]).then_inc(x_read[u], 16)
            if Do:
                sp.wait_ge(*d_dve.done("x1", t - 1))
                sp.dma_start(x1[bass.ds((t - 1) * P, P), :], x_out[:, (u + 1) % 2, :]).then_inc(x_written[(u + 1) % 2], 16)

        run(sp, pipeline(turn))
        for w in x_written:
            sp.wait_ge(w, 16 * (TILES // 2))

    @block.tensor
    def _(pe):
        pe.wait_ge(loaded, LOADS)
        pe.wait_ge(loaded_w, LOADS_W)
        pe.wait_ge(zeroed, ZEROED)
        nc.tensor.matmul(psX[0:2 * AH, 0:B], w_dgb[:], condT[:], start=True, stop=True)
        for i in range(2):
            last = nc.tensor.matmul(psY[:, i * B:(i + 1) * B], w_ugb[:, i, :], condT[:], start=True, stop=True)
        last.then_inc(s_pe("gates"), 1)
        pe.wait_ge(*s_act.done("ugb"))

        def turn(t, u, k, A, Bq, Cs, Do):
            ta, tb, td = t + 2, t + 1, t - 1
            if A:
                wait_if(pe, a_act, "xnT", ta - 1)
                nc.tensor.matmul(psA[0:2 * AH, 0:P], w_down[:], xT[:, bass.ds(ta * P, P)], start=True,
                                 stop=True).then_inc(a_pe("down"), 1)
            if Bq:
                pe.wait_ge(*a_act.done("xnT", tb))
                wait_if(pe, b_act, "qT", tb - 1)
                for j in range(2):
                    last = nc.tensor.matmul(psX[:, j * 512:(j + 1) * 512], xnT[:, (u + 1) % 2, :],
                                            w_qkv[:, j * 512:(j + 1) * 512], start=True, stop=True)
                last.then_inc(b_pe("q"), 1)
            if A:
                pe.wait_ge(*a_dve.done("gated", ta))
            if Cs:
                pe.wait_ge(*b_act.done("k1", t))
                wait_if(pe, d_dve, "x1", t - 2)
                for p in range(PAIRS):
                    for b in range(GB):
                        last = nc.tensor.matmul(psS[b * N:(b + 1) * N, p * 2 * N:(p + 1) * 2 * N],
                                                qT[:, p, b * N:(b + 1) * N], kbd[:, p, b, :, :],
                                                start=True, stop=True)
                last.then_inc(c_pe("scores"), 1)
            if A:
                nc.tensor.matmul(psA[0:AH, 128:256], fold[:], gated[:], start=True, stop=True).then_inc(a_pe("fold"), 1)
            if Bq:
                wait_if(pe, b_act, "k1", tb - 1)
                for j in range(2):
                    last = nc.tensor.matmul(psY[:, j * 512:(j + 1) * 512], xnT[:, (u + 1) % 2, :],
                                            w_qkv[:, INNER + j * 512:INNER + (j + 1) * 512], start=True, stop=True)
                last.then_inc(b_pe("k"), 1)
            if A:
                pe.wait_ge(*a_act.done("act", ta))
                for i in range(2):
                    last = nc.tensor.matmul(psA[:, 256 + i * P:256 + (i + 1) * P], w_up[:, i, :], act[:],
                                            start=True, stop=True)
                last.then_inc(a_pe("up"), 1)
            if Cs:
                wait_if(pe, d_act, "oT", t - 2)
                for j in range(2):
                    last = nc.tensor.matmul(psZ[:, j * 512:(j + 1) * 512], xnT[:, u, :],
                                            w_qkv[:, 2 * INNER + j * 512:2 * INNER + (j + 1) * 512],
                                            start=True, stop=True)
                last.then_inc(c_pe("v"), 1)
            if A:
                pe.wait_ge(*a_dve.done("hres", ta))
                nc.tensor.matmul(psA[:, 0:P], hres[:], ident[:], start=True, stop=False)
                nc.tensor.matmul(psA[:, 0:P], ups[:, 1, :], ident[:], start=False, stop=True).then_inc(a_pe("sum"), 1)
            if Bq:
                pe.wait_ge(*b_pool.done("q", tb))
                for p in range(PAIRS):
                    last = nc.tensor.transpose(psX[:, p * P:(p + 1) * P], rot[:, 0, p * P:(p + 1) * P], ident[:])
                last.then_inc(b_pe("qT"), 1)
            if Do:
                pe.wait_ge(*d_dve.done("probsT", td))
                if Cs:
                    pe.wait_ge(*c_act.done("v", t))
                for h in range(HEADS):
                    last = nc.tensor.matmul(psZ[h % 2 * HD:(h % 2 + 1) * HD, h // 2 * P:(h // 2 + 1) * P],
                                            v[:, (u + 1) % 2, h * HD:(h + 1) * HD], pbd[:, h, :], start=True, stop=True)
                last.then_inc(d_pe("pv"), 1)
            if A:
                pe.wait_ge(*a_dve.done("xn", ta))
                nc.tensor.transpose(psA[:, 128:256], xn[:], ident[:]).then_inc(a_pe("xnT"), 1)
            if Bq:
                pe.wait_ge(*b_pool.done("k", tb))
                for p in range(PAIRS):
                    last = nc.tensor.transpose(psY[:, p * P:(p + 1) * P], rot[:, 1, p * P:(p + 1) * P], ident[:])
                last.then_inc(b_pe("kT"), 1)
            if Do:
                pe.wait_ge(*d_act.done("oT", td))
                if Cs:
                    pe.wait_ge(*c_dve.done("sub", t))
                for p in range(PAIRS):
                    last = nc.tensor.matmul(psS[:, 0:P], oT[:, p, :], w_out[:, p, :], start=(p == 0), stop=(p == PAIRS - 1))
                last.then_inc(d_pe("y"), 1)

        run(pe, pipeline(turn))

    @block.scalar
    def _(sc_):
        sc_.wait_ge(*s_pe.done("gates"))
        nc.scalar.activation(dgb[:], psX[0:2 * AH, 0:B], ACT.Copy).then_inc(s_act("dgb"), 1)
        nc.scalar.activation(ugb[:], psY[:, 0:2 * B].rearrange("p (i b) -> p i b", i=2), ACT.Copy).then_inc(s_act("ugb"), 1)

        def turn(t, u, k, A, Bq, Cs, Do):
            ta, tb, td = t + 2, t + 1, t - 1
            if A:
                sc_.wait_ge(*a_pe.done("fold", ta))
                wait_if(sc_, a_pe, "up", ta - 1)
                nc.scalar.activation(act[:], psA[0:AH, 128:256], ACT.Relu).then_inc(a_act("act"), 1)
            if Cs:
                sc_.wait_ge(*c_pe.done("v", t))
                wait_if(sc_, d_pe, "pv", t - 2)
                nc.scalar.activation(v[:, u, :], psZ, ACT.Copy).then_inc(c_act("v"), 1)
                sc_.wait_ge(*c_dve.done("sub", t))
                wait_if(sc_, c_pool, "probs", t - 1)
                nc.scalar.activation(ex[:], sc[:], ACT.Exp, scale=float(HD) ** -0.5).then_inc(c_act("exp"), 1)
            if Bq:
                sc_.wait_ge(*b_pe.done("qT", tb))
                nc.scalar.activation(qT[:].rearrange("p a b -> p (a b)"), psX, ACT.Copy).then_inc(b_act("qT"), 1)
            if Do:
                sc_.wait_ge(*d_pe.done("pv", td))
                wait_if(sc_, d_pe, "y", td - 1)
                nc.scalar.activation(oT[:].rearrange("p a b -> p (a b)"), psZ, ACT.Copy).then_inc(d_act("oT"), 1)
            if A:
                sc_.wait_ge(*a_pe.done("xnT", ta))
                wait_if(sc_, c_pe, "v", ta - 2)
                nc.scalar.activation(xnT[:, u, :], psA[:, 128:256], ACT.Identity, scale=ln_gb[:, 0:1],
                                     bias=ln_gb[:, 1:2]).then_inc(a_act("xnT"), 1)
            if Bq:
                sc_.wait_ge(*b_pe.done("kT", tb))
                wait_if(sc_, c_pe, "scores", tb - 1)
                for h in range(2):
                    rows = slice(h * HD, (h + 1) * HD)
                    nc.scalar.activation(kbd[rows, :, :, h, :].rearrange("p a b n -> p (a b) n"),
                                         psY[rows, :].rearrange("p (c n) -> p c n", n=N), ACT.Copy).then_inc(b_act(f"k{h}"), 1)

        run(sc_, pipeline(turn))

    @block.gpsimd
    def _(pool):
        nc.gpsimd.memset(half[:], -0.5).then_inc(zeroed, 1)
        nc.gpsimd.memset(eps[:], 1e-5).then_inc(zeroed, 1)
        nc.gpsimd.memset(w_down[:, AH:], 1.0).then_inc(zeroed, 1)
        nc.gpsimd.memset(w_up[:, 1, :], 1.0).then_inc(zeroed, 1)
        nc.gpsimd.memset(kbd[:], 0.0).then_inc(zeroed, 1)
        nc.gpsimd.memset(pbd[:], 0.0).then_inc(zeroed, 1)
        pool.wait_ge(zeroed, ZEROED)

        def turn(t, u, k, A, Bq, Cs, Do):
            ta, tb, td = t + 2, t + 1, t - 1
            if Bq:
                pool.wait_ge(*b_dve.done("qs2", tb))
                wait_if(pool, b_pe, "qT", tb - 1)
                nc.gpsimd.tensor_tensor(rot[:, 0, :], rc[:, 0, :], rs[:, 0, :], ALU.add).then_inc(b_pool("q"), 1)
            if A:
                pool.wait_ge(*a_dve.done("mv", ta))
                nc.gpsimd.tensor_tensor(veps[:], mv[:, 1:2], eps[:], ALU.add).then_inc(a_pool("veps"), 1)
                pool.wait_ge(*a_pool.done("veps", ta))
                wait_if(pool, a_dve, "xn", ta - 1)
                nc.gpsimd.tensor_tensor(rstd[:], veps[:], half[:], ALU.pow).then_inc(a_pool("rstd"), 1)
            if Bq:
                pool.wait_ge(*b_dve.done("ks2", tb))
                wait_if(pool, b_pe, "kT", tb - 1)
                nc.gpsimd.tensor_tensor(rot[:, 1, :], rc[:, 1, :], rs[:, 1, :], ALU.add).then_inc(b_pool("k"), 1)
            if Cs:
                pool.wait_ge(x_read[u], (k + 1) * 16)
                wait_if(pool, d_dve, "x1", t - 2)
                nc.gpsimd.tensor_tensor(xb[:, u, :], x_in[:, u, :], b_out[:], ALU.add).then_inc(e_pool("xb"), 1)
                pool.wait_ge(*c_dve.done("rsum", t))
                wait_if(pool, d_dve, "probsT", t - 1)
                nc.gpsimd.tensor_tensor(pr[:], ex[:], rsm[:].unsqueeze(2).broadcast_to([P, HEADS, N]),
                                        ALU.mult).then_inc(c_pool("probs"), 1)

        run(pool, pipeline(turn))

    @block.vector
    def _(dve):
        dve.wait_ge(*s_act.done("ugb"))

        def rope(t, i, psum, made, free):
            name = "qk"[i]
            dve.wait_ge(*b_pe.done(name, t))
            wait_if(dve, b_pool, name, t - 1)
            q3 = psum.rearrange("p (h f) -> p h f", f=HD)
            nc.vector.tensor_tensor(rc[:, i, :].rearrange("p (h f) -> p h f", f=HD), q3,
                                    cos[:].unsqueeze(1).broadcast_to([P, HEADS, HD]), ALU.mult).then_inc(b_dve(name + "c"), 1)
            r3 = rs[:, i, :].rearrange("p (h f) -> p h f", f=HD)
            for j in range(2):
                out, other = slice(j * HALF, (j + 1) * HALF), slice((1 - j) * HALF, (2 - j) * HALF)
                nc.vector.tensor_tensor(r3[:, :, out], q3[:, :, other],
                                        sin[:, out].unsqueeze(1).broadcast_to([P, HEADS, HALF]),
                                        ALU.mult).then_inc(b_dve(f"{name}s{j + 1}"), 1)

        def turn(t, u, k, A, Bq, Cs, Do):
            ta, tb, td = t + 2, t + 1, t - 1
            if A:
                dve.wait_ge(*a_pe.done("down", ta))
                wait_if(dve, a_pe, "fold", ta - 1)
                nc.vector.tensor_tensor(gated[:].rearrange("p (b n) -> p b n", b=GB),
                                        psA[0:2 * AH, 0:P].rearrange("p (b n) -> p b n", b=GB),
                                        dgb[:, bass.ds(ta * GB, GB)].unsqueeze(2).broadcast_to([2 * AH, GB, N]),
                                        ALU.mult).then_inc(a_dve("gated"), 1)
            if Do:
                dve.wait_ge(*c_pool.done("probs", td))
                wait_if(dve, d_pe, "pv", td - 1)
                for b in range(GB):
                    rows = slice(b * N, (b + 1) * N)
                    last = nc.vector.transpose(pbd[rows, :, rows], pr[rows, :, :])
                last.then_inc(d_dve("probsT"), 1)
            if Bq:
                rope(tb, 0, psX, None, None)
            if Cs:
                dve.wait_ge(*c_pe.done("scores", t))
                wait_if(dve, c_dve, "sub", t - 1)
                s3 = psS.rearrange("p (h n) -> p h n", n=N)
                nc.vector.tensor_reduce(mx[:], s3, AX, ALU.max).then_inc(c_dve("max"), 1)
                dve.wait_ge(*c_dve.done("max", t))
                wait_if(dve, c_act, "exp", t - 1)
                nc.vector.tensor_tensor(sc[:], s3, mx[:].unsqueeze(2).broadcast_to([P, HEADS, N]),
                                        ALU.subtract).then_inc(c_dve("sub"), 1)
            if A:
                dve.wait_ge(*a_pe.done("up", ta))
                wait_if(dve, a_pe, "sum", ta - 1)
                nc.vector.tensor_tensor(ups[:].rearrange("p i (b n) -> p i b n", b=GB),
                                        psA[:, 256:512].rearrange("p (i b n) -> p i b n", i=2, b=GB),
                                        ugb[:, :, bass.ds(ta * GB, GB)].unsqueeze(3).broadcast_to([P, 2, GB, N]),
                                        ALU.mult).then_inc(a_dve("ups"), 1)
                dve.wait_ge(*a_dve.done("ups", ta))
                nc.vector.tensor_tensor(hres[:], ups[:, 0, :], xT[:, bass.ds(ta * P, P)], ALU.add).then_inc(a_dve("hres"), 1)
            if Bq:
                rope(tb, 1, psY, None, None)
            if A:
                dve.wait_ge(*a_pe.done("sum", ta))
                nc.vector.bn_stats(stats[:], psA[:, 0:P]).then_inc(a_dve("stats"), 1)
                dve.wait_ge(*a_dve.done("stats", ta))
                wait_if(dve, a_pool, "veps", ta - 1)
            if Cs:
                dve.wait_ge(*c_act.done("exp", t))
                nc.vector.tensor_reduce(sm[:], ex[:], AX, ALU.add).then_inc(c_dve("sum"), 1)
            if A:
                nc.vector.bn_aggr(mv[:], stats[:]).then_inc(a_dve("mv"), 1)
            if Cs:
                dve.wait_ge(*c_dve.done("sum", t))
                wait_if(dve, c_pool, "probs", t - 1)
                nc.vector.reciprocal(rsm[:], sm[:]).then_inc(c_dve("rsum"), 1)
            if A:
                dve.wait_ge(*a_pool.done("rstd", ta))
                wait_if(dve, a_pe, "xnT", ta - 1)
                nc.vector.tensor_scalar(xn[:], psA[:, 0:P], mv[:, 0:1], rstd[:, 0:1], ALU.subtract,
                                        ALU.mult).then_inc(a_dve("xn"), 1)
            if Do:
                dve.wait_ge(*d_pe.done("y", td))
                dve.wait_ge(*e_pool.done("xb", td))
                if not isinstance(td, int) or td >= 2:
                    dve.wait_ge(x_written[(u + 1) % 2], (k if u else k - 1) * 16)
                nc.vector.tensor_tensor(x_out[:, (u + 1) % 2, :], psS[:, 0:P], xb[:, (u + 1) % 2, :], ALU.add).then_inc(d_dve("x1"), 1)

        run(dve, pipeline(turn))



EXPERTS, HID = 8, 256
EX0 = EXPERTS + 1
TOP_K = 2
NC = 4
CH = NC * B
CHUNKS = N // NC
H1, D1 = 16, 8
OFF = H1 // 2 + 1
KDEC = 30
SYS = NC * H1
GATES = ("styleC", "styleK", "styleO")


def mixing_phase(nc, ctx, dram, x1, out):

    def sb(name, shape):
        return ctx.enter_context(nc.sbuf_tensor("p2_" + name, shape, F32))

    def sem(name):
        return ctx.enter_context(nc.semaphore("p2_" + name))

    ident = sb("ident", [P, P])
    half = sb("half", [P, 64])
    w2c = sb("w2c", [P, D])
    vecs = sb("vecs", [P, 8])
    w_r0, w_r1 = sb("w_r0", [P, EXPERTS]), sb("w_r1", [P, EXPERTS])
    w13 = sb("w13", [P, EX0, 2, HID])
    w2 = sb("w2", [P, EX0, 2, D])
    kwT, owT = sb("kwT", [P, D]), sb("owT", [P, D])
    wqkv1 = sb("wqkv1", [P, 3, D])
    wfb = sb("wfb", [P, 2 * H1])
    wo1 = sb("wo1", [P, D])
    g1 = sb("g1", [P, D1])
    g2 = sb("g2", [D1, D])
    rows = sb("rows", [P, 4, D])
    fbias = sb("fbias", [P, 2 * H1])
    bdec = sb("bdec", [P, KDEC])
    bdecb = sb("bdecb", [KDEC, 1])
    vmat = sb("vmat", [KDEC, D])
    w_up = sb("w_up", [P, EXPERTS, 2 * HID])
    w_dn = sb("w_dn", [P, EXPERTS, 2, D])
    tri = sb("tri", [P, 2, EXPERTS * EXPERTS])
    style = sb("style", [P, 3, B])
    demod = sb("demod", [P, 3, B])
    lam = sb("lam", [P, D])
    Uw = sb("Uw", [P, KDEC, B])
    Ub = sb("Ub", [KDEC, B])

    xs = sb("xs", [P, CH])
    xm = sb("xm", [P, CH])
    yT = sb("yT", [P, CH])
    ex8 = sb("ex8", [P, NC, EXPERTS])
    s8 = sb("s8", [P, NC, EXPERTS])
    m4 = sb("m4", [P, NC])
    p8 = sb("p8", [P, NC, EXPERTS])
    ge = sb("ge", [P, NC, EXPERTS * EXPERTS])
    gt = sb("gt", [P, NC, EXPERTS * EXPERTS])
    rank = sb("rank", [P, NC, EXPERTS])
    cw0 = sb("cw0", [P, NC, EX0])
    cw1 = sb("cw1", [P, NC, EXPERTS])
    sil = sb("sil", [P, 2, CH])
    hid = sb("hid", [P, 2, CH])
    ssq = sil[:, 0, 0:3 * B].rearrange("p (i b) -> p i b", i=3)
    wsq = hid[:, 0, 0:3 * B].rearrange("p (i b) -> p i b", i=3)
    scaled = sb("scaled", [P, 2, CH])
    ltmp = scaled[:, 0, 0:D]
    x2 = sb("x2", [P, CH])
    xk = sb("xk", [P, CH])
    kx0 = sb("kx0", [P, CH])
    kx = sb("kx", [P, NC, 2, D])
    prod = sb("prod", [P, (D1 - 1) * D1 * SYS])
    sd = sb("sd", [P, NC, OFF, 2, H1])
    sf = sb("sf", [P, NC, H1, H1])
    mxh = sb("mxh", [P, NC, H1])
    smh = sb("smh", [P, NC, H1])
    rsh = sb("rsh", [P, NC, H1])
    mixed = sb("mixed", [P, CH])
    y2T = sb("y2T", [P, CH])
    sqr = mixed
    ssr = sb("ssr", [P, 2, SYS])
    rn = sb("rn", [P, 2, SYS])
    kv = sb("kv", [P, 2 * D1, SYS])
    fb0 = sb("fb0", [P, NC, 2, H1])
    fbt = sb("fbt", [P, NC, 2, H1])
    fb = sb("fb", [P, NC, 2, H1])
    bk = sb("bk", [P, D1, SYS])
    Hv = sb("Hv", [P, D1 * D1, NC, H1])
    carry = sb("carry", [P, 2, D1 * D1, H1])
    A = sb("A", [P, D1, D1 + 1, SYS])
    T = prod[:].rearrange("p (a s) -> p a s", s=SYS)
    early = A[0:C, :, :, :].rearrange("p i j s -> p (i j s)")
    WDEC, AFF = (D + 1) * KDEC, 3 * D
    wdec = early[:, 0:WDEC]
    aff = early[:, WDEC:WDEC + AFF].rearrange("c (i d) -> c i d", i=3)
    condT = early[:, WDEC + AFF:WDEC + AFF + B]
    A4 = A[:].rearrange("p i j (n h) -> p i j n h", n=NC)
    rinv = sb("rinv", [P, SYS])
    gT = sb("gT", [D1, CH])
    gate = sb("gate", [P, CH])
    o1 = sb("o1", [P, CH])
    og = kx0
    ogT = xk
    x3 = sb("x3", [P, CH])
    x3T = sb("x3T", [P, CH])
    tK = sb("tK", [KDEC, NC, B])
    z = sb("z", [P, CH])
    ms4 = sb("ms4", [P, 2, NC])
    zn = sb("zn", [P, CH])
    znT = x3T
    tiny = sb("tiny", [P, SYS])
    neps = sb("neps", [P, 3, SYS])

    loaded = sem("loaded")
    zeroed = sem("zeroed")
    S = {}
    su_pe = Steps(sem("gates_pe"), "gates sums uw")
    su_dve = Steps(sem("gates_dve"), "st0 st1 st2 ssq0 ssq1 ssq2 wsq0 wsq1 wsq2 dem0 dem1 dem2 l0 l1 l2 nw uw ub")
    su_act = Steps(sem("gates_act"), "e ln")
    su_pool = Steps(sem("gates_pool"), "dem")
    UG = [(g, min(g + 4, KDEC)) for g in range(0, KDEC, 4)]
    su_u = Steps(sem("uw_pe"), " ".join(f"g{i}" for i in range(len(UG))))
    su_v = Steps(sem("uw_dve"), " ".join(f"g{i}" for i in range(len(UG))))

    x_read = sem("x_read")
    f_pe = Steps(sem("f_pe"), "x1 y router")
    f_act = Steps(sem("f_act"), "exp")
    f_dve = Steps(sem("f_dve"), "xm dm bias yT max sub sum rsum probs ge gel gt gtu cmp rank rk2 cw")
    U0, U1 = 2 * EX0, 2 * EXPERTS
    F0 = [Steps(sem("f0_" + n), " ".join(f"{k}" for k in ks)) for n, ks in (
        ("up", [f"a{k} b{k}" for k in range(U0)]), ("silu", [f"s{k}" for k in range(U0)]),
        ("mul", [f"h{k}" for k in range(U0)]), ("down", [f"d{k}" for k in range(U0)]),
        ("scale", [f"c{e}" for e in range(EX0)]), ("acc", [f"x{e}" for e in range(EX0)]))]
    F1 = [Steps(sem("f1_" + n), " ".join(f"{k}" for k in ks)) for n, ks in (
        ("up", [f"a{k} b{k}" for k in range(U1)]), ("silu", [f"s{k}" for k in range(U1)]),
        ("mul", [f"h{k}" for k in range(U1)]), ("down", [f"d{k}" for k in range(U1)]),
        ("scale", [f"c{e}" for e in range(EXPERTS)]), ("acc", [f"x{e}" for e in range(EXPERTS)]))]
    k_pe = Steps(sem("k_pe"), "x2T kx oT y")
    k_dve = Steps(sem("k_dve"), "xk kx0 prod0 sd0 prod1 sd1 sf1 max sub sum rsum " + " ".join(f"ap{n} av{n}" for n in range(NC)) + " xo y1")
    k_pool = Steps(sem("k_pool"), "kx probs")
    k_act = Steps(sem("k_act"), "kxdup sddup sf0 exp y2T")
    m_pe = Steps(sem("m_pe"), "q k v fb g gate ogT x3")
    m_act = Steps(sem("m_act"), "sqq sqk v fbt gT gate carry ogT")
    ELIM = " ".join(f"ri{k} row{k} t{k} a{k}" if k < D1 - 1 else f"ri{k} row{k}" for k in range(D1))
    BACK = " ".join(f"bt{k} bx{k}" for k in range(D1 - 1, 0, -1))
    m_dve = Steps(sem("m_dve"), "ssq q ssk k fb0 fb bk Uk U " + " ".join(f"mk{n} mv{n} hk{n} hv{n}" for n in range(NC)) + " diag " + ELIM + " " + BACK
                  + " oprod o1 og ss ogn x3")
    m_pool = Steps(sem("m_pool"), "eq rq ek rk sq ms eps rs og2")
    g_pe = Steps(sem("g_pe"), "x3T t z znT router")
    g_act = Steps(sem("g_act"), "x3T z znT exp")
    g_dve = Steps(sem("g_dve"), "t ms " + " ".join(f"zn{n}" for n in range(NC)) + " max sub raw ge gel gt gtu cmp rank em sum rsum cw")
    g_pool = Steps(sem("g_pool"), "sq mean eps rs base")
    stored = sem("stored")

    ps = ctx.enter_context(nc.psum_tensor("p2_ps", [P, 8, 512], F32))
    psU, psDn = ps[:, 0:4, :], ps[:, 4:6, :]
    ps6, ps7 = ps[:, 6, :], ps[:, 7, :]

    def by_n(ap):
        return ap.rearrange("p (n b) -> p n b", n=NC)

    def bc_n(ap, parts=P):
        return ap.unsqueeze(1).broadcast_to([parts, NC, ap.shape[-1]])

    block = ctx.enter_context(nc.Block())
    loads = [(ident, "ident"), (condT, "condT"), (w2c, "w2c"), (vecs, "vecs"), (w_r0, "w_r0"), (w_r1, "w_r1"),
             (aff, "aff"), (kwT, "kwT"), (owT, "owT"), (wqkv1, "wqkv1"), (wfb, "wfb"), (wo1, "wo1"), (g1, "g1"),
             (g2, "g2"), (rows, "rows"), (fbias, "fbias"), (wdec, "wdec"), (bdec, "bdec"), (bdecb, "bdecb"),
             (vmat, "vmat"), (tri, "tri"), (w13, "w13"), (w2, "w2"), (w_up, "w_up1"), (w_dn, "w_dn1")]
    LOADED = 16 * len(loads)
    ZEROED = 4
    STYLE, SCALE_C = range(3), 0.125

    @block.sync
    def _(sp):
        for dst, name in loads:
            sp.dma_start(dst if dst.__class__ is bass.AP else dst[:], dram[name]).then_inc(loaded, 16)

        def read(c):
            sp.dma_start(xs[:], x1[:, bass.ds(c * CH, CH)]).then_inc(x_read, 16)

        read(0)

        def turn(c, last):
            if not last:
                sp.wait_ge(*F0[5].done("x0", c))
                read(c + 1)
            sp.wait_ge(*F1[5].done(f"x{EXPERTS - 1}", c))
            sp.dma_start(out[:, bass.ds(c * CH, CH)], x3[:]).then_inc(stored, 16)

        with sp.Fori(0, CHUNKS - 1) as c:
            turn(c, False)
        turn(CHUNKS - 1, True)
        sp.wait_ge(stored, 16 * CHUNKS)

    @block.tensor
    def _(pe):
        pe.wait_ge(loaded, LOADED)
        for i in STYLE:
            last = nc.tensor.matmul(ps6[:, i * B:(i + 1) * B], aff[:, i, :], condT, start=True, stop=True)
        last.then_inc(su_pe("gates"), 1)
        pe.wait_ge(*su_dve.done("wsq2"))
        nc.tensor.matmul(ps7[:, 0:B], wsq[:, 0, :], ssq[:, 0, :], start=True, stop=True)
        nc.tensor.matmul(ps7[:, B:2 * B], ssq[:, 1, :], wsq[:, 1, :], start=True, stop=True)
        nc.tensor.matmul(ps7[:, 2 * B:3 * B], wsq[:, 2, :], ssq[:, 2, :], start=True, stop=True).then_inc(su_pe("sums"), 1)
        wk = wdec.rearrange("c (i k) -> c k i", k=KDEC)
        for g, (lo, hi) in enumerate(UG):
            if g:
                pe.wait_ge(*su_v.done(f"g{g - 1}"))
            for k in range(lo, hi):
                last = nc.tensor.matmul(ps6[:, (k - lo) * B:(k - lo + 1) * B], wk[:, k, 0:D], condT, start=True, stop=True)
            last.then_inc(su_u(f"g{g}"), 1)
        pe.wait_ge(*su_dve.done("dem2"))
        nc.tensor.matmul(ps7[0:KDEC, 0:B], wk[:, :, D], condT, start=True, stop=True).then_inc(su_pe("uw"), 1)
        pe.wait_ge(*su_dve.done("ub"))

        def experts(F, c, units_, up_a, up_b, x_in, down, before):
            up, silu, mul, dn, scale, acc = F
            for k in range(units_ + 1):
                if k < units_:
                    q = k % 2
                    if k >= 2:
                        pe.wait_ge(*mul.done(f"h{k - 2}", c))
                    else:
                        before(k)
                    nc.tensor.matmul(psU[:, 2 * q, :], up_a(k), x_in, start=True, stop=True).then_inc(up(f"a{k}"), 1)
                    nc.tensor.matmul(psU[:, 2 * q + 1, :], up_b(k), x_in, start=True, stop=True).then_inc(up(f"b{k}"), 1)
                if k > 0:
                    j = k - 1
                    e, half_ = j // 2, j % 2
                    pe.wait_ge(*mul.done(f"h{j}", c))
                    if half_ == 0 and e >= 2:
                        pe.wait_ge(*scale.done(f"c{e - 2}", c))
                    for n in range(NC):
                        last = nc.tensor.matmul(psDn[:, e % 2, n * P:(n + 1) * P], hid[:, half_, n * P:(n + 1) * P],
                                                down(e, half_), start=(half_ == 0 and n == 0), stop=(half_ == 1),
                                                skip_group_check=True)
                    last.then_inc(dn(f"d{j}"), 1)

        def turn(c):
            pe.wait_ge(x_read, (c + 1) * 16)
            wait_if(pe, m_dve, "x3", c - 1)
            for n in range(NC):
                last = nc.tensor.transpose(ps6[:, n * P:(n + 1) * P], xs[:, n * P:(n + 1) * P], ident[:])
            last.then_inc(f_pe("x1"), 1)
            wait_if(pe, g_dve, "raw", c - 1)
            pe.wait_ge(*f_dve.done("xm", c))
            nc.tensor.matmul(ps7, w2c[:], xm[:], start=True, stop=True).then_inc(f_pe("y"), 1)
            pe.wait_ge(*f_dve.done("yT", c))
            for n in range(NC):
                last = nc.tensor.matmul(ps7[:, n * EXPERTS:(n + 1) * EXPERTS], yT[:, n * P:(n + 1) * P], w_r0[:], start=True, stop=True)
            last.then_inc(f_pe("router"), 1)

            def before0(k):
                wait_if(pe, F1[2], f"h{U1 - 2 + k}", c - 1)
                wait_if(pe, F1[4], f"c{EXPERTS - 2 + k}", c - 1)

            experts(F0, c, U0, lambda k: w13[:, k // 2, 0, k % 2 * P:(k % 2 + 1) * P],
                    lambda k: w13[:, k // 2, 1, k % 2 * P:(k % 2 + 1) * P], yT[:], lambda e, h: w2[:, e, h, :], before0)
            pe.wait_ge(*F0[5].done(f"x{EX0 - 1}", c))
            for n in range(NC):
                last = nc.tensor.transpose(ps6[:, n * P:(n + 1) * P], x2[:, n * P:(n + 1) * P], ident[:])
            last.then_inc(k_pe("x2T"), 1)
            pe.wait_ge(*k_dve.done("xk", c))
            for n in range(NC):
                last = nc.tensor.matmul(ps6[:, n * P:(n + 1) * P], xk[:, n * P:(n + 1) * P], kwT[:], start=True, stop=True)
            last.then_inc(k_pe("kx"), 1)
            pe.wait_ge(*k_dve.done(f"av{NC - 1}", c))
            for n in range(NC):
                last = nc.tensor.transpose(ps6[:, n * P:(n + 1) * P], mixed[:, n * P:(n + 1) * P], ident[:])
            last.then_inc(k_pe("oT"), 1)
            pe.wait_ge(*k_dve.done("xo", c))
            nc.tensor.matmul(ps6, owT[:], xk[:], start=True, stop=True).then_inc(k_pe("y"), 1)
            pe.wait_ge(*k_act.done("y2T", c))
            free = (None, m_dve.done("q", c), m_dve.done("k", c))
            for i, name in enumerate("qkv"):
                if free[i]:
                    pe.wait_ge(*free[i])
                for n in range(NC):
                    last = nc.tensor.matmul(ps6[:, n * P:(n + 1) * P], y2T[:, n * P:(n + 1) * P], wqkv1[:, i, :], start=True, stop=True)
                last.then_inc(m_pe(name), 1)
            pe.wait_ge(*m_act.done("v", c))
            for n in range(NC):
                last = nc.tensor.matmul(ps6[:, n * 32:(n + 1) * 32], y2T[:, n * P:(n + 1) * P], wfb[:], start=True, stop=True)
            last.then_inc(m_pe("fb"), 1)
            pe.wait_ge(*m_dve.done("fb0", c))
            nc.tensor.matmul(ps6[0:D1, :], g1[:], y2T[:], start=True, stop=True).then_inc(m_pe("g"), 1)
            pe.wait_ge(*m_act.done("gT", c))
            for n in range(NC):
                last = nc.tensor.matmul(ps6[:, n * P:(n + 1) * P], gT[:, n * P:(n + 1) * P], g2[:], start=True, stop=True)
            last.then_inc(m_pe("gate"), 1)
            pe.wait_ge(*m_pool.done("og2", c))
            pe.wait_ge(*m_act.done("gate", c))
            for n in range(NC):
                last = nc.tensor.transpose(ps6[:, n * P:(n + 1) * P], o1[:, n * P:(n + 1) * P], ident[:])
            last.then_inc(m_pe("ogT"), 1)
            pe.wait_ge(*m_act.done("ogT", c))
            for n in range(NC):
                last = nc.tensor.matmul(ps6[:, n * P:(n + 1) * P], ogT[:, n * P:(n + 1) * P], wo1[:], start=True, stop=True)
            last.then_inc(m_pe("x3"), 1)
            pe.wait_ge(*m_dve.done("x3", c))
            for n in range(NC):
                last = nc.tensor.transpose(ps7[:, n * P:(n + 1) * P], x3[:, n * P:(n + 1) * P], ident[:])
            last.then_inc(g_pe("x3T"), 1)
            pe.wait_ge(*g_act.done("x3T", c))
            for b in range(B):
                last = nc.tensor.matmul(ps7[0:KDEC, b * NC:(b + 1) * NC], Uw[:, :, b], by_n(x3T[:])[:, :, b], start=True, stop=True)
            last.then_inc(g_pe("t"), 1)
            pe.wait_ge(*g_dve.done("t", c))
            for n in range(NC):
                last = nc.tensor.matmul(ps7[:, n * P:(n + 1) * P], tK[:, n, :], vmat[:], start=True, stop=True)
            last.then_inc(g_pe("z"), 1)
            pe.wait_ge(*g_dve.done(f"zn{NC - 1}", c))
            pe.wait_ge(*g_act.done("z", c))
            for n in range(NC):
                last = nc.tensor.transpose(ps7[:, n * P:(n + 1) * P], zn[:, n * P:(n + 1) * P], ident[:])
            last.then_inc(g_pe("znT"), 1)
            pe.wait_ge(*g_act.done("znT", c))
            for n in range(NC):
                last = nc.tensor.matmul(ps7[:, n * EXPERTS:(n + 1) * EXPERTS], znT[:, n * P:(n + 1) * P], w_r1[:], start=True, stop=True)
            last.then_inc(g_pe("router"), 1)

            def before1(k):
                pe.wait_ge(*F0[2].done(f"h{U0 - 2 + k}", c))
                pe.wait_ge(*F0[4].done(f"c{EX0 - 2 + k}", c))

            experts(F1, c, U1, lambda k: w_up[:, k // 2, HID + k % 2 * P:HID + (k % 2 + 1) * P],
                    lambda k: w_up[:, k // 2, k % 2 * P:(k % 2 + 1) * P], znT[:], lambda e, h: w_dn[:, e, h, :], before1)

        turn(0)
        with pe.Fori(1, CHUNKS) as c:
            turn(c)

    @block.scalar
    def _(act):
        act.wait_ge(*su_dve.done("l0"))
        nc.scalar.activation(lam[:], ltmp, ACT.Exp).then_inc(su_act("e"), 1)
        act.wait_ge(*su_act.done("e"))
        nc.scalar.activation(ltmp, lam[:], ACT.Ln, bias=1.0).then_inc(su_act("ln"), 1)

        def silus(F, c, units_, before):
            up, silu, mul, dn, scale, acc = F
            for k in range(units_):
                q = k % 2
                act.wait_ge(*up.done(f"a{k}", c))
                if k >= 2:
                    act.wait_ge(*mul.done(f"h{k - 2}", c))
                else:
                    before(k)
                nc.scalar.activation(sil[:, q, :], psU[:, 2 * q, :], ACT.Silu).then_inc(silu(f"s{k}"), 1)

        def turn(c):
            act.wait_ge(*f_dve.done("sub", c))
            nc.scalar.activation(ex8[:], s8[:], ACT.Exp).then_inc(f_act("exp"), 1)
            silus(F0, c, U0, lambda k: wait_if(act, F1[2], f"h{U1 - 2 + k}", c - 1))
            act.wait_ge(*k_pool.done("kx", c))
            nc.scalar.activation(kx[:, :, 1, :], kx[:, :, 0, :], ACT.Copy).then_inc(k_act("kxdup"), 1)
            act.wait_ge(*k_dve.done(f"sd{NC // 2 - 1}", c))
            nc.scalar.activation(sd[:, :, :, 1, :], sd[:, :, :, 0, :], ACT.Copy).then_inc(k_act("sddup"), 1)
            nc.scalar.activation(sf[:, :, 0:OFF, :], sd[:, :, :, 0, :], ACT.Copy).then_inc(k_act("sf0"), 1)
            act.wait_ge(*k_dve.done("sub", c))
            nc.scalar.activation(sf[:].rearrange("p n o h -> p (n o h)"), sf[:].rearrange("p n o h -> p (n o h)"), ACT.Exp,
                                 scale=float(D1) ** -0.5).then_inc(k_act("exp"), 1)
            act.wait_ge(*k_dve.done("y1", c))
            nc.scalar.activation(y2T[:], kx0[:], ACT.Identity, bias=vecs[:, 1:2]).then_inc(k_act("y2T"), 1)
            act.wait_ge(*m_pe.done("q", c))
            nc.scalar.activation(sqr[:], ps6, ACT.Square).then_inc(m_act("sqq"), 1)
            act.wait_ge(*m_pe.done("k", c))
            act.wait_ge(*m_dve.done("ssq", c))
            nc.scalar.activation(sqr[:], ps6, ACT.Square).then_inc(m_act("sqk"), 1)
            act.wait_ge(*m_pe.done("v", c))
            wait_if(act, m_dve, "U", c - 1)
            nc.scalar.activation(kv[:, D1:2 * D1, :].rearrange("p j (n h) -> p j n h", n=NC),
                                 ps6.rearrange("p (n h j) -> p j n h", n=NC, h=H1), ACT.Copy).then_inc(m_act("v"), 1)
            act.wait_ge(*m_dve.done("fb0", c))
            nc.scalar.activation(fbt[:], fb0[:], ACT.Tanh, scale=0.5).then_inc(m_act("fbt"), 1)
            act.wait_ge(*m_pe.done("g", c))
            nc.scalar.activation(gT[:], ps6[0:D1, :], ACT.Copy).then_inc(m_act("gT"), 1)
            act.wait_ge(*m_pe.done("gate", c))
            nc.scalar.activation(gate[:], ps6, ACT.Tanh, scale=0.5).then_inc(m_act("gate"), 1)
            act.wait_ge(*m_dve.done(f"hv{NC - 1}", c))
            nc.scalar.activation(carry[:, 0, :, :].rearrange("p (i j) h -> p i j h", i=D1), A4[:, :, 0:D1, NC - 1, :],
                                 ACT.Copy)
            nc.scalar.activation(carry[:, 1, :, :], Hv[:, :, NC - 1, :], ACT.Copy).then_inc(m_act("carry"), 1)
            act.wait_ge(*m_pe.done("ogT", c))
            nc.scalar.activation(ogT[:], ps6, ACT.Copy).then_inc(m_act("ogT"), 1)
            act.wait_ge(*g_pe.done("x3T", c))
            nc.scalar.activation(x3T[:], ps7, ACT.Copy).then_inc(g_act("x3T"), 1)
            act.wait_ge(*g_pe.done("z", c))
            nc.scalar.activation(z[:], ps7, ACT.Copy).then_inc(g_act("z"), 1)
            act.wait_ge(*g_pe.done("znT", c))
            wait_if(act, F1[0], f"b{U1 - 1}", c - 1)
            nc.scalar.activation(znT[:], ps7, ACT.Copy).then_inc(g_act("znT"), 1)
            act.wait_ge(*g_dve.done("sub", c))
            nc.scalar.activation(ex8[:], s8[:], ACT.Exp).then_inc(g_act("exp"), 1)
            silus(F1, c, U1, lambda k: act.wait_ge(*F0[2].done(f"h{U0 - 2 + k}", c)))

        turn(0)
        with act.Fori(1, CHUNKS) as c:
            turn(c)

    @block.gpsimd
    def _(pool):
        for dst, val in ((half, -0.5), (carry, 0.0), (cw0, 1.0 / (TOP_K + 1)), (tiny, 1e-6)):
            nc.gpsimd.memset(dst if dst.__class__ is bass.AP else dst[:], val).then_inc(zeroed, 1)
        nc.gpsimd.memset(neps[:, 0, :], 1e-5).then_inc(zeroed, 1)
        nc.gpsimd.memset(neps[:, 1, :], 1.0 / (4 * D1)).then_inc(zeroed, 1)
        nc.gpsimd.memset(neps[:, 2, :], 1.0 / D).then_inc(zeroed, 1)
        pool.wait_ge(zeroed, ZEROED + 3)
        pool.wait_ge(*su_dve.done("dem2"))
        nc.gpsimd.tensor_tensor(demod[:], demod[:], half[:, 0:1].unsqueeze(1).broadcast_to([P, 3, B]), ALU.pow).then_inc(su_pool("dem"), 1)
        pool.wait_ge(*su_pool.done("dem"))

        def accs(F, c, n_exp, acc_tile, base):
            up, silu, mul, dn, scale, acc = F
            for e in range(n_exp):
                pool.wait_ge(*scale.done(f"c{e}", c))
                if e:
                    pool.wait_ge(*acc.done(f"x{e - 1}", c))
                nc.gpsimd.tensor_tensor(acc_tile[:], (acc_tile if e else base)[:], scaled[:, e % 2, :], ALU.add).then_inc(acc(f"x{e}"), 1)

        def turn(c):
            pool.wait_ge(x_read, (c + 1) * 16)
            accs(F0, c, EX0, x2, xs)
            pool.wait_ge(*k_dve.done("kx0", c))
            nc.gpsimd.tensor_tensor(kx[:, :, 0, :], by_n(kx0[:]), bc_n(rows[:, 0, :]), ALU.add).then_inc(k_pool("kx"), 1)
            pool.wait_ge(*k_dve.done("rsum", c))
            nc.gpsimd.tensor_tensor(sf[:], sf[:], rsh[:].unsqueeze(2).broadcast_to([P, NC, H1, H1]), ALU.mult).then_inc(k_pool("probs"), 1)
            for i, (s_, e_, r_) in enumerate((("ssq", "eq", "rq"), ("ssk", "ek", "rk"))):
                pool.wait_ge(*m_dve.done(s_, c))
                nc.gpsimd.tensor_tensor(ssr[:, i, :], ssr[:, i, :], tiny[:], ALU.add).then_inc(m_pool(e_), 1)
                pool.wait_ge(*m_pool.done(e_, c))
                nc.gpsimd.tensor_tensor(rn[:, i, :], ssr[:, i, :], half[:], ALU.pow).then_inc(m_pool(r_), 1)
            pool.wait_ge(*m_dve.done("og", c))
            nc.gpsimd.tensor_tensor(sqr[:], og[:], og[:], ALU.mult).then_inc(m_pool("sq"), 1)
            pool.wait_ge(*m_dve.done("ss", c))
            nc.gpsimd.tensor_tensor(ssr[:, 0, :], ssr[:, 0, :], neps[:, 1, 0:SYS], ALU.mult).then_inc(m_pool("ms"), 1)
            pool.wait_ge(*m_pool.done("ms", c))
            nc.gpsimd.tensor_tensor(ssr[:, 0, :], ssr[:, 0, :], neps[:, 0, 0:SYS], ALU.add).then_inc(m_pool("eps"), 1)
            pool.wait_ge(*m_pool.done("eps", c))
            nc.gpsimd.tensor_tensor(rn[:, 0, :], ssr[:, 0, :], half[:], ALU.pow).then_inc(m_pool("rs"), 1)
            pool.wait_ge(*m_dve.done("ogn", c))
            nc.gpsimd.tensor_tensor(by_n(o1[:]), by_n(o1[:]), bc_n(rows[:, 2, :]), ALU.mult).then_inc(m_pool("og2"), 1)
            pool.wait_ge(*g_act.done("z", c))
            nc.gpsimd.tensor_tensor(zn[:], z[:], z[:], ALU.mult).then_inc(g_pool("sq"), 1)
            pool.wait_ge(*g_dve.done("ms", c))
            nc.gpsimd.tensor_tensor(ms4[:, 0, :], ms4[:, 0, :], neps[:, 2, 0:NC], ALU.mult).then_inc(g_pool("mean"), 1)
            pool.wait_ge(*g_pool.done("mean", c))
            nc.gpsimd.tensor_tensor(ms4[:, 0, :], ms4[:, 0, :], tiny[:, 0:NC], ALU.add).then_inc(g_pool("eps"), 1)
            pool.wait_ge(*g_pool.done("eps", c))
            nc.gpsimd.tensor_tensor(ms4[:, 1, :], ms4[:, 0, :], half[:, 0:NC], ALU.pow).then_inc(g_pool("rs"), 1)
            nc.gpsimd.tensor_tensor(x3[:], x3[:], z[:], ALU.add).then_inc(g_pool("base"), 1)
            pool.wait_ge(*g_pool.done("base", c))
            accs(F1, c, EXPERTS, x3, x3)

        turn(0)
        with pool.Fori(1, CHUNKS) as c:
            turn(c)

    @block.vector
    def _(dve):
        tt, red = nc.vector.tensor_tensor, nc.vector.tensor_reduce
        dve.wait_ge(loaded, LOADED)
        dve.wait_ge(zeroed, ZEROED + 3)
        dve.wait_ge(*su_pe.done("gates"))
        for i in STYLE:
            nc.vector.tensor_scalar(style[:, i, :], ps6[:, i * B:(i + 1) * B], SCALE_C if i == 0 else 1.0, vecs[:, 2 + i:3 + i],
                                    ALU.mult, ALU.add).then_inc(su_dve(f"st{i}"), 1)
        for i in STYLE:
            dve.wait_ge(*su_dve.done(f"st{i}"))
            tt(ssq[:, i, :], style[:, i, :], style[:, i, :], ALU.mult).then_inc(su_dve(f"ssq{i}"), 1)
        for i, w in enumerate((w2c, kwT, owT)):
            tt(wsq[:, i, :], w[:], w[:], ALU.mult).then_inc(su_dve(f"wsq{i}"), 1)
        dve.wait_ge(*su_pe.done("sums"))
        for i in STYLE:
            nc.vector.tensor_scalar(demod[:, i, :], ps7[:, i * B:(i + 1) * B], 1e-8, None, ALU.add).then_inc(su_dve(f"dem{i}"), 1)
        nc.vector.scalar_tensor_tensor(out=ltmp, in0=rows[:, 1, :], scalar=-1.0, in1=rows[:, 1, :], op0=ALU.mult,
                                       op1=ALU.min).then_inc(su_dve("l0"), 1)
        dve.wait_ge(*su_act.done("ln"))
        nc.vector.scalar_tensor_tensor(out=lam[:], in0=rows[:, 1, :], scalar=0.0, in1=ltmp, op0=ALU.max,
                                       op1=ALU.add).then_inc(su_dve("l1"), 1)
        dve.wait_ge(*su_dve.done("l1"))
        nc.vector.tensor_scalar(lam[:], lam[:], 0.25, None, ALU.add).then_inc(su_dve("l2"), 1)
        nc.vector.tensor_scalar(rows[:, 2, :], rows[:, 2, :], 0.5, None, ALU.mult).then_inc(su_dve("nw"), 1)
        for g, (lo, hi) in enumerate(UG):
            dve.wait_ge(*su_u.done(f"g{g}"))
            tt(Uw[:, lo:hi, :], ps6[:, 0:(hi - lo) * B].rearrange("p (k b) -> p k b", b=B),
               bdec[:, lo:hi].unsqueeze(2).broadcast_to([P, hi - lo, B]), ALU.add).then_inc(su_v(f"g{g}"), 1)
        dve.wait_ge(*su_v.done(f"g{len(UG) - 1}"))
        nc.vector.tensor_copy(ltmp[:, 0:1], vecs[:, 0:1]).then_inc(su_dve("uw"), 1)
        dve.wait_ge(*su_pe.done("uw"))
        nc.vector.tensor_scalar(Ub[:], ps7[0:KDEC, 0:B], bdecb[:, 0:1], None, ALU.add).then_inc(su_dve("ub"), 1)
        dve.wait_ge(*su_pool.done("dem"))

        def muls(F, c, n_exp, cw, before):
            up, silu, mul, dn, scale, acc = F
            for k in range(2 * n_exp + 2):
                if k < 2 * n_exp:
                    q = k % 2
                    dve.wait_ge(*silu.done(f"s{k}", c))
                    dve.wait_ge(*up.done(f"b{k}", c))
                    if k >= 2:
                        dve.wait_ge(*dn.done(f"d{k - 2}", c))
                    tt(hid[:, q, :], sil[:, q, :], psU[:, 2 * q + 1, :], ALU.mult).then_inc(mul(f"h{k}"), 1)
                if k % 2 == 1 and k > 2:
                    e = (k - 3) // 2
                    dve.wait_ge(*dn.done(f"d{2 * e + 1}", c))
                    if e >= 2:
                        dve.wait_ge(*acc.done(f"x{e - 2}", c))
                    else:
                        before(e)
                    tt(by_n(scaled[:, e % 2, :]), by_n(psDn[:, e % 2, :]), cw[:, :, e:e + 1].broadcast_to([P, NC, D]),
                       ALU.mult).then_inc(scale(f"c{e}"), 1)

        def ranks(S_, c, vals):
            a = vals.unsqueeze(2).broadcast_to([P, NC, EXPERTS, EXPERTS])
            b = vals.unsqueeze(3).broadcast_to([P, NC, EXPERTS, EXPERTS])
            sq = lambda t: t[:].rearrange("p n (e f) -> p n e f", e=EXPERTS)
            tt(sq(ge), a, b, ALU.is_ge).then_inc(S_("ge"), 1)
            dve.wait_ge(*S_.done("ge", c))
            tt(ge[:], ge[:], bc_n(tri[:, 0, :]), ALU.mult).then_inc(S_("gel"), 1)
            tt(sq(gt), a, b, ALU.is_gt).then_inc(S_("gt"), 1)
            dve.wait_ge(*S_.done("gt", c))
            tt(gt[:], gt[:], bc_n(tri[:, 1, :]), ALU.mult).then_inc(S_("gtu"), 1)
            dve.wait_ge(*S_.done("gtu", c))
            tt(ge[:], ge[:], gt[:], ALU.add).then_inc(S_("cmp"), 1)
            dve.wait_ge(*S_.done("cmp", c))
            red(rank[:], sq(ge), AX, ALU.add).then_inc(S_("rank"), 1)
            dve.wait_ge(*S_.done("rank", c))

        def experts0_in(c):
            dve.wait_ge(*f_pe.done("x1", c))
            tt(by_n(xm[:]), by_n(ps6), bc_n(style[:, 0, :]), ALU.mult).then_inc(f_dve("xm"), 1)
            dve.wait_ge(*f_pe.done("y", c))
            wait_if(dve, F0[0], f"b{U0 - 1}", c - 1)
            tt(by_n(yT[:]), by_n(ps7), bc_n(demod[:, 0, :]), ALU.mult).then_inc(f_dve("dm"), 1)
            dve.wait_ge(*f_dve.done("dm", c))
            nc.vector.tensor_scalar(yT[:], yT[:], vecs[:, 0:1], 256.0, ALU.add, ALU.min).then_inc(f_dve("bias"), 1)
            dve.wait_ge(*f_dve.done("bias", c))
            nc.vector.tensor_scalar(yT[:], yT[:], -256.0, None, ALU.max).then_inc(f_dve("yT"), 1)
            dve.wait_ge(*f_pe.done("router", c))
            r = ps7[:, 0:NC * EXPERTS].rearrange("p (n e) -> p n e", n=NC)
            red(m4[:], r, AX, ALU.max).then_inc(f_dve("max"), 1)
            dve.wait_ge(*f_dve.done("max", c))
            tt(s8[:], r, m4[:].unsqueeze(2).broadcast_to([P, NC, EXPERTS]), ALU.subtract).then_inc(f_dve("sub"), 1)
            dve.wait_ge(*f_act.done("exp", c))
            red(m4[:], ex8[:], AX, ALU.add).then_inc(f_dve("sum"), 1)
            dve.wait_ge(*f_dve.done("sum", c))
            nc.vector.reciprocal(m4[:], m4[:]).then_inc(f_dve("rsum"), 1)
            dve.wait_ge(*f_dve.done("rsum", c))
            tt(p8[:], ex8[:], m4[:].unsqueeze(2).broadcast_to([P, NC, EXPERTS]), ALU.mult).then_inc(f_dve("probs"), 1)
            dve.wait_ge(*f_dve.done("probs", c))
            ranks(f_dve, c, p8[:])
            nc.vector.tensor_scalar(rank[:], rank[:], float(TOP_K), TOP_K / (TOP_K + 1.0), ALU.is_lt, ALU.mult).then_inc(f_dve("rk2"), 1)
            dve.wait_ge(*f_dve.done("rk2", c))
            tt(cw0[:, :, 0:EXPERTS], rank[:], p8[:], ALU.mult).then_inc(f_dve("cw"), 1)
            dve.wait_ge(*f_dve.done("cw", c))

        def mixing(c):
            dve.wait_ge(*k_pe.done("x2T", c))
            tt(by_n(xk[:]), by_n(ps6), bc_n(style[:, 1, :]), ALU.mult).then_inc(k_dve("xk"), 1)
            dve.wait_ge(*k_pe.done("kx", c))
            tt(by_n(kx0[:]), by_n(ps6), bc_n(demod[:, 1, :]), ALU.mult).then_inc(k_dve("kx0"), 1)
            dve.wait_ge(*k_act.done("kxdup", c))
            window = kx[:].rearrange("p n t d -> p n (t d)")

            def shifted(n, count):
                w = window[:, n, 0:D]
                return bass.AP(w.tensor, w.offset, [list(w.ap[0]), [D1, count], [1, D]])

            pr4 = prod[:, 0:2 * OFF * D].rearrange("p (n o x) -> p n o x", n=2, o=OFF)
            for m in range(NC // 2):
                if m:
                    dve.wait_ge(*k_dve.done(f"sd{m - 1}", c))
                for n in range(2):
                    last = tt(pr4[:, n, :, :], window[:, 2 * m + n, 0:D].unsqueeze(1).broadcast_to([P, OFF, D]),
                              shifted(2 * m + n, OFF), ALU.mult)
                last.then_inc(k_dve(f"prod{m}"), 1)
                dve.wait_ge(*k_dve.done(f"prod{m}", c))
                red(sd[:, 2 * m:2 * m + 2, :, 0, :].rearrange("p n o h -> p (n o) h"),
                    prod[:, 0:2 * OFF * D].rearrange("p (a h d) -> p a h d", h=H1, d=D1), AX, ALU.add).then_inc(k_dve(f"sd{m}"), 1)
            dve.wait_ge(*k_act.done("sddup", c))
            for n in range(NC):
                s0 = sd[:, n, 0, 0, 0:1]
                back = bass.AP(s0.tensor, s0.offset + (H1 - OFF) * 2 * H1 + OFF, [list(s0.ap[0]), [1 - 2 * H1, H1 - OFF], [1, H1]])
                last = nc.vector.tensor_copy(sf[:, n, OFF:H1, :], back)
            last.then_inc(k_dve("sf1"), 1)
            dve.wait_ge(*k_dve.done("sf1", c))
            dve.wait_ge(*k_act.done("sf0", c))
            red(mxh[:], sf[:].rearrange("p n o h -> p n h o"), AX, ALU.max).then_inc(k_dve("max"), 1)
            dve.wait_ge(*k_dve.done("max", c))
            tt(sf[:], sf[:], mxh[:].unsqueeze(2).broadcast_to([P, NC, H1, H1]), ALU.subtract).then_inc(k_dve("sub"), 1)
            dve.wait_ge(*k_act.done("exp", c))
            red(smh[:], sf[:].rearrange("p n o h -> p n h o"), AX, ALU.add).then_inc(k_dve("sum"), 1)
            dve.wait_ge(*k_dve.done("sum", c))
            nc.vector.reciprocal(rsh[:], smh[:]).then_inc(k_dve("rsum"), 1)
            dve.wait_ge(*k_pool.done("probs", c))
            for n in range(NC):
                if n >= 1:
                    dve.wait_ge(*k_dve.done(f"av{n - 1}", c))
                w = window[:, n, 0:D]
                win = bass.AP(w.tensor, w.offset, [list(w.ap[0]), [D1, H1], [D1, H1], [1, D1]])
                tt(prod[:, 0:H1 * H1 * D1].rearrange("p (o h d) -> p o h d", o=H1, h=H1),
                   sf[:, n, :, :].unsqueeze(3).broadcast_to([P, H1, H1, D1]), win, ALU.mult).then_inc(k_dve(f"ap{n}"), 1)
                dve.wait_ge(*k_dve.done(f"ap{n}", c))
                red(mixed[:, n * D:(n + 1) * D], prod[:, 0:H1 * H1 * D1].rearrange("p (o x) -> p x o", o=H1),
                    AX, ALU.add).then_inc(k_dve(f"av{n}"), 1)
            dve.wait_ge(*k_pe.done("oT", c))
            tt(by_n(xk[:]), by_n(ps6), bc_n(style[:, 2, :]), ALU.mult).then_inc(k_dve("xo"), 1)
            dve.wait_ge(*k_pe.done("y", c))
            tt(by_n(kx0[:]), by_n(ps6), bc_n(demod[:, 2, :]), ALU.mult).then_inc(k_dve("y1"), 1)

        def recurrence(c):
            planes = ps6.rearrange("p (n h j) -> p j n h", n=NC, h=H1)
            for i, (sq_, s_, r_, name) in enumerate((("sqq", "ssq", "rq", "q"), ("sqk", "ssk", "rk", "k"))):
                dve.wait_ge(*m_act.done(sq_, c))
                red(ssr[:, i, :], sqr[:].rearrange("p (s j) -> p s j", j=D1), AX, ALU.add).then_inc(m_dve(s_), 1)
                dve.wait_ge(*m_pool.done(r_, c))
                dst = A[:, :, D1, :] if i == 0 else kv[:, 0:D1, :]
                tt(dst.rearrange("p j (n h) -> p j n h", n=NC), planes,
                   rn[:, i, :].rearrange("p (n h) -> p n h", n=NC).unsqueeze(1).broadcast_to([P, D1, NC, H1]), ALU.mult).then_inc(m_dve(name), 1)
            dve.wait_ge(*m_pe.done("fb", c))
            tt(fb0[:], ps6[:, 0:NC * 2 * H1].rearrange("p (n t h) -> p n t h", n=NC, t=2), bc_n(fbias[:]).rearrange("p n (t h) -> p n t h", t=2),
               ALU.add).then_inc(m_dve("fb0"), 1)
            dve.wait_ge(*m_act.done("fbt", c))
            nc.vector.tensor_scalar(fb[:], fbt[:], 0.5, 0.5, ALU.mult, ALU.add).then_inc(m_dve("fb"), 1)
            dve.wait_ge(*m_dve.done("fb", c))
            tt(bk[:].rearrange("p j (n h) -> p j n h", n=NC), kv[:, 0:D1, :].rearrange("p j (n h) -> p j n h", n=NC),
               fb[:, :, 1, :].unsqueeze(1).broadcast_to([P, D1, NC, H1]), ALU.mult).then_inc(m_dve("bk"), 1)
            dve.wait_ge(*m_dve.done("bk", c))
            dve.wait_ge(*m_act.done("v", c))
            wait_if(dve, m_act, "carry", c - 1)
            tt(A[:, :, 0:D1, :], bk[:].unsqueeze(2).broadcast_to([P, D1, D1, SYS]),
               kv[:, 0:D1, :].unsqueeze(1).broadcast_to([P, D1, D1, SYS]), ALU.mult).then_inc(m_dve("Uk"), 1)
            tt(Hv[:].rearrange("p (i j) n h -> p i j (n h)", i=D1), bk[:].unsqueeze(2).broadcast_to([P, D1, D1, SYS]),
               kv[:, D1:, :].unsqueeze(1).broadcast_to([P, D1, D1, SYS]), ALU.mult).then_inc(m_dve("U"), 1)
            dve.wait_ge(*m_dve.done("U", c))
            T4 = prod[:, 0:2 * D1 * D1 * H1].rearrange("p (t a h) -> p t a h", t=2, h=H1)
            for n in range(NC):
                if n:
                    dve.wait_ge(*m_dve.done(f"hv{n - 1}", c))
                f_n = fb[:, n, 0, :]
                tt(T4[:, 0, :, :].rearrange("p (i j) h -> p i j h", i=D1),
                   carry[:, 0, :, :].rearrange("p (i j) h -> p i j h", i=D1) if n == 0 else A4[:, :, 0:D1, n - 1, :],
                   f_n.unsqueeze(1).unsqueeze(1).broadcast_to([P, D1, D1, H1]), ALU.mult).then_inc(m_dve(f"mk{n}"), 1)
                tt(T4[:, 1, :, :], carry[:, 1, :, :] if n == 0 else Hv[:, :, n - 1, :],
                   f_n.unsqueeze(1).broadcast_to([P, D1 * D1, H1]), ALU.mult).then_inc(m_dve(f"mv{n}"), 1)
                dve.wait_ge(*m_dve.done(f"mk{n}", c))
                tt(A4[:, :, 0:D1, n, :], A4[:, :, 0:D1, n, :], T4[:, 0, :, :].rearrange("p (i j) h -> p i j h", i=D1), ALU.add).then_inc(m_dve(f"hk{n}"), 1)
                dve.wait_ge(*m_dve.done(f"mv{n}", c))
                tt(Hv[:, :, n, :], Hv[:, :, n, :], T4[:, 1, :, :], ALU.add).then_inc(m_dve(f"hv{n}"), 1)
            dve.wait_ge(*m_act.done("carry", c))
            a0 = A[:, 0, 0, 0:1]
            diag = bass.AP(a0.tensor, a0.offset, [list(a0.ap[0]), [(D1 + 2) * SYS, D1], [H1, NC], [1, H1]])
            tt(diag, diag, lam[:].rearrange("p (h i) -> p i h", h=H1).unsqueeze(2).broadcast_to([P, D1, NC, H1]), ALU.add).then_inc(m_dve("diag"), 1)
            prev = "diag"
            for k in range(D1):
                r = D1 - 1 - k
                dve.wait_ge(*m_dve.done(prev, c))
                nc.vector.reciprocal(rinv[:], A[:, k, k, :]).then_inc(m_dve(f"ri{k}"), 1)
                dve.wait_ge(*m_dve.done(f"ri{k}", c))
                tt(A[:, k, k + 1:, :], A[:, k, k + 1:, :], rinv[:].unsqueeze(1).broadcast_to([P, r + 1, SYS]), ALU.mult).then_inc(m_dve(f"row{k}"), 1)
                prev = f"row{k}"
                if r:
                    dve.wait_ge(*m_dve.done(f"row{k}", c))
                    Tk = T[:, 0:r * (r + 1), :].rearrange("p (i j) s -> p i j s", i=r)
                    tt(Tk, A[:, k + 1:, k, :].unsqueeze(2).broadcast_to([P, r, r + 1, SYS]),
                       A[:, k, k + 1:, :].unsqueeze(1).broadcast_to([P, r, r + 1, SYS]), ALU.mult).then_inc(m_dve(f"t{k}"), 1)
                    dve.wait_ge(*m_dve.done(f"t{k}", c))
                    tt(A[:, k + 1:, k + 1:, :], A[:, k + 1:, k + 1:, :], Tk, ALU.subtract).then_inc(m_dve(f"a{k}"), 1)
                    prev = f"a{k}"
            for k in range(D1 - 1, 0, -1):
                dve.wait_ge(*m_dve.done(prev, c))
                tt(T[:, 0:k, :], A[:, 0:k, k, :], A[:, k, D1, :].unsqueeze(1).broadcast_to([P, k, SYS]), ALU.mult).then_inc(m_dve(f"bt{k}"), 1)
                dve.wait_ge(*m_dve.done(f"bt{k}", c))
                tt(A[:, 0:k, D1, :], A[:, 0:k, D1, :], T[:, 0:k, :], ALU.subtract).then_inc(m_dve(f"bx{k}"), 1)
                prev = f"bx{k}"
            dve.wait_ge(*m_dve.done(prev, c))
            tt(A[:, :, 0:D1, :], A[:, :, D1, :].unsqueeze(2).broadcast_to([P, D1, D1, SYS]),
               Hv[:].rearrange("p (i j) n h -> p i j (n h)", i=D1), ALU.mult).then_inc(m_dve("oprod"), 1)
            dve.wait_ge(*m_dve.done("oprod", c))
            wait_if(dve, m_pool, "og2", c - 1)
            red(o1[:].rearrange("p (s j) -> p j s", j=D1), A[:, :, 0:D1, :].rearrange("p i j s -> p j s i"), AX, ALU.add).then_inc(m_dve("o1"), 1)
            dve.wait_ge(*m_dve.done("o1", c))
            dve.wait_ge(*m_act.done("gate", c))
            nc.vector.scalar_tensor_tensor(out=og[:], in0=gate[:], scalar=1.0, in1=o1[:], op0=ALU.add, op1=ALU.mult).then_inc(m_dve("og"), 1)
            dve.wait_ge(*m_pool.done("sq", c))
            red(ssr[:, 0, :], sqr[:].rearrange("p (s j) -> p s j", j=D1), AX, ALU.add).then_inc(m_dve("ss"), 1)
            dve.wait_ge(*m_pool.done("rs", c))
            tt(o1[:].rearrange("p (s j) -> p s j", j=D1), og[:].rearrange("p (s j) -> p s j", j=D1),
               rn[:, 0, :].unsqueeze(2).broadcast_to([P, SYS, D1]), ALU.mult).then_inc(m_dve("ogn"), 1)
            dve.wait_ge(*m_pe.done("x3", c))
            if not isinstance(c, int) or c > 0:
                dve.wait_ge(stored, c * 16)
            tt(x3[:], ps6, x2[:], ALU.add).then_inc(m_dve("x3"), 1)

        def experts1_in(c):
            dve.wait_ge(*g_pe.done("t", c))
            tt(tK[:].rearrange("k n b -> k b n"), ps7[0:KDEC, :].rearrange("k (b n) -> k b n", n=NC),
               Ub[:].unsqueeze(2).broadcast_to([KDEC, B, NC]), ALU.add).then_inc(g_dve("t"), 1)
            dve.wait_ge(*g_pool.done("sq", c))
            red(ms4[:, 0, :], by_n(zn[:]), AX, ALU.add).then_inc(g_dve("ms"), 1)
            dve.wait_ge(*g_pool.done("rs", c))
            for n in range(NC):
                nc.vector.scalar_tensor_tensor(out=zn[:, n * D:(n + 1) * D], in0=z[:, n * D:(n + 1) * D], scalar=ms4[:, 1, n:n + 1],
                                               in1=rows[:, 3, :], op0=ALU.mult, op1=ALU.mult).then_inc(g_dve(f"zn{n}"), 1)
            dve.wait_ge(*g_pe.done("router", c))
            r = ps7[:, 0:NC * EXPERTS].rearrange("p (n e) -> p n e", n=NC)
            red(m4[:], r, AX, ALU.max).then_inc(g_dve("max"), 1)
            dve.wait_ge(*g_dve.done("max", c))
            tt(s8[:], r, m4[:].unsqueeze(2).broadcast_to([P, NC, EXPERTS]), ALU.subtract).then_inc(g_dve("sub"), 1)
            dve.wait_ge(*g_dve.done("sub", c))
            nc.vector.tensor_copy(p8[:], r).then_inc(g_dve("raw"), 1)
            dve.wait_ge(*g_dve.done("raw", c))
            ranks(g_dve, c, p8[:])
            dve.wait_ge(*g_act.done("exp", c))
            nc.vector.scalar_tensor_tensor(out=cw1[:], in0=rank[:], scalar=float(TOP_K), in1=ex8[:], op0=ALU.is_lt,
                                           op1=ALU.mult).then_inc(g_dve("em"), 1)
            dve.wait_ge(*g_dve.done("em", c))
            red(m4[:], cw1[:], AX, ALU.add).then_inc(g_dve("sum"), 1)
            dve.wait_ge(*g_dve.done("sum", c))
            nc.vector.reciprocal(m4[:], m4[:]).then_inc(g_dve("rsum"), 1)
            dve.wait_ge(*g_dve.done("rsum", c))
            tt(cw1[:], cw1[:], m4[:].unsqueeze(2).broadcast_to([P, NC, EXPERTS]), ALU.mult).then_inc(g_dve("cw"), 1)
            dve.wait_ge(*g_dve.done("cw", c))

        def turn(c):
            experts0_in(c)
            muls(F0, c, EX0, cw0, lambda e: wait_if(dve, F1[5], f"x{EXPERTS - 2 + e}", c - 1))
            mixing(c)
            recurrence(c)
            experts1_in(c)
            muls(F1, c, EXPERTS, cw1, lambda e: dve.wait_ge(*F0[5].done(f"x{EX0 - 2 + e}", c)))

        turn(0)
        with dve.Fori(1, CHUNKS) as c:
            turn(c)


def layouts(inp):
    f = lambda k: np.asarray(inp[k])
    a = {}
    x = f("x")
    inv = 1.0 / 10000.0 ** (np.arange(0, HD, 2, dtype=np.float32) / HD)
    ang = np.tile(np.arange(N, dtype=np.float32)[:, None] * inv[None, :], (GB, 1))
    a["cos"] = np.concatenate([np.cos(ang)] * 2, 1)
    a["sin"] = np.concatenate([-np.sin(ang), np.sin(ang)], 1)
    a["fold"] = np.tile(np.eye(AH, dtype=np.float32), (2, 1))
    a["ident"] = np.eye(P, dtype=np.float32)
    e = np.arange(EXPERTS)
    lower = (e[None, :] < e[:, None]).astype(np.float32).reshape(-1)
    upper = (e[None, :] > e[:, None]).astype(np.float32).reshape(-1)
    a["tri"] = np.tile(np.stack([lower, upper])[None], (P, 1, 1))
    a["xT"] = x.reshape(TOK, D).T
    a["condT"] = f("cond_512").T
    a["dgb"] = np.concatenate([f("L0_cond_down_gamma"), f("L0_cond_down_beta")], 1)
    a["ugb"] = np.stack([f("L0_cond_up_gamma"), f("L0_cond_up_beta")], 1)
    a["down"], a["up"] = f("L0_cond_down_project"), f("L0_cond_up_project")
    a["ln_gb"] = np.stack([f("L0_attn_ln_gamma"), f("L0_attn_ln_beta")], 1)
    a["b_out"] = np.tile(f("L0_attn_b_out")[None], (P, 1))
    a["x"] = x.reshape(TOK, D)
    a["w_qkv"] = f("L0_attn_w_qkv")
    a["w_out"] = f("L0_attn_w_out").reshape(PAIRS, P, D).transpose(1, 0, 2)
    a["w2c"] = f("L0_cond2_weight").T
    zero = np.zeros(D, np.float32)
    a["vecs"] = np.stack([f("L0_cond2_bias"), f("L1_cond_o_b"), f("L0_cond2_affine_b"), f("L1_cond_k_aff_b"),
                          f("L1_cond_o_aff_b"), zero, zero, zero], 1)
    a["w_r0"], a["w_r1"] = f("L0_ffn_w_router"), f("L1_ffn_w_router").T
    w1 = np.concatenate([f("L0_ffn_w1"), f("L0_ffn_ws1")[None]])
    w3 = np.concatenate([f("L0_ffn_w3"), f("L0_ffn_ws3")[None]])
    w2 = np.concatenate([f("L0_ffn_w2"), f("L0_ffn_ws2")[None]])
    a["w13"] = np.stack([w1, w3], 2).transpose(1, 0, 2, 3)
    a["w2"] = w2.reshape(EX0, 2, P, D).transpose(2, 0, 1, 3)
    a["aff"] = np.stack([f("L0_cond2_affine_w").T, f("L1_cond_k_aff_w").T, f("L1_cond_o_aff_w").T], 1)
    a["kwT"], a["owT"] = f("L1_cond_k_w").T, f("L1_cond_o_w").T
    a["wqkv1"] = np.stack([f("L1_attn_Wq"), f("L1_attn_Wk"), f("L1_attn_Wv")], 1)
    a["wfb"] = np.concatenate([f("L1_attn_Wf"), f("L1_attn_Wbet")], 1)
    a["wo1"], a["g1"], a["g2"] = f("L1_attn_Wo"), f("L1_attn_gate_w1"), f("L1_attn_gate_w2")
    a["rows"] = np.tile(np.stack([f("L1_cond_k_b"), f("L1_attn_lamb_params"), f("L1_attn_norm_weight"),
                                  f("L1_ffn_norm_scale")])[None], (P, 1, 1))
    a["fbias"] = np.tile(np.concatenate([f("L1_attn_delta"), np.zeros(H1, np.float32)])[None], (P, 1))
    a["wdec"] = f("L1_cond2_W_dec")
    b = f("L1_cond2_b_dec").reshape(D + 1, KDEC)
    a["bdec"], a["bdecb"] = b[:D], b[D][:, None]
    a["vmat"] = f("L1_cond2_V")
    a["w_up1"] = f("L1_ffn_w_up").transpose(2, 0, 1)
    a["w_dn1"] = f("L1_ffn_w_down").transpose(0, 2, 1).reshape(EXPERTS, 2, P, D).transpose(2, 0, 1, 3)
    return {k: np.ascontiguousarray(v) for k, v in a.items()}


def block_pair(nc, dram, x1, out):
    with ExitStack() as ctx:
        attention_phase(nc, ctx, dram, x1)
    with ExitStack() as ctx:
        mixing_phase(nc, ctx, dram, x1.rearrange("(b n) d -> b (n d)", b=B), out)


def kernel(**inputs):
    import concourse.bacc as bacc
    from concourse.bass_utils import run_bass_kernel_spmd

    nc = bacc.Bacc("TRN2", target_bir_lowering=False, num_devices=1)
    arrays = layouts(inputs)
    dram = {name: nc.dram_tensor(name, a.shape, F32, kind="ExternalInput").ap() for name, a in arrays.items()}
    x1 = nc.dram_tensor("x1", (TOK, D), F32, kind="Internal").ap()
    out = nc.dram_tensor("out", (B, N * D), F32, kind="ExternalOutput").ap()
    block_pair(nc, dram, x1, out)
    r = run_bass_kernel_spmd(nc, [arrays], core_ids=[0])
    return np.asarray(r.results[0]["out"]).reshape(B, N, D)
```

```python
from contextlib import ExitStack

import concourse.bass as bass
import numpy as np
from concourse import mybir

F32 = mybir.dt.float32
ALU = mybir.AluOpType
ACT = mybir.ActivationFunctionType
AX = mybir.AxisListType.X

P = 128
B, N, D, C = 128, 32, 128, 64
TOK = B * N
AH = 32
HEADS, HD = 16, 64
HALF = HD // 2
PAIRS = HEADS // 2
INNER = HEADS * HD
GB = P // N
TILES = TOK // P


class Steps:

    def __init__(self, sem, names):
        self.sem, self.names, self.at = sem, names.split(), 0

    def __call__(self, name):
        assert self.names[self.at % len(self.names)] == name, (name, self.names, self.at)
        self.at += 1
        return self.sem

    def step(self, name, upto=None):
        first, last = self.names.index(name), self.names.index(upto or name)
        assert self.at <= first, (name, self.names[self.at])
        raised, self.at = last + 1 - self.at, (last + 1) % len(self.names)
        return self.sem, raised

    def done(self, name, t=0):
        return self.sem, t * len(self.names) + (self.names.index(name) + 1)


def wait_if(eng, steps, name, t):
    if not isinstance(t, int) or t >= 0:
        eng.wait_ge(*steps.done(name, t))


def attention_phase(nc, ctx, dram, x1):

    def sb(name, shape):
        return ctx.enter_context(nc.sbuf_tensor("p1_" + name, shape, F32))

    xT = sb("xT", [P, TOK])
    condT = sb("condT", [C, B])
    w_dgb = sb("w_dgb", [C, 2 * AH])
    w_ugb = sb("w_ugb", [C, 2, D])
    w_down = sb("w_down", [P, 2 * AH])
    w_up = sb("w_up", [AH, 2, D])
    fold = sb("fold", [2 * AH, AH])
    ident = sb("ident", [P, P])
    ln_gb = sb("ln_gb", [P, 2])
    b_out = sb("b_out", [P, D])
    x_in = sb("x_in", [P, 2, D])
    xb = sb("xb", [P, 2, D])
    x_out = sb("x_out", [P, 2, D])
    w_qkv = sb("w_qkv", [P, 3 * INNER])
    w_out = sb("w_out", [P, PAIRS, D])
    cos = sb("cos", [P, HD])
    sin = sb("sin", [P, HD])
    dgb = sb("dgb", [2 * AH, B])
    ugb = sb("ugb", [P, 2, B])
    half = sb("half", [P, 1])
    eps = sb("eps", [P, 1])

    gated = sb("gated", [2 * AH, P])
    act = sb("act", [AH, P])
    ups = sb("ups", [P, 2, P])
    hres = sb("hres", [P, P])
    stats = sb("stats", [P, 6])
    mv = sb("mv", [P, 2])
    veps = sb("veps", [P, 1])
    rstd = sb("rstd", [P, 1])
    xn = sb("xn", [P, P])
    xnT = sb("xnT", [P, 2, P])
    rc = sb("rc", [P, 2, INNER])
    rs = sb("rs", [P, 2, INNER])
    rot = sb("rot", [P, 2, INNER])
    qT = sb("qT", [P, PAIRS, P])
    kbd = sb("kbd", [P, PAIRS, GB, 2, N])
    v = sb("v", [P, 2, INNER])
    mx = sb("mx", [P, HEADS])
    sc = sb("sc", [P, HEADS, N])
    ex = sb("ex", [P, HEADS, N])
    sm = sb("sm", [P, HEADS])
    rsm = sb("rsm", [P, HEADS])
    pr = sb("pr", [P, HEADS, N])
    pbd = sb("pbd", [P, HEADS, P])
    oT = sb("oT", [P, PAIRS, P])

    def sem(name):
        return ctx.enter_context(nc.semaphore("p1_" + name))

    loaded = sem("loaded")
    loaded_w = sem("loaded_w")
    LOADS, LOADS_W = 13 * 16, 2 * 16
    zeroed = sem("zeroed")
    ZEROED = 6
    s_pe = Steps(sem("setup_pe"), "gates")
    s_act = Steps(sem("setup_act"), "dgb ugb")
    a_pe = Steps(sem("adapter_pe"), "down fold up sum xnT")
    a_dve = Steps(sem("adapter_dve"), "gated ups hres stats mv xn")
    a_act = Steps(sem("adapter_act"), "act xnT")
    x_read = [sem("x_read_even"), sem("x_read_odd")]
    x_written = [sem("x_written_even"), sem("x_written_odd")]
    e_pool = Steps(sem("bias_pool"), "xb")
    a_pool = Steps(sem("adapter_pool"), "veps rstd")
    b_pe = Steps(sem("qk_pe"), "q k qT kT")
    b_dve = Steps(sem("rope_dve"), "qc qs1 qs2 kc ks1 ks2")
    b_pool = Steps(sem("rope_pool"), "q k")
    b_act = Steps(sem("qk_act"), "qT k0 k1")
    c_pe = Steps(sem("scores_pe"), "scores v")
    c_act = Steps(sem("scores_act"), "v exp")
    c_dve = Steps(sem("softmax_dve"), "max sub sum rsum")
    c_pool = Steps(sem("softmax_pool"), "probs")
    d_dve = Steps(sem("out_dve"), "probsT x1")
    d_pe = Steps(sem("out_pe"), "pv y")
    d_act = Steps(sem("out_act"), "oT")

    ps = ctx.enter_context(nc.psum_tensor("p1_ps", [P, 8, 512], F32))

    def two_banks(k):
        return ps[:, k:k + 2, :].rearrange("p a b -> p (a b)")

    psX, psY, psZ = two_banks(0), two_banks(2), two_banks(4)
    psS, psA = ps[:, 6, :], ps[:, 7, :]

    block = ctx.enter_context(nc.Block())

    def pipeline(stages):

        def turn(t, u, k):
            stages(t, u, k, *(not isinstance(t, int) or 0 <= t + d < TILES for d in (2, 1, 0, -1)))

        return turn

    FIRST, LAST = 2, TILES - 2

    def run(eng, turn):
        for t in range(-2, FIRST):
            turn(t, t % 2, t // 2)
        with eng.Fori(FIRST // 2, LAST // 2) as two:
            turn(two * 2, 0, two)
            turn(two * 2 + 1, 1, two)
        for t in range(LAST, TILES + 1):
            turn(t, t % 2, t // 2)

    @block.sync
    def _(sp):
        for dst, src in ((condT, "condT"), (w_dgb, "dgb"), (w_ugb, "ugb"), (w_down[:, 0:AH], "down"),
                         (w_up[:, 0, :], "up"), (fold, "fold"), (ident, "ident"), (ln_gb, "ln_gb"),
                         (b_out, "b_out"), (cos, "cos"), (sin, "sin")):
            sp.dma_start(dst if dst.__class__ is bass.AP else dst[:], dram[src]).then_inc(loaded, 16)
        for c in range(2):
            sp.dma_start(xT[:, c * TOK // 2:(c + 1) * TOK // 2], dram["xT"][:, c * TOK // 2:(c + 1) * TOK // 2]).then_inc(loaded, 16)
        sp.dma_start(w_qkv[:], dram["w_qkv"]).then_inc(loaded_w, 16)
        sp.dma_start(w_out[:], dram["w_out"]).then_inc(loaded_w, 16)

        def turn(t, u, k, A, Bq, Cs, Do):
            if A:
                wait_if(sp, e_pool, "xb", t)
                sp.dma_start(x_in[:, u, :], dram["x"][bass.ds((t + 2) * P, P), :]).then_inc(x_read[u], 16)
            if Do:
                sp.wait_ge(*d_dve.done("x1", t - 1))
                sp.dma_start(x1[bass.ds((t - 1) * P, P), :], x_out[:, (u + 1) % 2, :]).then_inc(x_written[(u + 1) % 2], 16)

        run(sp, pipeline(turn))
        for w in x_written:
            sp.wait_ge(w, 16 * (TILES // 2))

    @block.tensor
    def _(pe):
        pe.wait_ge(loaded, LOADS)
        pe.wait_ge(loaded_w, LOADS_W)
        pe.wait_ge(zeroed, ZEROED)
        nc.tensor.matmul(psX[0:2 * AH, 0:B], w_dgb[:], condT[:], start=True, stop=True)
        for i in range(2):
            last = nc.tensor.matmul(psY[:, i * B:(i + 1) * B], w_ugb[:, i, :], condT[:], start=True, stop=True)
        last.then_inc(s_pe("gates"), 1)
        pe.wait_ge(*s_act.done("ugb"))

        def turn(t, u, k, A, Bq, Cs, Do):
            ta, tb, td = t + 2, t + 1, t - 1
            if A:
                wait_if(pe, a_act, "xnT", ta - 1)
                nc.tensor.matmul(psA[0:2 * AH, 0:P], w_down[:], xT[:, bass.ds(ta * P, P)], start=True,
                                 stop=True).then_inc(a_pe("down"), 1)
            if Bq:
                pe.wait_ge(*a_act.done("xnT", tb))
                wait_if(pe, b_act, "qT", tb - 1)
                for j in range(2):
                    last = nc.tensor.matmul(psX[:, j * 512:(j + 1) * 512], xnT[:, (u + 1) % 2, :],
                                            w_qkv[:, j * 512:(j + 1) * 512], start=True, stop=True)
                last.then_inc(b_pe("q"), 1)
            if A:
                pe.wait_ge(*a_dve.done("gated", ta))
            if Cs:
                pe.wait_ge(*b_act.done("k1", t))
                wait_if(pe, d_dve, "x1", t - 2)
                for p in range(PAIRS):
                    for b in range(GB):
                        last = nc.tensor.matmul(psS[b * N:(b + 1) * N, p * 2 * N:(p + 1) * 2 * N],
                                                qT[:, p, b * N:(b + 1) * N], kbd[:, p, b, :, :],
                                                start=True, stop=True)
                last.then_inc(c_pe("scores"), 1)
            if A:
                nc.tensor.matmul(psA[0:AH, 128:256], fold[:], gated[:], start=True, stop=True).then_inc(a_pe("fold"), 1)
            if Bq:
                wait_if(pe, b_act, "k1", tb - 1)
                for j in range(2):
                    last = nc.tensor.matmul(psY[:, j * 512:(j + 1) * 512], xnT[:, (u + 1) % 2, :],
                                            w_qkv[:, INNER + j * 512:INNER + (j + 1) * 512], start=True, stop=True)
                last.then_inc(b_pe("k"), 1)
            if A:
                pe.wait_ge(*a_act.done("act", ta))
                for i in range(2):
                    last = nc.tensor.matmul(psA[:, 256 + i * P:256 + (i + 1) * P], w_up[:, i, :], act[:],
                                            start=True, stop=True)
                last.then_inc(a_pe("up"), 1)
            if Cs:
                wait_if(pe, d_act, "oT", t - 2)
                for j in range(2):
                    last = nc.tensor.matmul(psZ[:, j * 512:(j + 1) * 512], xnT[:, u, :],
                                            w_qkv[:, 2 * INNER + j * 512:2 * INNER + (j + 1) * 512],
                                            start=True, stop=True)
                last.then_inc(c_pe("v"), 1)
            if A:
                pe.wait_ge(*a_dve.done("hres", ta))
                nc.tensor.matmul(psA[:, 0:P], hres[:], ident[:], start=True, stop=False)
                nc.tensor.matmul(psA[:, 0:P], ups[:, 1, :], ident[:], start=False, stop=True).then_inc(a_pe("sum"), 1)
            if Bq:
                pe.wait_ge(*b_pool.done("q", tb))
                for p in range(PAIRS):
                    last = nc.tensor.transpose(psX[:, p * P:(p + 1) * P], rot[:, 0, p * P:(p + 1) * P], ident[:])
                last.then_inc(b_pe("qT"), 1)
            if Do:
                pe.wait_ge(*d_dve.done("probsT", td))
                if Cs:
                    pe.wait_ge(*c_act.done("v", t))
                for h in range(HEADS):
                    last = nc.tensor.matmul(psZ[h % 2 * HD:(h % 2 + 1) * HD, h // 2 * P:(h // 2 + 1) * P],
                                            v[:, (u + 1) % 2, h * HD:(h + 1) * HD], pbd[:, h, :], start=True, stop=True)
                last.then_inc(d_pe("pv"), 1)
            if A:
                pe.wait_ge(*a_dve.done("xn", ta))
                nc.tensor.transpose(psA[:, 128:256], xn[:], ident[:]).then_inc(a_pe("xnT"), 1)
            if Bq:
                pe.wait_ge(*b_pool.done("k", tb))
                for p in range(PAIRS):
                    last = nc.tensor.transpose(psY[:, p * P:(p + 1) * P], rot[:, 1, p * P:(p + 1) * P], ident[:])
                last.then_inc(b_pe("kT"), 1)
            if Do:
                pe.wait_ge(*d_act.done("oT", td))
                if Cs:
                    pe.wait_ge(*c_dve.done("sub", t))
                for p in range(PAIRS):
                    last = nc.tensor.matmul(psS[:, 0:P], oT[:, p, :], w_out[:, p, :], start=(p == 0), stop=(p == PAIRS - 1))
                last.then_inc(d_pe("y"), 1)

        run(pe, pipeline(turn))

    @block.scalar
    def _(sc_):
        sc_.wait_ge(*s_pe.done("gates"))
        nc.scalar.activation(dgb[:], psX[0:2 * AH, 0:B], ACT.Copy).then_inc(s_act("dgb"), 1)
        nc.scalar.activation(ugb[:], psY[:, 0:2 * B].rearrange("p (i b) -> p i b", i=2), ACT.Copy).then_inc(s_act("ugb"), 1)

        def turn(t, u, k, A, Bq, Cs, Do):
            ta, tb, td = t + 2, t + 1, t - 1
            if A:
                sc_.wait_ge(*a_pe.done("fold", ta))
                wait_if(sc_, a_pe, "up", ta - 1)
                nc.scalar.activation(act[:], psA[0:AH, 128:256], ACT.Relu).then_inc(a_act("act"), 1)
            if Cs:
                sc_.wait_ge(*c_pe.done("v", t))
                wait_if(sc_, d_pe, "pv", t - 2)
                nc.scalar.activation(v[:, u, :], psZ, ACT.Copy).then_inc(c_act("v"), 1)
                sc_.wait_ge(*c_dve.done("sub", t))
                wait_if(sc_, c_pool, "probs", t - 1)
                nc.scalar.activation(ex[:], sc[:], ACT.Exp, scale=float(HD) ** -0.5).then_inc(c_act("exp"), 1)
            if Bq:
                sc_.wait_ge(*b_pe.done("qT", tb))
                nc.scalar.activation(qT[:].rearrange("p a b -> p (a b)"), psX, ACT.Copy).then_inc(b_act("qT"), 1)
            if Do:
                sc_.wait_ge(*d_pe.done("pv", td))
                wait_if(sc_, d_pe, "y", td - 1)
                nc.scalar.activation(oT[:].rearrange("p a b -> p (a b)"), psZ, ACT.Copy).then_inc(d_act("oT"), 1)
            if A:
                sc_.wait_ge(*a_pe.done("xnT", ta))
                wait_if(sc_, c_pe, "v", ta - 2)
                nc.scalar.activation(xnT[:, u, :], psA[:, 128:256], ACT.Identity, scale=ln_gb[:, 0:1],
                                     bias=ln_gb[:, 1:2]).then_inc(a_act("xnT"), 1)
            if Bq:
                sc_.wait_ge(*b_pe.done("kT", tb))
                wait_if(sc_, c_pe, "scores", tb - 1)
                for h in range(2):
                    rows = slice(h * HD, (h + 1) * HD)
                    nc.scalar.activation(kbd[rows, :, :, h, :].rearrange("p a b n -> p (a b) n"),
                                         psY[rows, :].rearrange("p (c n) -> p c n", n=N), ACT.Copy).then_inc(b_act(f"k{h}"), 1)

        run(sc_, pipeline(turn))

    @block.gpsimd
    def _(pool):
        nc.gpsimd.memset(half[:], -0.5).then_inc(zeroed, 1)
        nc.gpsimd.memset(eps[:], 1e-5).then_inc(zeroed, 1)
        nc.gpsimd.memset(w_down[:, AH:], 1.0).then_inc(zeroed, 1)
        nc.gpsimd.memset(w_up[:, 1, :], 1.0).then_inc(zeroed, 1)
        nc.gpsimd.memset(kbd[:], 0.0).then_inc(zeroed, 1)
        nc.gpsimd.memset(pbd[:], 0.0).then_inc(zeroed, 1)
        pool.wait_ge(zeroed, ZEROED)

        def turn(t, u, k, A, Bq, Cs, Do):
            ta, tb, td = t + 2, t + 1, t - 1
            if Bq:
                pool.wait_ge(*b_dve.done("qs2", tb))
                wait_if(pool, b_pe, "qT", tb - 1)
                nc.gpsimd.tensor_tensor(rot[:, 0, :], rc[:, 0, :], rs[:, 0, :], ALU.add).then_inc(b_pool("q"), 1)
            if A:
                pool.wait_ge(*a_dve.done("mv", ta))
                nc.gpsimd.tensor_tensor(veps[:], mv[:, 1:2], eps[:], ALU.add).then_inc(a_pool("veps"), 1)
                pool.wait_ge(*a_pool.done("veps", ta))
                wait_if(pool, a_dve, "xn", ta - 1)
                nc.gpsimd.tensor_tensor(rstd[:], veps[:], half[:], ALU.pow).then_inc(a_pool("rstd"), 1)
            if Bq:
                pool.wait_ge(*b_dve.done("ks2", tb))
                wait_if(pool, b_pe, "kT", tb - 1)
                nc.gpsimd.tensor_tensor(rot[:, 1, :], rc[:, 1, :], rs[:, 1, :], ALU.add).then_inc(b_pool("k"), 1)
            if Cs:
                pool.wait_ge(x_read[u], (k + 1) * 16)
                wait_if(pool, d_dve, "x1", t - 2)
                nc.gpsimd.tensor_tensor(xb[:, u, :], x_in[:, u, :], b_out[:], ALU.add).then_inc(e_pool("xb"), 1)
                pool.wait_ge(*c_dve.done("rsum", t))
                wait_if(pool, d_dve, "probsT", t - 1)
                nc.gpsimd.tensor_tensor(pr[:], ex[:], rsm[:].unsqueeze(2).broadcast_to([P, HEADS, N]),
                                        ALU.mult).then_inc(c_pool("probs"), 1)

        run(pool, pipeline(turn))

    @block.vector
    def _(dve):
        dve.wait_ge(*s_act.done("ugb"))

        def rope(t, i, psum, made, free):
            name = "qk"[i]
            dve.wait_ge(*b_pe.done(name, t))
            wait_if(dve, b_pool, name, t - 1)
            q3 = psum.rearrange("p (h f) -> p h f", f=HD)
            nc.vector.tensor_tensor(rc[:, i, :].rearrange("p (h f) -> p h f", f=HD), q3,
                                    cos[:].unsqueeze(1).broadcast_to([P, HEADS, HD]), ALU.mult).then_inc(b_dve(name + "c"), 1)
            r3 = rs[:, i, :].rearrange("p (h f) -> p h f", f=HD)
            for j in range(2):
                out, other = slice(j * HALF, (j + 1) * HALF), slice((1 - j) * HALF, (2 - j) * HALF)
                nc.vector.tensor_tensor(r3[:, :, out], q3[:, :, other],
                                        sin[:, out].unsqueeze(1).broadcast_to([P, HEADS, HALF]),
                                        ALU.mult).then_inc(b_dve(f"{name}s{j + 1}"), 1)

        def turn(t, u, k, A, Bq, Cs, Do):
            ta, tb, td = t + 2, t + 1, t - 1
            if A:
                dve.wait_ge(*a_pe.done("down", ta))
                wait_if(dve, a_pe, "fold", ta - 1)
                nc.vector.tensor_tensor(gated[:].rearrange("p (b n) -> p b n", b=GB),
                                        psA[0:2 * AH, 0:P].rearrange("p (b n) -> p b n", b=GB),
                                        dgb[:, bass.ds(ta * GB, GB)].unsqueeze(2).broadcast_to([2 * AH, GB, N]),
                                        ALU.mult).then_inc(a_dve("gated"), 1)
            if Do:
                dve.wait_ge(*c_pool.done("probs", td))
                wait_if(dve, d_pe, "pv", td - 1)
                for b in range(GB):
                    rows = slice(b * N, (b + 1) * N)
                    last = nc.vector.transpose(pbd[rows, :, rows], pr[rows, :, :])
                last.then_inc(d_dve("probsT"), 1)
            if Bq:
                rope(tb, 0, psX, None, None)
            if Cs:
                dve.wait_ge(*c_pe.done("scores", t))
                wait_if(dve, c_dve, "sub", t - 1)
                s3 = psS.rearrange("p (h n) -> p h n", n=N)
                nc.vector.tensor_reduce(mx[:], s3, AX, ALU.max).then_inc(c_dve("max"), 1)
                dve.wait_ge(*c_dve.done("max", t))
                wait_if(dve, c_act, "exp", t - 1)
                nc.vector.tensor_tensor(sc[:], s3, mx[:].unsqueeze(2).broadcast_to([P, HEADS, N]),
                                        ALU.subtract).then_inc(c_dve("sub"), 1)
            if A:
                dve.wait_ge(*a_pe.done("up", ta))
                wait_if(dve, a_pe, "sum", ta - 1)
                nc.vector.tensor_tensor(ups[:].rearrange("p i (b n) -> p i b n", b=GB),
                                        psA[:, 256:512].rearrange("p (i b n) -> p i b n", i=2, b=GB),
                                        ugb[:, :, bass.ds(ta * GB, GB)].unsqueeze(3).broadcast_to([P, 2, GB, N]),
                                        ALU.mult).then_inc(a_dve("ups"), 1)
                dve.wait_ge(*a_dve.done("ups", ta))
                nc.vector.tensor_tensor(hres[:], ups[:, 0, :], xT[:, bass.ds(ta * P, P)], ALU.add).then_inc(a_dve("hres"), 1)
            if Bq:
                rope(tb, 1, psY, None, None)
            if A:
                dve.wait_ge(*a_pe.done("sum", ta))
                nc.vector.bn_stats(stats[:], psA[:, 0:P]).then_inc(a_dve("stats"), 1)
                dve.wait_ge(*a_dve.done("stats", ta))
                wait_if(dve, a_pool, "veps", ta - 1)
            if Cs:
                dve.wait_ge(*c_act.done("exp", t))
                nc.vector.tensor_reduce(sm[:], ex[:], AX, ALU.add).then_inc(c_dve("sum"), 1)
            if A:
                nc.vector.bn_aggr(mv[:], stats[:]).then_inc(a_dve("mv"), 1)
            if Cs:
                dve.wait_ge(*c_dve.done("sum", t))
                wait_if(dve, c_pool, "probs", t - 1)
                nc.vector.reciprocal(rsm[:], sm[:]).then_inc(c_dve("rsum"), 1)
            if A:
                dve.wait_ge(*a_pool.done("rstd", ta))
                wait_if(dve, a_pe, "xnT", ta - 1)
                nc.vector.tensor_scalar(xn[:], psA[:, 0:P], mv[:, 0:1], rstd[:, 0:1], ALU.subtract,
                                        ALU.mult).then_inc(a_dve("xn"), 1)
            if Do:
                dve.wait_ge(*d_pe.done("y", td))
                dve.wait_ge(*e_pool.done("xb", td))
                if not isinstance(td, int) or td >= 2:
                    dve.wait_ge(x_written[(u + 1) % 2], (k if u else k - 1) * 16)
                nc.vector.tensor_tensor(x_out[:, (u + 1) % 2, :], psS[:, 0:P], xb[:, (u + 1) % 2, :], ALU.add).then_inc(d_dve("x1"), 1)

        run(dve, pipeline(turn))



EXPERTS, HID = 8, 256
EX0 = EXPERTS + 1
TOP_K = 2
NC = 4
CH = NC * B
CHUNKS = N // NC
H1, D1 = 16, 8
OFF = H1 // 2 + 1
KDEC = 30
SYS = NC * H1
GATES = ("styleC", "styleK", "styleO")


UNITS0, UNITS = 2 * EX0, 2 * (EX0 + EXPERTS)
TG = 4

AT = dict(x2T=0, x3T=0, xk=1, kx=1, x3Ta=1, t0=1, kx0=2, t1=2, kxdup=3, t2=3, prod0=3, t3=4, sd0=4, prod1=5, t=5, z=5,
          sd1=6, za=6, sddup=6, zsq=6, sf1=7, ms=7, exp=7, sub=7, zn=8, znT=8, sum=8, znTa=9, r1=9, ap0=9, sub1=10, e1=10, av0=10, ranks1=11,
          ap1=11, av1=12, ap2=12, cw1=12, av2=13, ap3=13, av3=14, oT=14, xo=14, y=14, y1=15, y2T=15,
          q=15, sqq=15, k=16, sqk=16, v=17, va=17, ssq=17, fb=18, fb0=18, eps0=18, fbt=18, qk=19, g=19, gT=19, fb1=19, gate=19, gatea=19,
          bk=19, x1=18, U=19, Uk=20, xm=20, hk0=20, yy=20, dm=21, hk1=21, r0=21, hk2=22, sub0=22, e0=22, hk3=22, probs0=22, carry=22, diag=22,
          el0=23, ranks0=23, el1=24, cw0=24, el2=25, el3=26, el4=27, el5=27, el6=28, rhs=28, oprod=29, o1=30, og=30, ogsq=30,
          ss=31, ogrs=31, ogn=31, ogT=32, ogTa=32, x3m=33, x3=33)


def mixing_phase(nc, ctx, dram, x1, out):

    def sb(name, shape):
        return ctx.enter_context(nc.sbuf_tensor("p2_" + name, shape, F32))

    def sem(name):
        return ctx.enter_context(nc.semaphore("p2_" + name))

    ident = sb("ident", [P, P])
    half = sb("half", [P, 64])
    w2c = sb("w2c", [P, D])
    vecs = sb("vecs", [P, 8])
    w_r0, w_r1 = sb("w_r0", [P, EXPERTS]), sb("w_r1", [P, EXPERTS])
    w13 = sb("w13", [P, EX0, 2, HID])
    w2 = sb("w2", [P, EX0, 2, D])
    kwT, owT = sb("kwT", [P, D]), sb("owT", [P, D])
    wqkv1 = sb("wqkv1", [P, 3, D])
    wfb = sb("wfb", [P, 2 * H1])
    wo1 = sb("wo1", [P, D])
    g1 = sb("g1", [P, D1])
    g2 = sb("g2", [D1, D])
    rows = sb("rows", [P, 4, D])
    fbias = sb("fbias", [P, 2 * H1])
    bdec = sb("bdec", [P, KDEC])
    bdecb = sb("bdecb", [KDEC, 1])
    vmat = sb("vmat", [KDEC, D])
    w_up = sb("w_up", [P, EXPERTS, 2 * HID])
    w_dn = sb("w_dn", [P, EXPERTS, 2, D])
    tri = sb("tri", [P, 2, EXPERTS * EXPERTS])
    style = sb("style", [P, 3, B])
    demod = sb("demod", [P, 3, B])
    lam = sb("lam", [P, D])
    Uw = sb("Uw", [P, KDEC, B])
    Ub = sb("Ub", [KDEC, B])

    xs = sb("xs", [P, CH])
    xm = sb("xm", [P, CH])
    yT = sb("yT", [P, CH])
    ex8 = sb("ex8", [P, NC, EXPERTS])
    s8 = sb("s8", [P, NC, EXPERTS])
    m4 = sb("m4", [P, NC])
    p8 = sb("p8", [P, NC, EXPERTS])
    ge = sb("ge", [P, NC, EXPERTS * EXPERTS])
    gt = sb("gt", [P, NC, EXPERTS * EXPERTS])
    rank = sb("rank", [P, NC, EXPERTS])
    cw0 = sb("cw0", [P, NC, EX0])
    cw1 = sb("cw1", [P, NC, EXPERTS])
    sil = sb("sil", [P, 2, CH])
    hid = sb("hid", [P, 2, CH])
    ssq = sil[:, 0, 0:3 * B].rearrange("p (i b) -> p i b", i=3)
    wsq = hid[:, 0, 0:3 * B].rearrange("p (i b) -> p i b", i=3)
    acc0 = sb("acc0", [P, CH])
    x2 = sb("x2", [P, CH])
    ltmp = acc0[:, 0:D]
    xk = sb("xk", [P, CH])
    kx0 = sb("kx0", [P, CH])
    kx = sb("kx", [P, NC, 2, D])
    prod = sb("prod", [P, (D1 - 1) * D1 * SYS])
    sd = sb("sd", [P, NC, OFF, 2, H1])
    sf = sb("sf", [P, NC, H1, H1])
    mxh = sb("mxh", [P, NC, H1])
    smh = sb("smh", [P, NC, H1])
    rsh = sb("rsh", [P, NC, H1])
    mixed = sb("mixed", [P, CH])
    y2T = sb("y2T", [P, CH])
    ssr = sb("ssr", [P, 2, SYS])
    rn = sb("rn", [P, 2, SYS])
    kv = sb("kv", [P, 2 * D1, SYS])
    fb0 = sb("fb0", [P, NC, 2, H1])

    fb = fbt = sb("fb", [P, NC, 2, H1])
    bk = sb("bk", [P, D1, SYS])
    Hv = sb("Hv", [P, D1 * D1, NC, H1])
    carry = sb("carry", [P, 2, D1 * D1, H1])
    A = sb("A", [P, D1, D1 + 1, SYS])
    poolT = sb("poolT", [P, D1 * D1 * H1])
    T = prod[:].rearrange("p (a s) -> p a s", s=SYS)
    early = A[0:C, :, :, :].rearrange("p i j s -> p (i j s)")
    WDEC, AFF = (D + 1) * KDEC, 3 * D
    wdec = early[:, 0:WDEC]
    aff = early[:, WDEC:WDEC + AFF].rearrange("c (i d) -> c i d", i=3)
    condT = early[:, WDEC + AFF:WDEC + AFF + B]
    A4 = A[:].rearrange("p i j (n h) -> p i j n h", n=NC)
    gT = sb("gT", [D1, CH])
    gate = sb("gate", [P, CH])
    sqr = (mixed, gate)
    o1 = sb("o1", [P, CH])
    og = kx0
    ogT = xk
    x3 = sb("x3", [P, CH])
    x3T = sb("x3T", [P, CH])
    tK = sb("tK", [KDEC, NC, B])
    z = sb("z", [P, CH])
    ms4 = sb("ms4", [P, 2, NC])
    zn = sb("zn", [P, CH])
    res = sb("res", [P, CH])
    znT = x3T
    tiny = sb("tiny", [P, SYS])
    neps = sb("neps", [P, 3, SYS])

    loaded = sem("loaded")
    zeroed = sem("zeroed")
    S = {}
    su_pe = Steps(sem("gates_pe"), "gates sums uw")
    su_dve = Steps(sem("gates_dve"), "st0 st1 st2 ssq0 ssq1 ssq2 wsq0 wsq1 wsq2 dem0 dem1 dem2 l0 l1 l2 nw uw ub")
    su_act = Steps(sem("gates_act"), "e ln")
    su_pool = Steps(sem("gates_pool"), "dem")
    UG = [(g, min(g + 4, KDEC)) for g in range(0, KDEC, 4)]
    su_u = Steps(sem("uw_pe"), " ".join(f"g{i}" for i in range(len(UG))))
    su_v = Steps(sem("uw_dve"), " ".join(f"g{i}" for i in range(len(UG))))

    x_read = sem("x_read")
    res_free = sem("res_free")
    up = Steps(sem("up"), " ".join(f"a{g} b{g}" for g in range(UNITS)))
    silu = Steps(sem("silu"), " ".join(f"s{g}" for g in range(UNITS)))
    mul = Steps(sem("mul"), " ".join(f"h{g}" for g in range(UNITS)))
    down = Steps(sem("down"), " ".join(f"d{g}" for g in range(UNITS)))
    acc = Steps(sem("acc"), " ".join(f"x{e}" for e in range(UNITS // 2)))
    in_pe = Steps(sem("in_pe"), "x3T " + " ".join(f"t{j}" for j in range(TG)) + " z znT r1 x1 y r0")
    in_act = Steps(sem("in_act"), "x3T z znT e1 e0")
    in_dve = Steps(sem("in_dve"), "t ms " + " ".join(f"zn{n}" for n in range(NC)) + " max1 sub1 raw ge1 gel1 gt1 gtu1 cmp1 rank1 em sum1 rsum1 cw1"
                   " xm dm bias yT max0 sub0 sum0 rsum0 probs ge0 gel0 gt0 gtu0 cmp0 rank0 rk2 cw0")
    in_pool = Steps(sem("in_pool"), "sq mean eps rs base")
    k_pe = Steps(sem("k_pe"), "x2T kx oT y")
    k_dve = Steps(sem("k_dve"), "xk kx0 prod0 sd0 prod1 sd1 sf1 max sub sum rsum " + " ".join(f"ap{n} av{n}" for n in range(NC)) + " xo y1")
    k_pool = Steps(sem("k_pool"), "kx probs")
    k_act = Steps(sem("k_act"), "x2 kxdup sddup sf0 exp y2T")
    m_pe = Steps(sem("m_pe"), "q k v fb g gate ogT x3")
    m_act = Steps(sem("m_act"), "sqq q sqk k v fbt gT gate carry_k carry_v ogT")
    LOW = D1 - 2
    ELIM = " ".join(f"ri{k} " + (f"col{k} " if k < D1 - 1 else "") + (f"t{k} a{k}" if k < LOW - 1 or k == LOW else "") for k in range(D1))
    BACK = " ".join(f"bt{k} bx{k}" for k in range(D1 - 1, 0, -1))
    m_dve = Steps(sem("m_dve"), "ssq ssk fb0 q k fb bk Uk " + " ".join(f"mk{n} hk{n}" for n in range(NC)) + " diag " + ELIM + " rhs " + BACK
                  + " oprod o1 og ss ogn x3")
    m_pool = Steps(sem("m_pool"), "eps0 rqk U " + " ".join(f"mv{n} hv{n}" for n in range(NC)) + " " + " ".join(f"lt{k} la{k}" for k in range(LOW))
                   + " sq ms eps rs og2")
    stored = sem("stored")

    ps = ctx.enter_context(nc.psum_tensor("p2_ps", [P, 8, 512], F32))
    psU, psDn = ps[:, 0:4, :], ps[:, 4:6, :]
    ps6, ps7 = ps[:, 6, :], ps[:, 7, :]

    def by_n(ap):
        return ap.rearrange("p (n b) -> p n b", n=NC)

    def bc_n(ap, parts=P):
        return ap.unsqueeze(1).broadcast_to([parts, NC, ap.shape[-1]])

    block = ctx.enter_context(nc.Block())
    loads = [(ident, "ident"), (condT, "condT"), (w2c, "w2c"), (vecs, "vecs"), (w_r0, "w_r0"), (w_r1, "w_r1"),
             (aff, "aff"), (kwT, "kwT"), (owT, "owT"), (wqkv1, "wqkv1"), (wfb, "wfb"), (wo1, "wo1"), (g1, "g1"),
             (g2, "g2"), (rows, "rows"), (fbias, "fbias"), (wdec, "wdec"), (bdec, "bdec"), (bdecb, "bdecb"),
             (vmat, "vmat"), (tri, "tri"), (w13, "w13"), (w2, "w2"), (w_up, "w_up1"), (w_dn, "w_dn1")]
    LOADED = 16 * len(loads)
    ZEROED = 4
    STYLE, SCALE_C = range(3), 0.125

    def active(g, F, G):
        return F if g < UNITS0 else G

    def earlier(g, d, t, F):
        if g >= UNITS0 and g - d < UNITS0 and not F:
            g -= UNITS0
        T = t + 1
        if g - d >= 0:
            return g - d, T
        if isinstance(T, int) and T < 1:
            return None
        return UNITS + g - d, T - 1

    def wait_unit(eng, steps, name, g, d, t, F):
        before = earlier(g, d, t, F)
        if before:
            eng.wait_ge(*steps.done(name + str(before[0]), before[1]))

    def fill(name, g, G):
        return name + str(UNITS - 1) if g == UNITS0 - 1 and not G else None

    class Slots:

        def __init__(self, unit):
            self.unit, self.next, self.at = unit, 0, 0

        def __call__(self, step):
            assert AT[step] >= self.at, (step, self.at)
            self.at = AT[step]
            self.up_to(self.at)

        def up_to(self, count):
            while self.next < count:
                self.unit(self.next)
                self.next += 1

    def run(eng, turn):
        def flags(t):
            return [0 <= t + d < CHUNKS for d in (2, 1, 0, -1)]

        for t in range(-2, 1):
            turn(t, *flags(t))
        with eng.Fori(1, CHUNKS - 2) as t:
            turn(t, True, True, True, True)
        for t in range(CHUNKS - 2, CHUNKS + 1):
            turn(t, *flags(t))

    @block.sync
    def _(sp):
        for dst, name in loads:
            sp.dma_start(dst if dst.__class__ is bass.AP else dst[:], dram[name]).then_inc(loaded, 16)

        def turn(t, I, F, M, G):
            if I:
                if F:
                    sp.wait_ge(*acc.done("x0", t + 1))
                sp.dma_start(xs[:], x1[:, bass.ds((t + 2) * CH, CH)]).then_inc(x_read, 16)
            if G:
                sp.wait_ge(*acc.done(f"x{UNITS // 2 - 1}", t + 1))
                sp.dma_start(out[:, bass.ds((t - 1) * CH, CH)], res[:]).then_inc(res_free, 16)

        run(sp, turn)
        sp.wait_ge(res_free, 16 * (CHUNKS + 1))

    @block.tensor
    def _(pe):
        pe.wait_ge(loaded, LOADED)
        for i in STYLE:
            last = nc.tensor.matmul(ps6[:, i * B:(i + 1) * B], aff[:, i, :], condT, start=True, stop=True)
        last.then_inc(su_pe("gates"), 1)
        pe.wait_ge(*su_dve.done("wsq2"))
        nc.tensor.matmul(ps7[:, 0:B], wsq[:, 0, :], ssq[:, 0, :], start=True, stop=True)
        nc.tensor.matmul(ps7[:, B:2 * B], ssq[:, 1, :], wsq[:, 1, :], start=True, stop=True)
        nc.tensor.matmul(ps7[:, 2 * B:3 * B], wsq[:, 2, :], ssq[:, 2, :], start=True, stop=True).then_inc(su_pe("sums"), 1)
        wk = wdec.rearrange("c (i k) -> c k i", k=KDEC)
        for g, (lo, hi) in enumerate(UG):
            if g:
                pe.wait_ge(*su_v.done(f"g{g - 1}"))
            for k in range(lo, hi):
                last = nc.tensor.matmul(ps6[:, (k - lo) * B:(k - lo + 1) * B], wk[:, k, 0:D], condT, start=True, stop=True)
            last.then_inc(su_u(f"g{g}"), 1)
        pe.wait_ge(*su_dve.done("dem2"))
        nc.tensor.matmul(ps7[0:KDEC, 0:B], wk[:, :, D], condT, start=True, stop=True).then_inc(su_pe("uw"), 1)
        pe.wait_ge(*su_dve.done("ub"))

        def turn(t, I, F, M, G):
            U, N2 = t + 1, t + 2

            def unit(g):
                if g < UNITS and active(g, F, G):
                    if g == 0:
                        pe.wait_ge(*in_dve.done("yT", N2 - 1))
                    if g == UNITS0:
                        pe.wait_ge(*in_act.done("znT", N2))
                    wait_unit(pe, mul, "h", g, 2, t, F)
                    q, x_in = g % 2, yT if g < UNITS0 else x3T
                    if g < UNITS0:
                        wa, wb = (w13[:, g // 2, i, g % 2 * P:(g % 2 + 1) * P] for i in (0, 1))
                    else:
                        wa, wb = (w_up[:, (g - UNITS0) // 2, i * HID + g % 2 * P:i * HID + (g % 2 + 1) * P] for i in (1, 0))
                    nc.tensor.matmul(psU[:, 2 * q, :], wa, x_in[:], start=True, stop=True).then_inc(*up.step(f"a{g}"))
                    nc.tensor.matmul(psU[:, 2 * q + 1, :], wb, x_in[:], start=True, stop=True).then_inc(*up.step(f"b{g}", fill("b", g, G)))
                j = g - 1
                if j >= 0 and active(j, F, G):
                    e, half_ = j // 2, j % 2
                    pe.wait_ge(*mul.done(f"h{j}", U))
                    if half_ == 0:
                        before = earlier(j, 4, t, F)
                        if before:
                            pe.wait_ge(*acc.done(f"x{before[0] // 2}", before[1]))
                    w = w2[:, e, half_, :] if j < UNITS0 else w_dn[:, e - EX0, half_, :]
                    for n in range(NC):
                        last = nc.tensor.matmul(psDn[:, e % 2, n * P:(n + 1) * P], hid[:, half_, n * P:(n + 1) * P], w,
                                                start=(half_ == 0 and n == 0), stop=(half_ == 1), skip_group_check=True)
                    last.then_inc(*down.step(f"d{j}", fill("d", j, G)))

            to = Slots(unit)

            def four(ps_, lhsT, rhs):
                for n in range(NC):
                    last = nc.tensor.matmul(ps_[:, n * P:(n + 1) * P], lhsT[:, n * P:(n + 1) * P], rhs, start=True, stop=True)
                return last

            def turned(ps_, x):
                for n in range(NC):
                    last = nc.tensor.transpose(ps_[:, n * P:(n + 1) * P], x[:, n * P:(n + 1) * P], ident[:])
                return last

            def generated(j):
                for b in range(j * B // TG, (j + 1) * B // TG):
                    last = nc.tensor.matmul(ps7[0:KDEC, b * NC:(b + 1) * NC], Uw[:, :, b], by_n(x3T[:])[:, :, b], start=True, stop=True)
                last.then_inc(*in_pe.step(f"t{j}"))

            if M:
                pe.wait_ge(*acc.done(f"x{EX0 - 1}", U - 1))
                wait_if(pe, m_dve, "x3", t - 1)
                turned(ps6, acc0).then_inc(*k_pe.step("x2T"))
            if G:
                pe.wait_ge(*m_dve.done("x3", t - 1))
                pe.wait_ge(*in_dve.done("sub0", N2 - 1))
                turned(ps7, x3).then_inc(*in_pe.step("x3T"))
            if M:
                to("kx")
                pe.wait_ge(*k_dve.done("xk", t))
                four(ps6, xk, kwT[:]).then_inc(*k_pe.step("kx"))
            if G:
                to("t0")
                pe.wait_ge(*in_act.done("x3T", N2))
                for j in range(TG):
                    to(f"t{j}")
                    generated(j)
                to("z")
                pe.wait_ge(*in_dve.done("t", N2))
                for n in range(NC):
                    last = nc.tensor.matmul(ps7[:, n * P:(n + 1) * P], tK[:, n, :], vmat[:], start=True, stop=True)
                last.then_inc(*in_pe.step("z"))
                to("znT")
                pe.wait_ge(*in_dve.done(f"zn{NC - 1}", N2))
                pe.wait_ge(*in_act.done("z", N2))
                turned(ps7, zn).then_inc(*in_pe.step("znT"))
                to("r1")
                pe.wait_ge(*in_act.done("znT", N2))
                for n in range(NC):
                    last = nc.tensor.matmul(ps7[:, n * EXPERTS:(n + 1) * EXPERTS], x3T[:, n * P:(n + 1) * P], w_r1[:], start=True, stop=True)
                last.then_inc(*in_pe.step("r1", None if I else "r0"))
            if M:
                to("oT")
                pe.wait_ge(*k_dve.done(f"av{NC - 1}", t))
                turned(ps6, mixed).then_inc(*k_pe.step("oT"))
                to("y")
                pe.wait_ge(*k_dve.done("xo", t))
                nc.tensor.matmul(ps6, owT[:], xk[:], start=True, stop=True).then_inc(*k_pe.step("y"))
                to("q")
                pe.wait_ge(*k_act.done("y2T", t))
                for i, name in enumerate("qkv"):
                    to(name)
                    if i:
                        pe.wait_ge(*m_act.done("qk"[i - 1], t))
                    four(ps6, y2T, wqkv1[:, i, :]).then_inc(*m_pe.step(name))
                to("fb")
                pe.wait_ge(*m_act.done("v", t))
                for n in range(NC):
                    last = nc.tensor.matmul(ps6[:, n * 32:(n + 1) * 32], y2T[:, n * P:(n + 1) * P], wfb[:], start=True, stop=True)
                last.then_inc(*m_pe.step("fb"))
            if I:
                to("x1")
                pe.wait_ge(x_read, (t + 3) * 16)
                if G:
                    pe.wait_ge(*in_dve.done("raw", N2))
                elif t > -2:
                    pe.wait_ge(*in_dve.done("sub0", N2 - 1))
                turned(ps7, xs).then_inc(*in_pe.step("x1"))
            if M:
                to("g")
                pe.wait_ge(*m_dve.done("fb0", t))
                nc.tensor.matmul(ps6[0:D1, :], g1[:], y2T[:], start=True, stop=True).then_inc(*m_pe.step("g"))
                to("gate")
                pe.wait_ge(*m_act.done("gT", t))
                four(ps6, gT, g2[:]).then_inc(*m_pe.step("gate"))
            if I:
                to("yy")
                pe.wait_ge(*in_dve.done("xm", N2))
                nc.tensor.matmul(ps7, w2c[:], xm[:], start=True, stop=True).then_inc(*in_pe.step("y"))
                to("r0")
                pe.wait_ge(*in_dve.done("yT", N2))
                for n in range(NC):
                    last = nc.tensor.matmul(ps7[:, n * EXPERTS:(n + 1) * EXPERTS], yT[:, n * P:(n + 1) * P], w_r0[:], start=True, stop=True)
                last.then_inc(*in_pe.step("r0"))
            if M:
                to("ogT")
                pe.wait_ge(*m_pool.done("og2", t))
                turned(ps6, o1).then_inc(*m_pe.step("ogT"))
                to("x3m")
                pe.wait_ge(*m_act.done("ogT", t))
                four(ps6, ogT, wo1[:]).then_inc(*m_pe.step("x3"))
            to.up_to(UNITS + 1)

        run(pe, turn)

    @block.scalar
    def _(act):
        act.wait_ge(*su_dve.done("l0"))
        nc.scalar.activation(lam[:], ltmp, ACT.Exp).then_inc(su_act("e"), 1)
        act.wait_ge(*su_act.done("e"))
        nc.scalar.activation(ltmp, lam[:], ACT.Ln, bias=1.0).then_inc(su_act("ln"), 1)

        def copy(out_, in_, func=ACT.Copy, **kw):
            return nc.scalar.activation(out_, in_, func, **kw)

        def turn(t, I, F, M, G):
            U, N2 = t + 1, t + 2

            def unit(g):
                if active(g, F, G):
                    act.wait_ge(*up.done(f"a{g}", U))
                    wait_unit(act, mul, "h", g, 2, t, F)
                    copy(sil[:, g % 2, :], psU[:, 2 * (g % 2), :], ACT.Silu).then_inc(*silu.step(f"s{g}", fill("s", g, G)))

            to = Slots(unit)
            if M:
                act.wait_ge(*acc.done(f"x{EX0 - 1}", U - 1))
                wait_if(act, m_dve, "x3", t - 1)
                copy(x2[:], acc0[:]).then_inc(*k_act.step("x2"))
            if G:
                to("x3Ta")
                act.wait_ge(*in_pe.done("x3T", N2))
                copy(x3T[:], ps7).then_inc(*in_act.step("x3T"))
            if M:
                to("kxdup")
                act.wait_ge(*k_pool.done("kx", t))
                copy(kx[:, :, 1, :], kx[:, :, 0, :]).then_inc(*k_act.step("kxdup"))
                to("sddup")
                act.wait_ge(*k_dve.done(f"sd{NC // 2 - 1}", t))
                copy(sd[:, :, :, 1, :], sd[:, :, :, 0, :]).then_inc(*k_act.step("sddup"))
                copy(sf[:, :, 0:OFF, :], sd[:, :, :, 0, :]).then_inc(*k_act.step("sf0"))
            if G:
                to("za")
                act.wait_ge(*in_pe.done("z", N2))
                copy(z[:], ps7).then_inc(*in_act.step("z"))
            if M:
                to("exp")
                act.wait_ge(*k_dve.done("sub", t))
                copy(sf[:].rearrange("p n o h -> p (n o h)"), sf[:].rearrange("p n o h -> p (n o h)"), ACT.Exp,
                     scale=float(D1) ** -0.5).then_inc(*k_act.step("exp"))
            if G:
                to("znTa")
                act.wait_ge(*in_pe.done("znT", N2))
                copy(x3T[:], ps7).then_inc(*in_act.step("znT"))
                to("e1")
                act.wait_ge(*in_dve.done("sub1", N2))
                copy(ex8[:], s8[:], ACT.Exp).then_inc(*in_act.step("e1", None if I else "e0"))
            if M:
                to("y2T")
                act.wait_ge(*k_dve.done("y1", t))
                copy(y2T[:], kx0[:], ACT.Identity, bias=vecs[:, 1:2]).then_inc(*k_act.step("y2T"))
                planes = ps6.rearrange("p (n h j) -> p j n h", n=NC, h=H1)
                for i, name in enumerate("qk"):
                    to("sq" + name)
                    act.wait_ge(*m_pe.done(name, t))
                    copy(sqr[i][:], ps6, ACT.Square).then_inc(*m_act.step("sq" + name))
                    dst = A[:, :, D1, :] if i == 0 else kv[:, 0:D1, :]
                    if t.__class__ is not int or t > 0:
                        act.wait_ge(*m_pool.done(f"hv{NC - 1}", t - 1))
                    copy(dst.rearrange("p j (n h) -> p j n h", n=NC), planes).then_inc(*m_act.step(name))
                to("va")
                act.wait_ge(*m_pe.done("v", t))
                copy(kv[:, D1:2 * D1, :].rearrange("p j (n h) -> p j n h", n=NC), planes).then_inc(*m_act.step("v"))
                to("fbt")
                act.wait_ge(*m_dve.done("fb0", t))
                copy(fbt[:], fb0[:], ACT.Tanh, scale=0.5).then_inc(*m_act.step("fbt"))
                to("gT")
                act.wait_ge(*m_pe.done("g", t))
                copy(gT[:], ps6[0:D1, :]).then_inc(*m_act.step("gT"))
                to("gatea")
                act.wait_ge(*m_pe.done("gate", t))
                act.wait_ge(*m_dve.done("ssk", t))
                copy(gate[:], ps6, ACT.Tanh, scale=0.5).then_inc(*m_act.step("gate"))
                to("carry")
                act.wait_ge(*m_dve.done(f"hk{NC - 1}", t))
                copy(carry[:, 0, :, :].rearrange("p (i j) h -> p i j h", i=D1), A4[:, :, 0:D1, NC - 1, :]).then_inc(*m_act.step("carry_k"))
            if I:
                to("e0")
                act.wait_ge(*in_dve.done("sub0", N2))
                copy(ex8[:], s8[:], ACT.Exp).then_inc(*in_act.step("e0"))
            if M:
                to("oprod")
                act.wait_ge(*m_pool.done(f"hv{NC - 1}", t))
                copy(carry[:, 1, :, :], Hv[:, :, NC - 1, :]).then_inc(*m_act.step("carry_v"))
                to("ogTa")
                act.wait_ge(*m_pe.done("ogT", t))
                copy(ogT[:], ps6).then_inc(*m_act.step("ogT"))
            to.up_to(UNITS)

        run(act, turn)

    @block.gpsimd
    def _(pool):
        for dst, val in ((half, -0.5), (carry, 0.0), (cw0, 1.0 / (TOP_K + 1)), (tiny, 1e-6)):
            nc.gpsimd.memset(dst if dst.__class__ is bass.AP else dst[:], val).then_inc(zeroed, 1)
        nc.gpsimd.memset(res[:], 0.0).then_inc(res_free, 16)
        nc.gpsimd.memset(neps[:, 0, :], 1e-5).then_inc(zeroed, 1)
        nc.gpsimd.memset(neps[:, 1, :], 1.0 / (4 * D1)).then_inc(zeroed, 1)
        nc.gpsimd.memset(neps[:, 2, :], 1.0 / D).then_inc(zeroed, 1)
        pool.wait_ge(zeroed, ZEROED + 3)
        pool.wait_ge(*su_dve.done("dem2"))
        nc.gpsimd.tensor_tensor(demod[:], demod[:], half[:, 0:1].unsqueeze(1).broadcast_to([P, 3, B]), ALU.pow).then_inc(su_pool("dem"), 1)
        pool.wait_ge(*su_pool.done("dem"))

        tt = nc.gpsimd.tensor_tensor

        def turn(t, I, F, M, G):
            U, N2 = t + 1, t + 2
            if M:
                pool.wait_ge(*k_dve.done("kx0", t))
                tt(kx[:, :, 0, :], by_n(kx0[:]), bc_n(rows[:, 0, :]), ALU.add).then_inc(*k_pool.step("kx"))
            if G:
                pool.wait_ge(*in_act.done("z", N2))
                tt(zn[:], z[:], z[:], ALU.mult).then_inc(*in_pool.step("sq"))
                pool.wait_ge(*in_dve.done("ms", N2))
                tt(ms4[:, 0, :], ms4[:, 0, :], neps[:, 2, 0:NC], ALU.mult).then_inc(*in_pool.step("mean"))
                pool.wait_ge(*in_pool.done("mean", t - 1))
                tt(ms4[:, 0, :], ms4[:, 0, :], tiny[:, 0:NC], ALU.add).then_inc(*in_pool.step("eps"))
                pool.wait_ge(*in_pool.done("eps", t - 1))
                tt(ms4[:, 1, :], ms4[:, 0, :], half[:, 0:NC], ALU.pow).then_inc(*in_pool.step("rs"))
                pool.wait_ge(res_free, t * 16)
                tt(res[:], x3[:], z[:], ALU.add).then_inc(*in_pool.step("base"))
            if M:
                pool.wait_ge(*k_dve.done("rsum", t))
                tt(sf[:], sf[:], rsh[:].unsqueeze(2).broadcast_to([P, NC, H1, H1]), ALU.mult).then_inc(*k_pool.step("probs"))
                pool.wait_ge(*m_dve.done("ssk", t))
                tt(ssr[:], ssr[:], tiny[:].unsqueeze(1).broadcast_to([P, 2, SYS]), ALU.add).then_inc(*m_pool.step("eps0"))
                pool.wait_ge(*m_pool.done("eps0", t))
                tt(rn[:], ssr[:], half[:].unsqueeze(1).broadcast_to([P, 2, SYS]), ALU.pow).then_inc(*m_pool.step("rqk"))
                pool.wait_ge(*m_dve.done("bk", t))
                pool.wait_ge(*m_act.done("v", t))
                wait_if(pool, m_act, "carry_v", t - 1)
                tt(Hv[:].rearrange("p (i j) n h -> p i j (n h)", i=D1), bk[:].unsqueeze(2).broadcast_to([P, D1, D1, SYS]),
                   kv[:, D1:, :].unsqueeze(1).broadcast_to([P, D1, D1, SYS]), ALU.mult).then_inc(*m_pool.step("U"))
                pT = poolT[:].rearrange("p (a h) -> p a h", h=H1)
                for n in range(NC):
                    pool.wait_ge(*m_pool.done(f"hv{n - 1}" if n else "U", t))
                    tt(pT, carry[:, 1, :, :] if n == 0 else Hv[:, :, n - 1, :],
                       fb[:, n, 0, :].unsqueeze(1).broadcast_to([P, D1 * D1, H1]), ALU.mult).then_inc(*m_pool.step(f"mv{n}"))
                    pool.wait_ge(*m_pool.done(f"mv{n}", t))
                    tt(Hv[:, :, n, :], Hv[:, :, n, :], pT, ALU.add).then_inc(*m_pool.step(f"hv{n}"))
                lT = poolT[:, 0:2 * 3 * SYS].rearrange("p (i j s) -> p i j s", i=2, j=3)
                for k in range(LOW):
                    pool.wait_ge(*m_dve.done(f"col{k}", t))
                    pool.wait_ge(*m_pool.done(f"la{k - 1}" if k else f"hv{NC - 1}", t))
                    tt(lT, A[:, LOW:, k, :].unsqueeze(2).broadcast_to([P, 2, 3, SYS]),
                       A[:, k, LOW:, :].unsqueeze(1).broadcast_to([P, 2, 3, SYS]), ALU.mult).then_inc(*m_pool.step(f"lt{k}"))
                    pool.wait_ge(*m_pool.done(f"lt{k}", t))
                    tt(A[:, LOW:, LOW:, :], A[:, LOW:, LOW:, :], lT, ALU.subtract).then_inc(*m_pool.step(f"la{k}"))
                pool.wait_ge(*m_dve.done("og", t))
                tt(mixed[:], og[:], og[:], ALU.mult).then_inc(*m_pool.step("sq"))
                pool.wait_ge(*m_dve.done("ss", t))
                tt(ssr[:, 0, :], ssr[:, 0, :], neps[:, 1, :], ALU.mult).then_inc(*m_pool.step("ms"))
                pool.wait_ge(*m_pool.done("ms", t))
                tt(ssr[:, 0, :], ssr[:, 0, :], neps[:, 0, :], ALU.add).then_inc(*m_pool.step("eps"))
                pool.wait_ge(*m_pool.done("eps", t))
                tt(rn[:, 0, :], ssr[:, 0, :], half[:], ALU.pow).then_inc(*m_pool.step("rs"))
                pool.wait_ge(*m_dve.done("ogn", t))
                tt(by_n(o1[:]), by_n(o1[:]), bc_n(rows[:, 2, :]), ALU.mult).then_inc(*m_pool.step("og2"))

        run(pool, turn)

    @block.vector
    def _(dve):
        tt, red = nc.vector.tensor_tensor, nc.vector.tensor_reduce
        dve.wait_ge(loaded, LOADED)
        dve.wait_ge(zeroed, ZEROED + 3)
        dve.wait_ge(*su_pe.done("gates"))
        for i in STYLE:
            nc.vector.tensor_scalar(style[:, i, :], ps6[:, i * B:(i + 1) * B], SCALE_C if i == 0 else 1.0, vecs[:, 2 + i:3 + i],
                                    ALU.mult, ALU.add).then_inc(su_dve(f"st{i}"), 1)
        for i in STYLE:
            dve.wait_ge(*su_dve.done(f"st{i}"))
            tt(ssq[:, i, :], style[:, i, :], style[:, i, :], ALU.mult).then_inc(su_dve(f"ssq{i}"), 1)
        for i, w in enumerate((w2c, kwT, owT)):
            tt(wsq[:, i, :], w[:], w[:], ALU.mult).then_inc(su_dve(f"wsq{i}"), 1)
        dve.wait_ge(*su_pe.done("sums"))
        for i in STYLE:
            nc.vector.tensor_scalar(demod[:, i, :], ps7[:, i * B:(i + 1) * B], 1e-8, None, ALU.add).then_inc(su_dve(f"dem{i}"), 1)
        nc.vector.scalar_tensor_tensor(out=ltmp, in0=rows[:, 1, :], scalar=-1.0, in1=rows[:, 1, :], op0=ALU.mult,
                                       op1=ALU.min).then_inc(su_dve("l0"), 1)
        dve.wait_ge(*su_act.done("ln"))
        nc.vector.scalar_tensor_tensor(out=lam[:], in0=rows[:, 1, :], scalar=0.0, in1=ltmp, op0=ALU.max,
                                       op1=ALU.add).then_inc(su_dve("l1"), 1)
        dve.wait_ge(*su_dve.done("l1"))
        nc.vector.tensor_scalar(lam[:], lam[:], 0.25, None, ALU.add).then_inc(su_dve("l2"), 1)
        nc.vector.tensor_scalar(rows[:, 2, :], rows[:, 2, :], 0.5, None, ALU.mult).then_inc(su_dve("nw"), 1)
        for g, (lo, hi) in enumerate(UG):
            dve.wait_ge(*su_u.done(f"g{g}"))
            tt(Uw[:, lo:hi, :], ps6[:, 0:(hi - lo) * B].rearrange("p (k b) -> p k b", b=B),
               bdec[:, lo:hi].unsqueeze(2).broadcast_to([P, hi - lo, B]), ALU.add).then_inc(su_v(f"g{g}"), 1)
        dve.wait_ge(*su_v.done(f"g{len(UG) - 1}"))
        nc.vector.tensor_copy(ltmp[:, 0:1], vecs[:, 0:1]).then_inc(su_dve("uw"), 1)
        dve.wait_ge(*su_pe.done("uw"))
        nc.vector.tensor_scalar(Ub[:], ps7[0:KDEC, 0:B], bdecb[:, 0:1], None, ALU.add).then_inc(su_dve("ub"), 1)
        dve.wait_ge(*su_pool.done("dem"))

        def ranks(layer, c, vals):
            a = vals.unsqueeze(2).broadcast_to([P, NC, EXPERTS, EXPERTS])
            b = vals.unsqueeze(3).broadcast_to([P, NC, EXPERTS, EXPERTS])
            sq = lambda t: t[:].rearrange("p n (e f) -> p n e f", e=EXPERTS)
            tt(sq(ge), a, b, ALU.is_ge).then_inc(*in_dve.step(f"ge{layer}"))
            dve.wait_ge(*in_dve.done(f"ge{layer}", c))
            tt(ge[:], ge[:], bc_n(tri[:, 0, :]), ALU.mult).then_inc(*in_dve.step(f"gel{layer}"))
            tt(sq(gt), a, b, ALU.is_gt).then_inc(*in_dve.step(f"gt{layer}"))
            dve.wait_ge(*in_dve.done(f"gt{layer}", c))
            tt(gt[:], gt[:], bc_n(tri[:, 1, :]), ALU.mult).then_inc(*in_dve.step(f"gtu{layer}"))
            dve.wait_ge(*in_dve.done(f"gtu{layer}", c))
            tt(ge[:], ge[:], gt[:], ALU.add).then_inc(*in_dve.step(f"cmp{layer}"))
            dve.wait_ge(*in_dve.done(f"cmp{layer}", c))
            red(rank[:], sq(ge), AX, ALU.add).then_inc(*in_dve.step(f"rank{layer}"))
            dve.wait_ge(*in_dve.done(f"rank{layer}", c))

        def turn(t, I, F, M, G):
            U, N2 = t + 1, t + 2

            def unit(g):
                if g < UNITS and active(g, F, G):
                    q = g % 2
                    dve.wait_ge(*silu.done(f"s{g}", U))
                    dve.wait_ge(*up.done(f"b{g}", U))
                    wait_unit(dve, down, "d", g, 2, t, F)
                    tt(hid[:, q, :], sil[:, q, :], psU[:, 2 * q + 1, :], ALU.mult).then_inc(*mul.step(f"h{g}", fill("h", g, G)))
                e = (g - 3) // 2
                if g % 2 == 1 and e >= 0 and active(2 * e, F, G):
                    dve.wait_ge(*down.done(f"d{2 * e + 1}", U))
                    first, sum_ = e in (0, EX0), acc0 if e < EX0 else res
                    if e == 0:
                        dve.wait_ge(x_read, (t + 2) * 16)
                        if M:
                            dve.wait_ge(*k_pe.done("x2T", t))
                            dve.wait_ge(*k_act.done("x2", t))
                        dve.wait_ge(*in_dve.done("cw0", N2 - 1))
                    elif first:
                        dve.wait_ge(*in_dve.done("cw1", N2))
                        dve.wait_ge(*in_pool.done("base", t - 1))
                    else:
                        dve.wait_ge(*acc.done(f"x{e - 1}", U))
                    for n in range(NC):
                        part = slice(n * D, (n + 1) * D)
                        w = cw0[:, n, e:e + 1] if e < EX0 else cw1[:, n, e - EX0:e - EX0 + 1]
                        last = nc.vector.scalar_tensor_tensor(out=sum_[:, part], in0=psDn[:, e % 2, part], scalar=w,
                                                              in1=(xs if e == 0 else sum_)[:, part], op0=ALU.mult, op1=ALU.add)
                    last.then_inc(*acc.step(f"x{e}", f"x{UNITS // 2 - 1}" if e == EX0 - 1 and not G else None))

            to = Slots(unit)

            def mul_n(out_, in_, per_batch):
                return tt(by_n(out_[:]), by_n(in_), bc_n(per_batch), ALU.mult)

            window = kx[:].rearrange("p n t d -> p n (t d)")

            def shifted(n, count):
                w = window[:, n, 0:D]
                return bass.AP(w.tensor, w.offset, [list(w.ap[0]), [D1, count], [1, D]])

            def score_products(m):
                pr4 = prod[:, 0:2 * OFF * D].rearrange("p (n o x) -> p n o x", n=2, o=OFF)
                for n in range(2):
                    last = tt(pr4[:, n, :, :], window[:, 2 * m + n, 0:D].unsqueeze(1).broadcast_to([P, OFF, D]),
                              shifted(2 * m + n, OFF), ALU.mult)
                last.then_inc(*k_dve.step(f"prod{m}"))

            def score_sums(m):
                dve.wait_ge(*k_dve.done(f"prod{m}", t))
                red(sd[:, 2 * m:2 * m + 2, :, 0, :].rearrange("p n o h -> p (n o) h"),
                    prod[:, 0:2 * OFF * D].rearrange("p (a h d) -> p a h d", h=H1, d=D1), AX, ALU.add).then_inc(*k_dve.step(f"sd{m}"))

            def head_products(n):
                w = window[:, n, 0:D]
                win = bass.AP(w.tensor, w.offset, [list(w.ap[0]), [D1, H1], [D1, H1], [1, D1]])
                tt(prod[:, 0:H1 * H1 * D1].rearrange("p (o h d) -> p o h d", o=H1, h=H1),
                   sf[:, n, :, :].unsqueeze(3).broadcast_to([P, H1, H1, D1]), win, ALU.mult).then_inc(*k_dve.step(f"ap{n}"))

            def head_sums(n):
                dve.wait_ge(*k_dve.done(f"ap{n}", t))
                red(mixed[:, n * D:(n + 1) * D], prod[:, 0:H1 * H1 * D1].rearrange("p (o x) -> p x o", o=H1),
                    AX, ALU.add).then_inc(*k_dve.step(f"av{n}"))

            if M:
                to("xk")
                dve.wait_ge(*k_pe.done("x2T", t))
                mul_n(xk, ps6, style[:, 1, :]).then_inc(*k_dve.step("xk"))
                to("kx0")
                dve.wait_ge(*k_pe.done("kx", t))
                mul_n(kx0, ps6, demod[:, 1, :]).then_inc(*k_dve.step("kx0"))
                to("prod0")
                dve.wait_ge(*k_act.done("kxdup", t))
                score_products(0)
                to("sd0")
                score_sums(0)
                to("prod1")
                dve.wait_ge(*k_dve.done("sd0", t))
                score_products(1)
            if G:
                to("t")
                dve.wait_ge(*in_pe.done(f"t{TG - 1}", N2))
                tt(tK[:].rearrange("k n b -> k b n"), ps7[0:KDEC, :].rearrange("k (b n) -> k b n", n=NC),
                   Ub[:].unsqueeze(2).broadcast_to([KDEC, B, NC]), ALU.add).then_inc(*in_dve.step("t"))
            if M:
                to("sd1")
                score_sums(1)
                to("sf1")
                dve.wait_ge(*k_act.done("sddup", t))
                for n in range(NC):
                    s0 = sd[:, n, 0, 0, 0:1]
                    back = bass.AP(s0.tensor, s0.offset + (H1 - OFF) * 2 * H1 + OFF, [list(s0.ap[0]), [1 - 2 * H1, H1 - OFF], [1, H1]])
                    last = nc.vector.tensor_copy(sf[:, n, OFF:H1, :], back)
                last.then_inc(*k_dve.step("sf1"))
                dve.wait_ge(*k_dve.done("sf1", t))
                dve.wait_ge(*k_act.done("sf0", t))
                red(mxh[:], sf[:].rearrange("p n o h -> p n h o"), AX, ALU.max).then_inc(*k_dve.step("max"))
                to("sub")
                dve.wait_ge(*k_dve.done("max", t))
                tt(sf[:], sf[:], mxh[:].unsqueeze(2).broadcast_to([P, NC, H1, H1]), ALU.subtract).then_inc(*k_dve.step("sub"))
            if G:
                to("ms")
                dve.wait_ge(*in_pool.done("sq", t - 1))
                red(ms4[:, 0, :], by_n(zn[:]), AX, ALU.add).then_inc(*in_dve.step("ms"))
                to("zn")
                dve.wait_ge(*in_pool.done("rs", t - 1))
                for n in range(NC):
                    nc.vector.scalar_tensor_tensor(out=zn[:, n * D:(n + 1) * D], in0=z[:, n * D:(n + 1) * D], scalar=ms4[:, 1, n:n + 1],
                                                   in1=rows[:, 3, :], op0=ALU.mult, op1=ALU.mult).then_inc(*in_dve.step(f"zn{n}"))
            if M:
                to("sum")
                dve.wait_ge(*k_act.done("exp", t))
                red(smh[:], sf[:].rearrange("p n o h -> p n h o"), AX, ALU.add).then_inc(*k_dve.step("sum"))
                dve.wait_ge(*k_dve.done("sum", t))
                nc.vector.reciprocal(rsh[:], smh[:]).then_inc(*k_dve.step("rsum"))
                to("ap0")
                dve.wait_ge(*k_pool.done("probs", t))
                head_products(0)
            if G:
                to("sub1")
                dve.wait_ge(*in_pe.done("r1", N2))
                r = ps7[:, 0:NC * EXPERTS].rearrange("p (n e) -> p n e", n=NC)
                red(m4[:], r, AX, ALU.max).then_inc(*in_dve.step("max1"))
                dve.wait_ge(*in_dve.done("max1", N2))
                tt(s8[:], r, m4[:].unsqueeze(2).broadcast_to([P, NC, EXPERTS]), ALU.subtract).then_inc(*in_dve.step("sub1"))
                dve.wait_ge(*in_dve.done("sub1", N2))
                nc.vector.tensor_copy(p8[:], r).then_inc(*in_dve.step("raw"))
            if M:
                to("av0")
                head_sums(0)
                to("ap1")
                dve.wait_ge(*k_dve.done("av0", t))
                head_products(1)
            if G:
                to("ranks1")
                dve.wait_ge(*in_dve.done("raw", N2))
                ranks(1, N2, p8[:])
                to("cw1")
                dve.wait_ge(*in_act.done("e1", N2))
                nc.vector.scalar_tensor_tensor(out=cw1[:], in0=rank[:], scalar=float(TOP_K), in1=ex8[:], op0=ALU.is_lt,
                                               op1=ALU.mult).then_inc(*in_dve.step("em"))
                dve.wait_ge(*in_dve.done("em", N2))
                red(m4[:], cw1[:], AX, ALU.add).then_inc(*in_dve.step("sum1"))
                dve.wait_ge(*in_dve.done("sum1", N2))
                nc.vector.reciprocal(m4[:], m4[:]).then_inc(*in_dve.step("rsum1"))
                dve.wait_ge(*in_dve.done("rsum1", N2))
                tt(cw1[:], cw1[:], m4[:].unsqueeze(2).broadcast_to([P, NC, EXPERTS]), ALU.mult).then_inc(*in_dve.step("cw1", None if I else "cw0"))
            if M:
                for n in range(1, NC):
                    to(f"av{n}")
                    head_sums(n)
                    if n + 1 < NC:
                        to(f"ap{n + 1}")
                        dve.wait_ge(*k_dve.done(f"av{n}", t))
                        head_products(n + 1)
                to("xo")
                dve.wait_ge(*k_pe.done("oT", t))
                mul_n(xk, ps6, style[:, 2, :]).then_inc(*k_dve.step("xo"))
                to("y1")
                dve.wait_ge(*k_pe.done("y", t))
                mul_n(kx0, ps6, demod[:, 2, :]).then_inc(*k_dve.step("y1"))
                to("ssq")
                for i, name in enumerate("qk"):
                    dve.wait_ge(*m_act.done("sq" + name, t))
                    red(ssr[:, i, :], sqr[i][:].rearrange("p (s j) -> p s j", j=D1), AX, ALU.add).then_inc(*m_dve.step("ss" + name))
                to("fb0")
                dve.wait_ge(*m_pe.done("fb", t))
                tt(fb0[:], ps6[:, 0:NC * 2 * H1].rearrange("p (n t h) -> p n t h", n=NC, t=2), bc_n(fbias[:]).rearrange("p n (t h) -> p n t h", t=2),
                   ALU.add).then_inc(*m_dve.step("fb0"))
                to("qk")
                dve.wait_ge(*m_pool.done("rqk", t))
                for i, name in enumerate("qk"):
                    dve.wait_ge(*m_act.done(name, t))
                    dst = A[:, :, D1, :] if i == 0 else kv[:, 0:D1, :]
                    tt(dst, dst, rn[:, i, :].unsqueeze(1).broadcast_to([P, D1, SYS]), ALU.mult).then_inc(*m_dve.step(name))
                to("fb1")
                dve.wait_ge(*m_act.done("fbt", t))
                nc.vector.tensor_scalar(fb[:], fbt[:], 0.5, 0.5, ALU.mult, ALU.add).then_inc(*m_dve.step("fb"))
                dve.wait_ge(*m_dve.done("fb", t))
                tt(bk[:].rearrange("p j (n h) -> p j n h", n=NC), kv[:, 0:D1, :].rearrange("p j (n h) -> p j n h", n=NC),
                   fb[:, :, 1, :].unsqueeze(1).broadcast_to([P, D1, NC, H1]), ALU.mult).then_inc(*m_dve.step("bk"))
                to("Uk")
                dve.wait_ge(*m_dve.done("bk", t))
                wait_if(dve, m_act, "carry_k", t - 1)
                tt(A[:, :, 0:D1, :], bk[:].unsqueeze(2).broadcast_to([P, D1, D1, SYS]),
                   kv[:, 0:D1, :].unsqueeze(1).broadcast_to([P, D1, D1, SYS]), ALU.mult).then_inc(*m_dve.step("Uk"))
            if I:
                to("xm")
                dve.wait_ge(*in_pe.done("x1", N2))
                mul_n(xm, ps7, style[:, 0, :]).then_inc(*in_dve.step("xm"))
            if M:
                T4 = prod[:, 0:D1 * D1 * H1].rearrange("p (i j h) -> p i j h", i=D1, h=H1)
            for n in range(NC):
                if M:
                    to(f"hk{n}")
                    dve.wait_ge(*m_dve.done(f"hk{n - 1}" if n else "Uk", t))
                    tt(T4, carry[:, 0, :, :].rearrange("p (i j) h -> p i j h", i=D1) if n == 0 else A4[:, :, 0:D1, n - 1, :],
                       fb[:, n, 0, :].unsqueeze(1).unsqueeze(1).broadcast_to([P, D1, D1, H1]), ALU.mult).then_inc(*m_dve.step(f"mk{n}"))
                    dve.wait_ge(*m_dve.done(f"mk{n}", t))
                    tt(A4[:, :, 0:D1, n, :], A4[:, :, 0:D1, n, :], T4, ALU.add).then_inc(*m_dve.step(f"hk{n}"))
                if I and n == 0:
                    to("dm")
                    dve.wait_ge(*in_pe.done("y", N2))
                    if F:
                        dve.wait_ge(*up.done(f"b{UNITS0 - 1}", U))
                    mul_n(yT, ps7, demod[:, 0, :]).then_inc(*in_dve.step("dm"))
                    dve.wait_ge(*in_dve.done("dm", N2))
                    nc.vector.tensor_scalar(yT[:], yT[:], vecs[:, 0:1], 256.0, ALU.add, ALU.min).then_inc(*in_dve.step("bias"))
                    dve.wait_ge(*in_dve.done("bias", N2))
                    nc.vector.tensor_scalar(yT[:], yT[:], -256.0, None, ALU.max).then_inc(*in_dve.step("yT"))
                if I and n == 2:
                    to("sub0")
                    dve.wait_ge(*in_pe.done("r0", N2))
                    r = ps7[:, 0:NC * EXPERTS].rearrange("p (n e) -> p n e", n=NC)
                    red(m4[:], r, AX, ALU.max).then_inc(*in_dve.step("max0"))
                    dve.wait_ge(*in_dve.done("max0", N2))
                    tt(s8[:], r, m4[:].unsqueeze(2).broadcast_to([P, NC, EXPERTS]), ALU.subtract).then_inc(*in_dve.step("sub0"))
            if I:
                to("probs0")
                dve.wait_ge(*in_act.done("e0", N2))
                red(m4[:], ex8[:], AX, ALU.add).then_inc(*in_dve.step("sum0"))
                dve.wait_ge(*in_dve.done("sum0", N2))
                nc.vector.reciprocal(m4[:], m4[:]).then_inc(*in_dve.step("rsum0"))
                dve.wait_ge(*in_dve.done("rsum0", N2))
                tt(p8[:], ex8[:], m4[:].unsqueeze(2).broadcast_to([P, NC, EXPERTS]), ALU.mult).then_inc(*in_dve.step("probs"))
            if M:
                to("diag")
                dve.wait_ge(*m_act.done("carry_k", t))
                diagonal = bass.AP(A[:, 0, 0, 0:1].tensor, A[:, 0, 0, 0:1].offset, [list(A[:, 0, 0, 0:1].ap[0]), [(D1 + 2) * SYS, D1], [1, SYS]])
                diag4 = diagonal.rearrange("p i (n h) -> p i n h", n=NC)
                tt(diag4, diag4, lam[:].rearrange("p (h i) -> p i h", h=H1).unsqueeze(2).broadcast_to([P, D1, NC, H1]), ALU.add).then_inc(*m_dve.step("diag"))
            if I:
                to("ranks0")
                dve.wait_ge(*in_dve.done("probs", N2))
                ranks(0, N2, p8[:])
                nc.vector.tensor_scalar(rank[:], rank[:], float(TOP_K), TOP_K / (TOP_K + 1.0), ALU.is_lt, ALU.mult).then_inc(*in_dve.step("rk2"))
                dve.wait_ge(*in_dve.done("rk2", N2))
                if F:
                    dve.wait_ge(*acc.done(f"x{EX0 - 1}", U))
                tt(cw0[:, :, 0:EXPERTS], rank[:], p8[:], ALU.mult).then_inc(*in_dve.step("cw0"))
            if M:
                prev = "diag"
                for k in range(D1 - 1):
                    to(f"el{k}")
                    dve.wait_ge(*m_dve.done(prev, t))
                    if k == LOW:
                        dve.wait_ge(*m_pool.done(f"la{LOW - 1}", t))
                    nc.vector.reciprocal(A[:, k, k, :], A[:, k, k, :]).then_inc(*m_dve.step(f"ri{k}"))
                    dve.wait_ge(*m_dve.done(f"ri{k}", t))
                    tt(A[:, k + 1:, k, :], A[:, k, k + 1:D1, :], A[:, k, k:k + 1, :].broadcast_to([P, D1 - 1 - k, SYS]),
                       ALU.mult).then_inc(*m_dve.step(f"col{k}"))
                    prev = f"col{k}"
                    if k == LOW or k < LOW - 1:
                        rows_ = range(k + 1, D1 if k == LOW else LOW)
                        dve.wait_ge(*m_dve.done(f"col{k}", t))
                        at, parts = 0, []
                        for i in rows_:
                            w = D1 + 1 - i
                            parts.append((i, T[:, at:at + w, :]))
                            at += w
                            last = tt(parts[-1][1], A[:, k, i:, :], A[:, i, k:k + 1, :].broadcast_to([P, w, SYS]), ALU.mult)
                        last.then_inc(*m_dve.step(f"t{k}"))
                        dve.wait_ge(*m_dve.done(f"t{k}", t))
                        for i, part in parts:
                            last = tt(A[:, i, i:, :], A[:, i, i:, :], part, ALU.subtract)
                        last.then_inc(*m_dve.step(f"a{k}"))
                        prev = f"a{k}"
                dve.wait_ge(*m_dve.done(prev, t))
                k = D1 - 1
                nc.vector.reciprocal(A[:, k, k, :], A[:, k, k, :]).then_inc(*m_dve.step(f"ri{k}"))
                to("rhs")
                dve.wait_ge(*m_dve.done(f"ri{k}", t))
                tt(A[:, :, D1, :], A[:, :, D1, :], diagonal, ALU.mult).then_inc(*m_dve.step("rhs"))
                prev = "rhs"
                for k in range(D1 - 1, 0, -1):
                    dve.wait_ge(*m_dve.done(prev, t))
                    tt(T[:, 0:k, :], A[:, k, 0:k, :], A[:, k, D1:D1 + 1, :].broadcast_to([P, k, SYS]), ALU.mult).then_inc(*m_dve.step(f"bt{k}"))
                    dve.wait_ge(*m_dve.done(f"bt{k}", t))
                    tt(A[:, 0:k, D1, :], A[:, 0:k, D1, :], T[:, 0:k, :], ALU.subtract).then_inc(*m_dve.step(f"bx{k}"))
                    prev = f"bx{k}"
                to("oprod")
                dve.wait_ge(*m_dve.done(prev, t))
                dve.wait_ge(*m_pool.done(f"hv{NC - 1}", t))
                tt(A[:, :, 0:D1, :], A[:, :, D1, :].unsqueeze(2).broadcast_to([P, D1, D1, SYS]),
                   Hv[:].rearrange("p (i j) n h -> p i j (n h)", i=D1), ALU.mult).then_inc(*m_dve.step("oprod"))
                to("o1")
                dve.wait_ge(*m_dve.done("oprod", t))
                red(o1[:].rearrange("p (s j) -> p j s", j=D1), A[:, :, 0:D1, :].rearrange("p i j s -> p j s i"), AX, ALU.add).then_inc(*m_dve.step("o1"))
                to("og")
                dve.wait_ge(*m_dve.done("o1", t))
                dve.wait_ge(*m_act.done("gate", t))
                nc.vector.scalar_tensor_tensor(out=og[:], in0=gate[:], scalar=1.0, in1=o1[:], op0=ALU.add, op1=ALU.mult).then_inc(*m_dve.step("og"))
                to("ss")
                dve.wait_ge(*m_pool.done("sq", t))
                red(ssr[:, 0, :], mixed[:].rearrange("p (s j) -> p s j", j=D1), AX, ALU.add).then_inc(*m_dve.step("ss"))
                to("ogn")
                dve.wait_ge(*m_pool.done("rs", t))
                tt(o1[:].rearrange("p (s j) -> p s j", j=D1), og[:].rearrange("p (s j) -> p s j", j=D1),
                   rn[:, 0, :].unsqueeze(2).broadcast_to([P, SYS, D1]), ALU.mult).then_inc(*m_dve.step("ogn"))
                to("x3")
                dve.wait_ge(*m_pe.done("x3", t))
                if G:
                    dve.wait_ge(*in_pool.done("base", t - 1))
                tt(x3[:], ps6, x2[:], ALU.add).then_inc(*m_dve.step("x3"))
            to.up_to(UNITS + 2)

        run(dve, turn)


def layouts(inp):
    f = lambda k: np.asarray(inp[k])
    a = {}
    x = f("x")
    inv = 1.0 / 10000.0 ** (np.arange(0, HD, 2, dtype=np.float32) / HD)
    ang = np.tile(np.arange(N, dtype=np.float32)[:, None] * inv[None, :], (GB, 1))
    a["cos"] = np.concatenate([np.cos(ang)] * 2, 1)
    a["sin"] = np.concatenate([-np.sin(ang), np.sin(ang)], 1)
    a["fold"] = np.tile(np.eye(AH, dtype=np.float32), (2, 1))
    a["ident"] = np.eye(P, dtype=np.float32)
    e = np.arange(EXPERTS)
    lower = (e[None, :] < e[:, None]).astype(np.float32).reshape(-1)
    upper = (e[None, :] > e[:, None]).astype(np.float32).reshape(-1)
    a["tri"] = np.tile(np.stack([lower, upper])[None], (P, 1, 1))
    a["xT"] = x.reshape(TOK, D).T
    a["condT"] = f("cond_512").T
    a["dgb"] = np.concatenate([f("L0_cond_down_gamma"), f("L0_cond_down_beta")], 1)
    a["ugb"] = np.stack([f("L0_cond_up_gamma"), f("L0_cond_up_beta")], 1)
    a["down"], a["up"] = f("L0_cond_down_project"), f("L0_cond_up_project")
    a["ln_gb"] = np.stack([f("L0_attn_ln_gamma"), f("L0_attn_ln_beta")], 1)
    a["b_out"] = np.tile(f("L0_attn_b_out")[None], (P, 1))
    a["x"] = x.reshape(TOK, D)
    a["w_qkv"] = f("L0_attn_w_qkv")
    a["w_out"] = f("L0_attn_w_out").reshape(PAIRS, P, D).transpose(1, 0, 2)
    a["w2c"] = f("L0_cond2_weight").T
    zero = np.zeros(D, np.float32)
    a["vecs"] = np.stack([f("L0_cond2_bias"), f("L1_cond_o_b"), f("L0_cond2_affine_b"), f("L1_cond_k_aff_b"),
                          f("L1_cond_o_aff_b"), zero, zero, zero], 1)
    a["w_r0"], a["w_r1"] = f("L0_ffn_w_router"), f("L1_ffn_w_router").T
    w1 = np.concatenate([f("L0_ffn_w1"), f("L0_ffn_ws1")[None]])
    w3 = np.concatenate([f("L0_ffn_w3"), f("L0_ffn_ws3")[None]])
    w2 = np.concatenate([f("L0_ffn_w2"), f("L0_ffn_ws2")[None]])
    a["w13"] = np.stack([w1, w3], 2).transpose(1, 0, 2, 3)
    a["w2"] = w2.reshape(EX0, 2, P, D).transpose(2, 0, 1, 3)
    a["aff"] = np.stack([f("L0_cond2_affine_w").T, f("L1_cond_k_aff_w").T, f("L1_cond_o_aff_w").T], 1)
    a["kwT"], a["owT"] = f("L1_cond_k_w").T, f("L1_cond_o_w").T
    a["wqkv1"] = np.stack([f("L1_attn_Wq"), f("L1_attn_Wk"), f("L1_attn_Wv")], 1)
    a["wfb"] = np.concatenate([f("L1_attn_Wf"), f("L1_attn_Wbet")], 1)
    a["wo1"], a["g1"], a["g2"] = f("L1_attn_Wo"), f("L1_attn_gate_w1"), f("L1_attn_gate_w2")
    a["rows"] = np.tile(np.stack([f("L1_cond_k_b"), f("L1_attn_lamb_params"), f("L1_attn_norm_weight"),
                                  f("L1_ffn_norm_scale")])[None], (P, 1, 1))
    a["fbias"] = np.tile(np.concatenate([f("L1_attn_delta"), np.zeros(H1, np.float32)])[None], (P, 1))
    a["wdec"] = f("L1_cond2_W_dec")
    b = f("L1_cond2_b_dec").reshape(D + 1, KDEC)
    a["bdec"], a["bdecb"] = b[:D], b[D][:, None]
    a["vmat"] = f("L1_cond2_V")
    a["w_up1"] = f("L1_ffn_w_up").transpose(2, 0, 1)
    a["w_dn1"] = f("L1_ffn_w_down").transpose(0, 2, 1).reshape(EXPERTS, 2, P, D).transpose(2, 0, 1, 3)
    return {k: np.ascontiguousarray(v) for k, v in a.items()}


def block_pair(nc, dram, x1, out):
    with ExitStack() as ctx:
        attention_phase(nc, ctx, dram, x1)
    with ExitStack() as ctx:
        mixing_phase(nc, ctx, dram, x1.rearrange("(b n) d -> b (n d)", b=B), out)


def kernel(**inputs):
    import concourse.bacc as bacc
    from concourse.bass_utils import run_bass_kernel_spmd

    nc = bacc.Bacc("TRN2", target_bir_lowering=False, num_devices=1)
    arrays = layouts(inputs)
    dram = {name: nc.dram_tensor(name, a.shape, F32, kind="ExternalInput").ap() for name, a in arrays.items()}
    x1 = nc.dram_tensor("x1", (TOK, D), F32, kind="Internal").ap()
    out = nc.dram_tensor("out", (B, N * D), F32, kind="ExternalOutput").ap()
    block_pair(nc, dram, x1, out)
    r = run_bass_kernel_spmd(nc, [arrays], core_ids=[0])
    return np.asarray(r.results[0]["out"]).reshape(B, N, D)
```

```python
from contextlib import ExitStack

import concourse.bass as bass
import numpy as np
from concourse import mybir

F32 = mybir.dt.float32
I32 = mybir.dt.int32
ALU = mybir.AluOpType
ACT = mybir.ActivationFunctionType
AX = mybir.AxisListType.X

P = 128
B, N, D, C = 128, 32, 128, 64
TOK = B * N
AH = 32
HEADS, HD = 16, 64
HALF = HD // 2
PAIRS = HEADS // 2
INNER = HEADS * HD
GB = P // N
TILES = TOK // P


class Steps:

    def __init__(self, sem, names):
        self.sem, self.names, self.at = sem, names.split(), 0

    def __call__(self, name):
        assert self.names[self.at % len(self.names)] == name, (name, self.names, self.at)
        self.at += 1
        return self.sem

    def step(self, name, upto=None):
        first, last = self.names.index(name), self.names.index(upto or name)
        assert self.at <= first, (name, self.names[self.at])
        raised, self.at = last + 1 - self.at, (last + 1) % len(self.names)
        return self.sem, raised

    def done(self, name, t=0):
        return self.sem, t * len(self.names) + (self.names.index(name) + 1)


def wait_if(eng, steps, name, t):
    if not isinstance(t, int) or t >= 0:
        eng.wait_ge(*steps.done(name, t))


def attention_phase(nc, ctx, dram, x1, later_loads):

    def sb(name, shape):
        return ctx.enter_context(nc.sbuf_tensor("p1_" + name, shape, F32))

    xT = sb("xT", [P, TOK])
    condT = sb("condT", [C, B])
    w_dgb = sb("w_dgb", [C, 2 * AH])
    w_ugb = sb("w_ugb", [C, 2, D])
    w_down = sb("w_down", [P, 2 * AH])
    w_up = sb("w_up", [AH, 2, D])
    fold = sb("fold", [2 * AH, AH])
    ident = sb("ident", [P, P])
    ln_gb = sb("ln_gb", [P, 2])
    b_out = sb("b_out", [P, D])
    x_in = sb("x_in", [P, 2, D])
    xb = sb("xb", [P, 2, D])
    x_out = sb("x_out", [P, 2, D])
    w_qkv = sb("w_qkv", [P, 3 * INNER])
    w_out = sb("w_out", [P, PAIRS, D])
    cos = sb("cos", [P, HD])
    sin = sb("sin", [P, HD])
    dgb = sb("dgb", [2 * AH, B])
    ugb = sb("ugb", [P, 2, B])
    half = sb("half", [P, 1])
    eps = sb("eps", [P, 1])

    gated = sb("gated", [2 * AH, P])
    act = sb("act", [AH, P])
    ups = sb("ups", [P, 2, P])
    hres = sb("hres", [P, P])
    stats = sb("stats", [P, 6])
    mv = sb("mv", [P, 2])
    veps = sb("veps", [P, 1])
    rstd = sb("rstd", [P, 1])
    xn = sb("xn", [P, P])
    xnT = sb("xnT", [P, 2, P])
    rc = sb("rc", [P, 2, INNER])
    rs = sb("rs", [P, 2, INNER])
    rot = sb("rot", [P, 2, INNER])
    qT = sb("qT", [P, PAIRS, P])
    kbd = sb("kbd", [P, PAIRS, GB, 2, N])
    v = sb("v", [P, 2, INNER])
    mx = sb("mx", [P, HEADS])
    sc = sb("sc", [P, HEADS, N])
    ex = sb("ex", [P, HEADS, N])
    sm = sb("sm", [P, HEADS])
    rsm = sb("rsm", [P, HEADS])
    pr = sb("pr", [P, HEADS, N])
    pbd = sb("pbd", [P, HEADS, P])
    oT = sb("oT", [P, PAIRS, P])

    def sem(name):
        return ctx.enter_context(nc.semaphore("p1_" + name))

    loaded = sem("loaded")
    loaded_w = sem("loaded_w")
    loaded_x = sem("loaded_x")
    LOADS, LOADS_W = 9 * 16, 5 * 16
    HEAD_START = 4 * P
    zeroed = sem("zeroed")
    ZEROED = 6
    s_pe = Steps(sem("setup_pe"), "gates")
    s_act = Steps(sem("setup_act"), "dgb ugb")
    a_pe = Steps(sem("adapter_pe"), "down fold up sum xnT")
    a_dve = Steps(sem("adapter_dve"), "gated ups hres stats mv xn")
    a_act = Steps(sem("adapter_act"), "act xnT")
    x_read = [sem("x_read_even"), sem("x_read_odd")]
    x_written = [sem("x_written_even"), sem("x_written_odd")]
    e_pool = Steps(sem("bias_pool"), "xb")
    a_pool = Steps(sem("adapter_pool"), "veps rstd")
    b_pe = Steps(sem("qk_pe"), "q k qT kT")
    b_dve = Steps(sem("rope_dve"), "qc qs1 qs2 kc ks1 ks2")
    b_pool = Steps(sem("rope_pool"), "q k")
    b_act = Steps(sem("qk_act"), "qT k0 k1")
    c_pe = Steps(sem("scores_pe"), "scores v")
    c_act = Steps(sem("scores_act"), "v exp")
    c_dve = Steps(sem("softmax_dve"), "max sub sum rsum")
    c_pool = Steps(sem("softmax_pool"), "probs")
    d_dve = Steps(sem("out_dve"), "probsT x1")
    d_pe = Steps(sem("out_pe"), "pv y")
    d_act = Steps(sem("out_act"), "oT")

    ps = ctx.enter_context(nc.psum_tensor("p1_ps", [P, 8, 512], F32))

    def two_banks(k):
        return ps[:, k:k + 2, :].rearrange("p a b -> p (a b)")

    psX, psY, psZ = two_banks(0), two_banks(2), two_banks(4)
    psS, psA = ps[:, 6, :], ps[:, 7, :]

    block = ctx.enter_context(nc.Block())

    def pipeline(stages):

        def turn(t, u, k):
            stages(t, u, k, *(not isinstance(t, int) or 0 <= t + d < TILES for d in (2, 1, 0, -1)))

        return turn

    FIRST, LAST = 2, TILES - 2

    def run(eng, turn):
        for t in range(-2, FIRST):
            turn(t, t % 2, t // 2)
        with eng.Fori(FIRST // 2, LAST // 2) as two:
            turn(two * 2, 0, two)
            turn(two * 2 + 1, 1, two)
        for t in range(LAST, TILES + 1):
            turn(t, t % 2, t // 2)

    @block.sync
    def _(sp):
        def load(dst, src, signal):
            sp.dma_start(dst, src).then_inc(signal, 16)

        for dst, name in ((condT[:], "condT"), (w_dgb[:], "dgb"), (w_ugb[:], "ugb"), (w_down[:, 0:AH], "down"),
                          (fold[:], "fold"), (w_up[:, 0, :], "up"), (ident[:], "ident"), (ln_gb[:], "ln_gb")):
            load(dst, dram[name], loaded)
        load(xT[:, 0:HEAD_START], dram["xT"][:, 0:HEAD_START], loaded)
        for dst, name in ((w_qkv[:], "w_qkv"), (cos[:], "cos"), (sin[:], "sin"), (b_out[:], "b_out"), (w_out[:], "w_out")):
            load(dst, dram[name], loaded_w)
        load(xT[:, HEAD_START:], dram["xT"][:, HEAD_START:], loaded_x)
        later_loads(sp)

        def turn(t, u, k, A, Bq, Cs, Do):
            if A:
                wait_if(sp, e_pool, "xb", t)
                sp.dma_start(x_in[:, u, :], dram["x"][bass.ds((t + 2) * P, P), :]).then_inc(x_read[u], 16)
            if Do:
                sp.wait_ge(*d_dve.done("x1", t - 1))
                sp.dma_start(x1[bass.ds((t - 1) * P, P), :], x_out[:, (u + 1) % 2, :]).then_inc(x_written[(u + 1) % 2], 16)

        run(sp, pipeline(turn))
        for w in x_written:
            sp.wait_ge(w, 16 * (TILES // 2))

    @block.tensor
    def _(pe):
        pe.wait_ge(loaded, LOADS)
        pe.wait_ge(zeroed, ZEROED)
        nc.tensor.matmul(psX[0:2 * AH, 0:B], w_dgb[:], condT[:], start=True, stop=True)
        for i in range(2):
            last = nc.tensor.matmul(psY[:, i * B:(i + 1) * B], w_ugb[:, i, :], condT[:], start=True, stop=True)
        last.then_inc(s_pe("gates"), 1)
        pe.wait_ge(*s_act.done("ugb"))

        def turn(t, u, k, A, Bq, Cs, Do):
            ta, tb, td = t + 2, t + 1, t - 1
            if isinstance(t, int) and t == 1:
                pe.wait_ge(loaded_x, 16)
            if A:
                wait_if(pe, a_act, "xnT", ta - 1)
                nc.tensor.matmul(psA[0:2 * AH, 0:P], w_down[:], xT[:, bass.ds(ta * P, P)], start=True,
                                 stop=True).then_inc(a_pe("down"), 1)
            if Bq:
                if isinstance(t, int) and t == -1:
                    pe.wait_ge(loaded_w, LOADS_W)
                pe.wait_ge(*a_act.done("xnT", tb))
                wait_if(pe, b_act, "qT", tb - 1)
                for j in range(2):
                    last = nc.tensor.matmul(psX[:, j * 512:(j + 1) * 512], xnT[:, (u + 1) % 2, :],
                                            w_qkv[:, j * 512:(j + 1) * 512], start=True, stop=True)
                last.then_inc(b_pe("q"), 1)
            if A:
                pe.wait_ge(*a_dve.done("gated", ta))
            if Cs:
                pe.wait_ge(*b_act.done("k1", t))
                wait_if(pe, d_dve, "x1", t - 2)
                for p in range(PAIRS):
                    for b in range(GB):
                        last = nc.tensor.matmul(psS[b * N:(b + 1) * N, p * 2 * N:(p + 1) * 2 * N],
                                                qT[:, p, b * N:(b + 1) * N], kbd[:, p, b, :, :],
                                                start=True, stop=True)
                last.then_inc(c_pe("scores"), 1)
            if A:
                nc.tensor.matmul(psA[0:AH, 128:256], fold[:], gated[:], start=True, stop=True).then_inc(a_pe("fold"), 1)
            if Cs:
                wait_if(pe, d_act, "oT", t - 2)
                for j in range(2):
                    last = nc.tensor.matmul(psZ[:, j * 512:(j + 1) * 512], xnT[:, u, :],
                                            w_qkv[:, 2 * INNER + j * 512:2 * INNER + (j + 1) * 512],
                                            start=True, stop=True)
                last.then_inc(c_pe("v"), 1)
            if A:
                pe.wait_ge(*a_act.done("act", ta))
                for i in range(2):
                    last = nc.tensor.matmul(psA[:, 256 + i * P:256 + (i + 1) * P], w_up[:, i, :], act[:],
                                            start=True, stop=True)
                last.then_inc(a_pe("up"), 1)
            if Bq:
                wait_if(pe, b_act, "k1", tb - 1)
                for j in range(2):
                    last = nc.tensor.matmul(psY[:, j * 512:(j + 1) * 512], xnT[:, (u + 1) % 2, :],
                                            w_qkv[:, INNER + j * 512:INNER + (j + 1) * 512], start=True, stop=True)
                last.then_inc(b_pe("k"), 1)
            if A:
                pe.wait_ge(*a_dve.done("hres", ta))
                nc.tensor.matmul(psA[:, 0:P], hres[:], ident[:], start=True, stop=False)
                nc.tensor.matmul(psA[:, 0:P], ups[:, 1, :], ident[:], start=False, stop=True).then_inc(a_pe("sum"), 1)
            if Do:
                pe.wait_ge(*d_dve.done("probsT", td))
                if Cs:
                    pe.wait_ge(*c_act.done("v", t))
                for h in range(HEADS):
                    last = nc.tensor.matmul(psZ[h % 2 * HD:(h % 2 + 1) * HD, h // 2 * P:(h // 2 + 1) * P],
                                            v[:, (u + 1) % 2, h * HD:(h + 1) * HD], pbd[:, h, :], start=True, stop=True)
                last.then_inc(d_pe("pv"), 1)
            if Bq:
                pe.wait_ge(*b_pool.done("q", tb))
                for p in range(PAIRS):
                    last = nc.tensor.transpose(psX[:, p * P:(p + 1) * P], rot[:, 0, p * P:(p + 1) * P], ident[:])
                last.then_inc(b_pe("qT"), 1)
            if Do:
                pe.wait_ge(*d_act.done("oT", td))
                if Cs:
                    pe.wait_ge(*c_dve.done("sub", t))
                for p in range(PAIRS):
                    last = nc.tensor.matmul(psS[:, 0:P], oT[:, p, :], w_out[:, p, :], start=(p == 0), stop=(p == PAIRS - 1))
                last.then_inc(d_pe("y"), 1)
            if A:
                pe.wait_ge(*a_dve.done("xn", ta))
                nc.tensor.transpose(psA[:, 128:256], xn[:], ident[:]).then_inc(a_pe("xnT"), 1)
            if Bq:
                pe.wait_ge(*b_pool.done("k", tb))
                for p in range(PAIRS):
                    last = nc.tensor.transpose(psY[:, p * P:(p + 1) * P], rot[:, 1, p * P:(p + 1) * P], ident[:])
                last.then_inc(b_pe("kT"), 1)

        run(pe, pipeline(turn))

    @block.scalar
    def _(sc_):
        sc_.wait_ge(*s_pe.done("gates"))
        nc.scalar.activation(dgb[:], psX[0:2 * AH, 0:B], ACT.Copy).then_inc(s_act("dgb"), 1)
        nc.scalar.activation(ugb[:], psY[:, 0:2 * B].rearrange("p (i b) -> p i b", i=2), ACT.Copy).then_inc(s_act("ugb"), 1)

        def turn(t, u, k, A, Bq, Cs, Do):
            ta, tb, td = t + 2, t + 1, t - 1
            if A:
                sc_.wait_ge(*a_pe.done("fold", ta))
                wait_if(sc_, a_pe, "up", ta - 1)
                nc.scalar.activation(act[:], psA[0:AH, 128:256], ACT.Relu).then_inc(a_act("act"), 1)
            if Cs:
                sc_.wait_ge(*c_pe.done("v", t))
                wait_if(sc_, d_pe, "pv", t - 2)
                nc.scalar.activation(v[:, u, :], psZ, ACT.Copy).then_inc(c_act("v"), 1)
                sc_.wait_ge(*c_dve.done("sub", t))
                wait_if(sc_, c_pool, "probs", t - 1)
                nc.scalar.activation(ex[:], sc[:], ACT.Exp, scale=float(HD) ** -0.5).then_inc(c_act("exp"), 1)
            if Do:
                sc_.wait_ge(*d_pe.done("pv", td))
                wait_if(sc_, d_pe, "y", td - 1)
                nc.scalar.activation(oT[:].rearrange("p a b -> p (a b)"), psZ, ACT.Copy).then_inc(d_act("oT"), 1)
            if Bq:
                sc_.wait_ge(*b_pe.done("qT", tb))
                nc.scalar.activation(qT[:].rearrange("p a b -> p (a b)"), psX, ACT.Copy).then_inc(b_act("qT"), 1)
            if A:
                sc_.wait_ge(*a_pe.done("xnT", ta))
                wait_if(sc_, c_pe, "v", ta - 2)
                nc.scalar.activation(xnT[:, u, :], psA[:, 128:256], ACT.Identity, scale=ln_gb[:, 0:1],
                                     bias=ln_gb[:, 1:2]).then_inc(a_act("xnT"), 1)
            if Bq:
                sc_.wait_ge(*b_pe.done("kT", tb))
                wait_if(sc_, c_pe, "scores", tb - 1)
                for h in range(2):
                    rows = slice(h * HD, (h + 1) * HD)
                    nc.scalar.activation(kbd[rows, :, :, h, :].rearrange("p a b n -> p (a b) n"),
                                         psY[rows, :].rearrange("p (c n) -> p c n", n=N), ACT.Copy).then_inc(b_act(f"k{h}"), 1)

        run(sc_, pipeline(turn))

    @block.gpsimd
    def _(pool):
        nc.gpsimd.memset(half[:], -0.5).then_inc(zeroed, 1)
        nc.gpsimd.memset(eps[:], 1e-5).then_inc(zeroed, 1)
        nc.gpsimd.memset(w_down[:, AH:], 1.0).then_inc(zeroed, 1)
        nc.gpsimd.memset(w_up[:, 1, :], 1.0).then_inc(zeroed, 1)
        nc.gpsimd.memset(kbd[:], 0.0).then_inc(zeroed, 1)
        nc.gpsimd.memset(pbd[:], 0.0).then_inc(zeroed, 1)
        pool.wait_ge(zeroed, ZEROED)

        def turn(t, u, k, A, Bq, Cs, Do):
            ta, tb, td = t + 2, t + 1, t - 1
            if Bq:
                pool.wait_ge(*b_dve.done("qs2", tb))
                wait_if(pool, b_pe, "qT", tb - 1)
                nc.gpsimd.tensor_tensor(rot[:, 0, :], rc[:, 0, :], rs[:, 0, :], ALU.add).then_inc(b_pool("q"), 1)
            if A:
                pool.wait_ge(*a_dve.done("mv", ta))
                nc.gpsimd.tensor_tensor(veps[:], mv[:, 1:2], eps[:], ALU.add).then_inc(a_pool("veps"), 1)
                pool.wait_ge(*a_pool.done("veps", ta))
                wait_if(pool, a_dve, "xn", ta - 1)
                nc.gpsimd.tensor_tensor(rstd[:], veps[:], half[:], ALU.pow).then_inc(a_pool("rstd"), 1)
            if Bq:
                pool.wait_ge(*b_dve.done("ks2", tb))
                wait_if(pool, b_pe, "kT", tb - 1)
                nc.gpsimd.tensor_tensor(rot[:, 1, :], rc[:, 1, :], rs[:, 1, :], ALU.add).then_inc(b_pool("k"), 1)
            if Cs:
                pool.wait_ge(x_read[u], (k + 1) * 16)
                wait_if(pool, d_dve, "x1", t - 2)
                nc.gpsimd.tensor_tensor(xb[:, u, :], x_in[:, u, :], b_out[:], ALU.add).then_inc(e_pool("xb"), 1)
                pool.wait_ge(*c_dve.done("rsum", t))
                wait_if(pool, d_dve, "probsT", t - 1)
                nc.gpsimd.tensor_tensor(pr[:], ex[:], rsm[:].unsqueeze(2).broadcast_to([P, HEADS, N]),
                                        ALU.mult).then_inc(c_pool("probs"), 1)

        run(pool, pipeline(turn))

    @block.vector
    def _(dve):
        dve.wait_ge(*s_act.done("ugb"))

        def rope_cos(t, i, psum):
            name = "qk"[i]
            dve.wait_ge(*b_pe.done(name, t))
            wait_if(dve, b_pool, name, t - 1)
            nc.vector.tensor_tensor(rc[:, i, :].rearrange("p (h f) -> p h f", f=HD), psum.rearrange("p (h f) -> p h f", f=HD),
                                    cos[:].unsqueeze(1).broadcast_to([P, HEADS, HD]), ALU.mult).then_inc(b_dve(name + "c"), 1)

        def rope_sin(t, i, psum, j):
            out, other = slice(j * HALF, (j + 1) * HALF), slice((1 - j) * HALF, (2 - j) * HALF)
            nc.vector.tensor_tensor(rs[:, i, :].rearrange("p (h f) -> p h f", f=HD)[:, :, out],
                                    psum.rearrange("p (h f) -> p h f", f=HD)[:, :, other],
                                    sin[:, out].unsqueeze(1).broadcast_to([P, HEADS, HALF]),
                                    ALU.mult).then_inc(b_dve(f"{'qk'[i]}s{j + 1}"), 1)

        def turn(t, u, k, A, Bq, Cs, Do):
            ta, tb, td = t + 2, t + 1, t - 1
            if A:
                dve.wait_ge(*a_pe.done("down", ta))
                wait_if(dve, a_pe, "fold", ta - 1)
                nc.vector.tensor_tensor(gated[:].rearrange("p (b n) -> p b n", b=GB),
                                        psA[0:2 * AH, 0:P].rearrange("p (b n) -> p b n", b=GB),
                                        dgb[:, bass.ds(ta * GB, GB)].unsqueeze(2).broadcast_to([2 * AH, GB, N]),
                                        ALU.mult).then_inc(a_dve("gated"), 1)
            if Do:
                dve.wait_ge(*c_pool.done("probs", td))
                wait_if(dve, d_pe, "pv", td - 1)
                for b in range(GB):
                    rows = slice(b * N, (b + 1) * N)
                    last = nc.vector.transpose(pbd[rows, :, rows], pr[rows, :, :])
                last.then_inc(d_dve("probsT"), 1)
            if Bq:
                rope_cos(tb, 0, psX)
                rope_sin(tb, 0, psX, 0)
                rope_sin(tb, 0, psX, 1)
            if Cs:
                dve.wait_ge(*c_pe.done("scores", t))
                wait_if(dve, c_dve, "sub", t - 1)
                s3 = psS.rearrange("p (h n) -> p h n", n=N)
                nc.vector.tensor_reduce(mx[:], s3, AX, ALU.max).then_inc(c_dve("max"), 1)
                dve.wait_ge(*c_dve.done("max", t))
                wait_if(dve, c_act, "exp", t - 1)
                nc.vector.tensor_tensor(sc[:], s3, mx[:].unsqueeze(2).broadcast_to([P, HEADS, N]),
                                        ALU.subtract).then_inc(c_dve("sub"), 1)
            if A:
                dve.wait_ge(*a_pe.done("up", ta))
                wait_if(dve, a_pe, "sum", ta - 1)
                nc.vector.tensor_tensor(ups[:].rearrange("p i (b n) -> p i b n", b=GB),
                                        psA[:, 256:512].rearrange("p (i b n) -> p i b n", i=2, b=GB),
                                        ugb[:, :, bass.ds(ta * GB, GB)].unsqueeze(3).broadcast_to([P, 2, GB, N]),
                                        ALU.mult).then_inc(a_dve("ups"), 1)
                dve.wait_ge(*a_dve.done("ups", ta))
                nc.vector.tensor_tensor(hres[:], ups[:, 0, :], xT[:, bass.ds(ta * P, P)], ALU.add).then_inc(a_dve("hres"), 1)
            if Bq:
                rope_cos(tb, 1, psY)
            if A:
                dve.wait_ge(*a_pe.done("sum", ta))
                nc.vector.bn_stats(stats[:], psA[:, 0:P]).then_inc(a_dve("stats"), 1)
                dve.wait_ge(*a_dve.done("stats", ta))
                wait_if(dve, a_pool, "veps", ta - 1)
            if Bq:
                rope_sin(tb, 1, psY, 0)
            if A:
                nc.vector.bn_aggr(mv[:], stats[:]).then_inc(a_dve("mv"), 1)
            if Bq:
                rope_sin(tb, 1, psY, 1)
            if A:
                dve.wait_ge(*a_pool.done("rstd", ta))
                wait_if(dve, a_pe, "xnT", ta - 1)
                nc.vector.tensor_scalar(xn[:], psA[:, 0:P], mv[:, 0:1], rstd[:, 0:1], ALU.subtract,
                                        ALU.mult).then_inc(a_dve("xn"), 1)
            if Cs:
                dve.wait_ge(*c_act.done("exp", t))
                nc.vector.tensor_reduce(sm[:], ex[:], AX, ALU.add).then_inc(c_dve("sum"), 1)
                dve.wait_ge(*c_dve.done("sum", t))
                wait_if(dve, c_pool, "probs", t - 1)
                nc.vector.reciprocal(rsm[:], sm[:]).then_inc(c_dve("rsum"), 1)
            if Do:
                dve.wait_ge(*d_pe.done("y", td))
                dve.wait_ge(*e_pool.done("xb", td))
                if not isinstance(td, int) or td >= 2:
                    dve.wait_ge(x_written[(u + 1) % 2], (k if u else k - 1) * 16)
                nc.vector.tensor_tensor(x_out[:, (u + 1) % 2, :], psS[:, 0:P], xb[:, (u + 1) % 2, :], ALU.add).then_inc(d_dve("x1"), 1)

        run(dve, pipeline(turn))


EXPERTS, HID = 8, 256
EX0 = EXPERTS + 1
TOP_K = 2
NC = 4
CH = NC * B
CHUNKS = N // NC
H1, D1 = 16, 8
OFF = H1 // 2 + 1
KDEC = 30
SYS = NC * H1


def weight_tiles(nc, ctx):

    def sb(name, shape):
        return ctx.enter_context(nc.sbuf_tensor("w_" + name, shape, F32))

    ident = sb("ident", [P, P])
    w2c = sb("w2c", [P, D])
    vecs = sb("vecs", [P, 6])
    w_r0, w_r1 = sb("w_r0", [P, EXPERTS]), sb("w_r1", [P, EXPERTS])
    w13 = sb("w13", [P, EX0, 2, HID])
    w2 = sb("w2", [P, EX0, 2, D])
    kwT, owT = sb("kwT", [P, D]), sb("owT", [P, D])
    wqkv1 = sb("wqkv1", [P, 3, D])
    wfb = sb("wfb", [P, 2 * H1])
    wo1 = sb("wo1", [P, D])
    g1 = sb("g1", [P, D1])
    g2 = sb("g2", [D1, D])
    rows = sb("rows", [P, 3, D])
    fbias = sb("fbias", [P, 2 * H1])
    bdec = sb("bdec", [P, KDEC])
    bdecb = sb("bdecb", [KDEC, 1])
    vmat = sb("vmat", [KDEC, D])
    w_up = sb("w_up", [P, EXPERTS, 2 * HID])
    w_dn = sb("w_dn", [P, EXPERTS, 2, D])
    ahead = sb("ahead", [P, EXPERTS * EXPERTS])
    return dict(ident=ident, w2c=w2c, vecs=vecs, w_r0=w_r0, w_r1=w_r1, kwT=kwT, owT=owT, wqkv1=wqkv1, wfb=wfb, wo1=wo1, g1=g1,
                g2=g2, rows=rows, fbias=fbias, bdec=bdec, bdecb=bdecb, vmat=vmat, ahead=ahead, w13=w13, w2=w2, w_up1=w_up, w_dn1=w_dn)


UNITS1, UNITS = 2 * EXPERTS, 2 * (EX0 + EXPERTS)
ROOTS = 3
MAGIC = float(0x5F3759DF)


def ROOT(of):
    return " ".join([f"h{of}"] + [f"{s}{of}{i}" for i in range(ROOTS) for s in "rstu"])


HO = 4
HP = (D1 - 1) * D1 * SYS - H1 * D
OWN = 5
UPPER = ((slice(0, D1 // 2), slice(0, D1)), (slice(D1 // 2, D1), slice(D1 // 2, D1)))


TG = 4

AT = dict(back=0, x2T=1, x1=1, xk=2, xm=2, oprod=2, op=2, kx=3, yy=3, dm=3, kx0=3, o1=3, r0=4, og=4, ogsq=4, kxadd=4,
          sub0=6, ss=6, kxdup=6, prod0=6, rooto=6, sd0=7, ogn=8, prod1=8, sd1=9, og2=9, ogT=10, sddup=10, ogTa=11,
          sf1=11, sub=11, x3m=12, x3=12, e0=12, exp=12, sum=12, probs0=12, copies=12, probs=12, ranks0=14, ap0=14, q=14,
          x3T=14, sqq=14, sqk=14, av0=15, k=15, av1=17, v=17, va=17, ssq=17, fb=18, av2=18, x3Ta=18, rootq=18, fb0=19,
          fbt=19, av3=19, t0=19, fb1=20, qk=20, g=20, t1=20, gT=20, mv0=20, Ua=20, gate=21, gatea=21, t2=21, Uk=21,
          oT=21, hk0=21, Ub=21, hv0=21, t3=22, xo=22, hk1=22, v1=22, y=23, y1=23, t=23, hk2=23, v2=23, y2T=24, z=24,
          hk3=24, za=25, carry=25, diag=25, el0=25, v3=25, ms=26, el1=26, rootz=26, el2=27, base=27, zn=28, lr0=28,
          lr1=28, lr2=28, znT=29, el3=29, el4=29, lr3=29, znTa=30, r1=30, lr4=30, sub1=31, el5=31, lr5=31, e1=32,
          ranks1=32, cw1=32, el6=33, rhs=33)


def mixing_phase(nc, ctx, dram, w, loaded, x1, out):

    def sb(name, shape):
        return ctx.enter_context(nc.sbuf_tensor("p2_" + name, shape, F32))

    def sem(name):
        return ctx.enter_context(nc.semaphore("p2_" + name))

    ident, w2c, vecs, w_r0, w_r1, kwT, owT, wqkv1, wfb, wo1 = (w[k] for k in "ident w2c vecs w_r0 w_r1 kwT owT wqkv1 wfb wo1".split())
    g1, g2, rows, fbias, bdec, bdecb, vmat, ahead = (w[k] for k in "g1 g2 rows fbias bdec bdecb vmat ahead".split())
    w13, w2, w_up, w_dn = w["w13"], w["w2"], w["w_up1"], w["w_dn1"]

    half = sb("half", [P, 2])
    style = sb("style", [P, 3, B])
    demod = sb("demod", [P, 3, B])
    lam = sb("lam", [P, D])
    Uw = sb("Uw", [P, KDEC, B])
    Ub = sb("Ub", [KDEC, B])

    xs = sb("xs", [P, CH])
    yT = sb("yT", [P, CH])
    ex8 = sb("ex8", [P, NC, EXPERTS])
    s8 = sb("s8", [P, NC, EXPERTS])
    m4 = sb("m4", [P, NC])
    p8 = sb("p8", [P, NC, EXPERTS])
    ge = sb("ge", [P, NC, EXPERTS * EXPERTS])
    rank = sb("rank", [P, NC, EXPERTS])
    cw0 = sb("cw0", [P, NC, EX0])
    cw1 = sb("cw1", [P, NC, EXPERTS])
    sil = sb("sil", [P, 2, CH])
    hid = sb("hid", [P, 2, CH])
    ssq = sil[:, 0, 0:3 * B].rearrange("p (i b) -> p i b", i=3)
    acc0 = sb("acc0", [P, CH])
    x2_next, x2_now = sb("x2_next", [P, CH]), sb("x2_now", [P, CH])
    ltmp = acc0[:, 0:D]
    xk = sb("xk", [P, CH])
    kx0 = sb("kx0", [P, CH])
    kx = sb("kx", [P, NC, 2, D])
    prod = sb("prod", [P, (D1 - 1) * D1 * SYS])
    wsq = prod[:, 0:3 * B].rearrange("p (i b) -> p i b", i=3)
    sd = sb("sd", [P, NC, OFF, 2, H1])
    sf = sb("sf", [P, NC, H1, H1])
    mxh = sb("mxh", [P, NC, H1])
    smh = sb("smh", [P, NC, H1])
    rsh = sb("rsh", [P, NC, H1])
    mixed = sb("mixed", [P, CH])
    y2T = sb("y2T", [P, CH])
    ssr = sb("ssr", [P, 2, SYS])
    rn = sb("rn", [P, 2, SYS])
    kv = sb("kv", [P, 2 * D1, SYS])
    fb0 = sb("fb0", [P, NC, 2, H1])
    fb = fbt = sb("fb", [P, NC, 2, H1])
    bk = sb("bk", [P, D1, SYS])
    Hv = sb("Hv", [P, D1 * D1, NC, H1])
    carry = sb("carry", [P, D1 * D1, H1])
    scaled = sb("scaled", [P, 2, CH])
    A = sb("A", [P, D1, D1 + 1, SYS])
    poolT = sb("poolT", [P, D1 * D1 * H1])
    T = prod[:].rearrange("p (a s) -> p a s", s=SYS)
    early = A[0:C, :, :, :].rearrange("p i j s -> p (i j s)")
    WDEC, AFF = (D + 1) * KDEC, 3 * D
    wdec = early[:, 0:WDEC]
    aff = early[:, WDEC:WDEC + AFF].rearrange("c (i d) -> c i d", i=3)
    condT = early[:, WDEC + AFF:WDEC + AFF + B]
    A4 = A[:].rearrange("p i j (n h) -> p i j n h", n=NC)
    gT = sb("gT", [D1, CH])
    gate = sb("gate", [P, CH])
    o1 = sb("o1", [P, CH])
    ogT = xk
    x3 = sb("x3", [P, CH])
    x3T = sb("x3T", [P, CH])
    tK = sb("tK", [KDEC, NC, B])
    z = sb("z", [P, CH])
    ms4 = sb("ms4", [P, 2, NC])
    zn = sb("zn", [P, CH])
    sqr = (zn, gate)
    res = sb("res", [P, CH])
    xm = zn
    newton = sb("newton", [P, 2, 2 * SYS])

    loaded_early = sem("loaded_early")
    zeroed = sem("zeroed")
    su_pe = Steps(sem("gates_pe"), "gates sums uw")
    su_dve = Steps(sem("gates_dve"), "st0 st1 st2 ssq0 ssq1 ssq2 wsq0 wsq1 wsq2 dem0 gs0 dem1 gs1 dem2 gs2 l0 l1 l2 nw ub")
    su_act = Steps(sem("gates_act"), "e ln")
    su_pool = Steps(sem("gates_pool"), " ".join(ROOT(f"d{i}") for i in range(3)))
    UG = [(g, min(g + 4, KDEC)) for g in range(0, KDEC, 4)]
    su_u = Steps(sem("uw_pe"), " ".join(f"g{i}" for i in range(len(UG))))
    su_v = Steps(sem("uw_dve"), " ".join(f"g{i}" for i in range(len(UG))))

    x_read = sem("x_read")
    res_free = sem("res_free")
    up = Steps(sem("up"), " ".join(f"a{g} b{g}" for g in range(UNITS)))
    silu = Steps(sem("silu"), " ".join(f"s{g}" for g in range(UNITS)))
    mul = Steps(sem("mul"), " ".join(f"h{g}" for g in range(UNITS)))
    down = Steps(sem("down"), " ".join(f"d{g}" for g in range(UNITS)))
    acc = Steps(sem("acc"), " ".join(f"x{e}" for e in range(UNITS // 2)))
    scale = Steps(sem("scale"), " ".join(f"c{e}" for e in range(UNITS // 2)))
    in_pe = Steps(sem("in_pe"), "x1 y r0 x3T " + " ".join(f"t{j}" for j in range(TG)) + " z znT r1")
    in_act = Steps(sem("in_act"), "e0 x3T z zsq zn znT e1")
    in_dve = Steps(sem("in_dve"), "xm dm bias yT max0 sub0 sum0 rsum0 probs dif0 cmp0 rank0 rk2 cw0 t ms me yz "
                   "max1 sub1 raw dif1 cmp1 rank1 em sum1 rsum1 cw1")
    in_pool = Steps(sem("in_pool"), ROOT("z") + " base")
    k_pe = Steps(sem("k_pe"), "x2T kx oT y")
    k_dve = Steps(sem("k_dve"), "xk kx0 prod0 sd0 prod1 sd1 max sub sum rsum " + " ".join(f"ap{n} av{n}" for n in range(NC)) + " xo y1")
    k_pool = Steps(sem("k_pool"), "kx probs hp")
    k_act = Steps(sem("k_act"), "kxdup sddup sf0 sf1 exp x2 y2T")
    m_pe = Steps(sem("m_pe"), "q k v fb g gate ogT x3")
    m_act = Steps(sem("m_act"), "x2 sqq q sqk k v fbt gT gate carry_k ogT")
    LOW = D1 - 2
    ELIM = " ".join(f"ri{k} " + (f"col{k} " if k < D1 - 1 else "") + (f"t{k} a{k}" if k < LOW - 1 or k == LOW else "") for k in range(D1))
    BACK = " ".join(f"bt{k} bx{k}" for k in range(D1 - 1, 0, -1))
    m_dve = Steps(sem("m_dve"), "ssq ssk aq yq fb0 fb q k bk Uk " + " ".join(f"mk{n} hk{n}" for n in range(NC)) + " diag " + ELIM + " rhs " + BACK
                  + " oprod o1 og ss ao yo ogn x3")
    m_pool = Steps(sem("m_pool"), ROOT("q") + " mv0 Ua U hv0 " + " ".join(f"mv{n} hv{n}" for n in range(1, NC)) + " "
                   + " ".join(f"lt{k} la{k}" for k in range(LOW)) + " op sq " + ROOT("o") + " og2")

    ps = ctx.enter_context(nc.psum_tensor("p2_ps", [P, 8, 512], F32))
    psU, psDn = ps[:, 0:4, :], ps[:, 4:6, :]
    ps6, ps7 = ps[:, 6, :], ps[:, 7, :]

    def by_n(ap):
        return ap.rearrange("p (n b) -> p n b", n=NC)

    def bc_n(ap, parts=P):
        return ap.unsqueeze(1).broadcast_to([parts, NC, ap.shape[-1]])

    def head_windows(n, lo, hi):
        w = kx[:].rearrange("p n t d -> p n (t d)")[:, n, lo * D1:lo * D1 + D]
        return bass.AP(w.tensor, w.offset, [list(w.ap[0]), [D1, hi - lo], [D1, H1], [1, D1]])

    block = ctx.enter_context(nc.Block())
    early_loads = ((condT, "condT"), (aff, "aff"), (wdec, "wdec"))
    LOADED, LOADED_EARLY = 16 * len(w), 16 * len(early_loads)
    ZEROED = 5
    STYLE, SCALE_C = range(3), 0.125

    def active(g, F, G):
        return G if g < UNITS1 else F

    def earlier(g, d, t, G):
        if g >= UNITS1 and g - d < UNITS1 and not G:
            g -= UNITS1
        T = t + 2
        if g - d >= 0:
            return g - d, T
        if isinstance(T, int) and T < 1:
            return None
        return UNITS + g - d, T - 1

    def wait_unit(eng, steps, name, g, d, t, G):
        before = earlier(g, d, t, G)
        if before:
            eng.wait_ge(*steps.done(name + str(before[0]), before[1]))

    def fill(name, g, F):
        return name + str(UNITS - 1) if g == UNITS1 - 1 and not F else None

    class Slots:

        def __init__(self, unit):
            self.unit, self.next, self.at = unit, 0, 0

        def __call__(self, step):
            assert AT[step] >= self.at, (step, self.at)
            self.at = AT[step]
            self.up_to(self.at)

        def up_to(self, count):
            while self.next < count:
                self.unit(self.next)
                self.next += 1

    def run(eng, turn, between=None):

        def flags(t):
            return [0 <= t + d < CHUNKS for d in (2, 1, 0, -1, -2)]

        for t in range(-2, 2):
            if t == -1 and between:
                between()
            turn(t, *flags(t))
        with eng.Fori(2, CHUNKS - 2) as t:
            turn(t, True, True, True, True, True)
        for t in range(CHUNKS - 2, CHUNKS + 2):
            turn(t, *flags(t))

    @block.sync
    def _(sp):
        for dst, name in early_loads:
            sp.dma_start(dst if dst.__class__ is bass.AP else dst[:], dram[name]).then_inc(loaded_early, 16)

        def turn(t, F, M, RA, RB, G):
            if F:
                wait_if(sp, acc, f"x{EXPERTS}", t + 1)
                sp.dma_start(xs[:], x1[:, bass.ds((t + 2) * CH, CH)]).then_inc(x_read, 16)
            if G:
                sp.wait_ge(*acc.done(f"x{EXPERTS - 1}", t + 2))
                sp.dma_start(out[:, bass.ds((t - 2) * CH, CH)], res[:]).then_inc(res_free, 16)

        run(sp, turn)
        sp.wait_ge(res_free, 16 * (CHUNKS + 1))

    @block.tensor
    def _(pe):
        pe.wait_ge(loaded, LOADED)
        pe.wait_ge(loaded_early, LOADED_EARLY)
        for i in STYLE:
            last = nc.tensor.matmul(ps6[:, i * B:(i + 1) * B], aff[:, i, :], condT, start=True, stop=True)
        last.then_inc(su_pe("gates"), 1)
        pe.wait_ge(*su_dve.done("wsq2"))
        nc.tensor.matmul(ps7[:, 0:B], wsq[:, 0, :], ssq[:, 0, :], start=True, stop=True)
        nc.tensor.matmul(ps7[:, B:2 * B], ssq[:, 1, :], wsq[:, 1, :], start=True, stop=True)
        nc.tensor.matmul(ps7[:, 2 * B:3 * B], wsq[:, 2, :], ssq[:, 2, :], start=True, stop=True).then_inc(su_pe("sums"), 1)
        pe.wait_ge(*su_dve.done("gs2"))

        def generated_weights():
            wk = wdec.rearrange("c (i k) -> c k i", k=KDEC)
            for g, (lo, hi) in enumerate(UG):
                if g:
                    pe.wait_ge(*su_v.done(f"g{g - 1}"))
                for k in range(lo, hi):
                    last = nc.tensor.matmul(ps6[:, (k - lo) * B:(k - lo + 1) * B], wk[:, k, 0:D], condT, start=True, stop=True)
                last.then_inc(su_u(f"g{g}"), 1)
            pe.wait_ge(*su_v.done(f"g{len(UG) - 1}"))
            nc.tensor.matmul(ps6[0:KDEC, 0:B], wk[:, :, D], condT, start=True, stop=True).then_inc(su_pe("uw"), 1)
            pe.wait_ge(*su_dve.done("ub"))

        def turn(t, F, M, RA, RB, G):
            U, K, N2 = t + 2, t + 1, t + 2

            def unit(g):
                if g < UNITS and active(g, F, G):
                    if g == 0:
                        pe.wait_ge(*in_act.done("znT", U - 1))
                    if g == UNITS1:
                        pe.wait_ge(*in_dve.done("yT", U))
                    wait_unit(pe, mul, "h", g, 2, t, G)
                    q, x_in = g % 2, x3T if g < UNITS1 else yT
                    e, part = g // 2, slice(g % 2 * P, (g % 2 + 1) * P)
                    if g < UNITS1:
                        wa, wb = w_up[:, e, HID:][:, part], w_up[:, e, 0:HID][:, part]
                    else:
                        wa, wb = w13[:, e - EXPERTS, 0, part], w13[:, e - EXPERTS, 1, part]
                    nc.tensor.matmul(psU[:, 2 * q, :], wa, x_in[:], start=True, stop=True).then_inc(*up.step(f"a{g}"))
                    nc.tensor.matmul(psU[:, 2 * q + 1, :], wb, x_in[:], start=True, stop=True).then_inc(*up.step(f"b{g}", fill("b", g, F)))
                j = g - 2
                if j >= 0 and active(j, F, G):
                    e, half_ = j // 2, j % 2
                    pe.wait_ge(*mul.done(f"h{j}", U))
                    if half_ == 0:
                        before = earlier(j, 4, t, G)
                        if before:
                            pe.wait_ge(*scale.done(f"c{before[0] // 2}", before[1]))
                    w = w_dn[:, e, half_, :] if j < UNITS1 else w2[:, e - EXPERTS, half_, :]
                    for n in range(NC):
                        last = nc.tensor.matmul(psDn[:, e % 2, n * P:(n + 1) * P], hid[:, half_, n * P:(n + 1) * P], w,
                                                start=(half_ == 0 and n == 0), stop=(half_ == 1), skip_group_check=True)
                    last.then_inc(*down.step(f"d{j}", fill("d", j, F)))

            to = Slots(unit)

            def four(ps_, lhsT, rhs):
                for n in range(NC):
                    last = nc.tensor.matmul(ps_[:, n * P:(n + 1) * P], lhsT[:, n * P:(n + 1) * P], rhs, start=True, stop=True)
                return last

            def turned(ps_, x):
                for n in range(NC):
                    last = nc.tensor.transpose(ps_[:, n * P:(n + 1) * P], x[:, n * P:(n + 1) * P], ident[:])
                return last

            def generated(j):
                for b in range(j * B // TG, (j + 1) * B // TG):
                    last = nc.tensor.matmul(ps7[0:KDEC, b * NC:(b + 1) * NC], Uw[:, :, b], by_n(x3T[:])[:, :, b], start=True, stop=True)
                last.then_inc(*in_pe.step(f"t{j}"))

            if M:
                to("x2T")
                pe.wait_ge(*acc.done(f"x{UNITS // 2 - 1}", U - 1))
                if RA:
                    pe.wait_ge(*k_dve.done("y1", t))
                turned(ps6, acc0).then_inc(*k_pe.step("x2T"))
            if F:
                to("x1")
                pe.wait_ge(x_read, (t + 3) * 16)
                wait_if(pe, in_dve, "raw", U - 1)
                turned(ps7, xs).then_inc(*in_pe.step("x1"))
            if M:
                to("kx")
                pe.wait_ge(*k_dve.done("xk", K))
                four(ps6, xk, kwT[:]).then_inc(*k_pe.step("kx"))
            if F:
                to("yy")
                pe.wait_ge(*in_dve.done("xm", N2))
                nc.tensor.matmul(ps7, w2c[:], xm[:], start=True, stop=True).then_inc(*in_pe.step("y"))
                to("r0")
                pe.wait_ge(*in_dve.done("yT", N2))
                for n in range(NC):
                    last = nc.tensor.matmul(ps7[:, n * EXPERTS:(n + 1) * EXPERTS], yT[:, n * P:(n + 1) * P], w_r0[:], start=True, stop=True)
                last.then_inc(*in_pe.step("r0", None if RB else "r1"))
            if RB:
                to("ogT")
                if M:
                    pe.wait_ge(*k_dve.done("kx0", K))
                elif RA:
                    pe.wait_ge(*k_dve.done("y1", t))
                else:
                    pe.wait_ge(*m_act.done("gate", t - 1))
                pe.wait_ge(*m_pool.done("og2", t - 1))
                turned(ps6, o1).then_inc(*m_pe.step("ogT"))
                to("x3m")
                pe.wait_ge(*m_act.done("ogT", t - 1))
                four(ps6, ogT, wo1[:]).then_inc(*m_pe.step("x3"))
            if RA:
                to("q")
                if RB:
                    pe.wait_ge(*m_dve.done("x3", t - 1))
                elif M:
                    pe.wait_ge(*k_dve.done("kx0", K))
                pe.wait_ge(*k_act.done("y2T", t))
                four(ps6, y2T, wqkv1[:, 0, :]).then_inc(*m_pe.step("q"))
            if RB:
                to("x3T")
                pe.wait_ge(*m_dve.done("x3", t - 1))
                if F:
                    pe.wait_ge(*in_dve.done("sub0", U))
                else:
                    pe.wait_ge(*in_dve.done("raw", U - 1))
                turned(ps7, x3).then_inc(*in_pe.step("x3T"))
            if RA:
                to("k")
                pe.wait_ge(*m_act.done("q", t))
                four(ps6, y2T, wqkv1[:, 1, :]).then_inc(*m_pe.step("k"))
                to("v")
                pe.wait_ge(*m_act.done("k", t))
                four(ps6, y2T, wqkv1[:, 2, :]).then_inc(*m_pe.step("v"))
                to("fb")
                pe.wait_ge(*m_act.done("v", t))
                for n in range(NC):
                    last = nc.tensor.matmul(ps6[:, n * 32:(n + 1) * 32], y2T[:, n * P:(n + 1) * P], wfb[:], start=True, stop=True)
                last.then_inc(*m_pe.step("fb"))
            if RB:
                to("t0")
                pe.wait_ge(*in_act.done("x3T", N2))
                generated(0)
            if RA:
                to("g")
                pe.wait_ge(*m_dve.done("fb0", t))
                nc.tensor.matmul(ps6[0:D1, :], g1[:], y2T[:], start=True, stop=True).then_inc(*m_pe.step("g"))
            if RB:
                to("t1")
                generated(1)
            if RA:
                to("gate")
                pe.wait_ge(*m_act.done("gT", t))
                four(ps6, gT, g2[:]).then_inc(*m_pe.step("gate"))
            if RB:
                to("t2")
                generated(2)
            if M:
                to("oT")
                if RA:
                    pe.wait_ge(*m_act.done("gate", t))
                else:
                    pe.wait_ge(*k_dve.done("kx0", K))
                pe.wait_ge(*k_dve.done(f"av{NC - 1}", K))
                turned(ps6, mixed).then_inc(*k_pe.step("oT"))
            if RB:
                to("t3")
                generated(3)
            if M:
                to("y")
                pe.wait_ge(*k_dve.done("xo", K))
                nc.tensor.matmul(ps6, owT[:], xk[:], start=True, stop=True).then_inc(*k_pe.step("y"))
            if RB:
                to("z")
                pe.wait_ge(*in_dve.done("t", N2))
                for n in range(NC):
                    last = nc.tensor.matmul(ps7[:, n * P:(n + 1) * P], tK[:, n, :], vmat[:], start=True, stop=True)
                last.then_inc(*in_pe.step("z"))
                to("znT")
                pe.wait_ge(*in_act.done("zn", N2))
                turned(ps7, zn).then_inc(*in_pe.step("znT"))
                to("r1")
                pe.wait_ge(*in_act.done("znT", N2))
                for n in range(NC):
                    last = nc.tensor.matmul(ps7[:, n * EXPERTS:(n + 1) * EXPERTS], x3T[:, n * P:(n + 1) * P], w_r1[:], start=True, stop=True)
                last.then_inc(*in_pe.step("r1"))
            to.up_to(UNITS + 2)

        run(pe, turn, generated_weights)

    @block.scalar
    def _(act):
        act.wait_ge(*su_dve.done("l0"))
        nc.scalar.activation(lam[:], ltmp, ACT.Exp).then_inc(su_act("e"), 1)
        act.wait_ge(*su_act.done("e"))
        nc.scalar.activation(ltmp, lam[:], ACT.Ln, bias=1.0).then_inc(su_act("ln"), 1)

        def copy(out_, in_, func=ACT.Copy, **kw):
            return nc.scalar.activation(out_, in_, func, **kw)

        def turn(t, F, M, RA, RB, G):
            U, K, N2 = t + 2, t + 1, t + 2

            def unit(g):
                if g < UNITS and active(g, F, G):
                    act.wait_ge(*up.done(f"a{g}", U))
                    wait_unit(act, mul, "h", g, 2, t, G)
                    copy(sil[:, g % 2, :], psU[:, 2 * (g % 2), :], ACT.Silu).then_inc(*silu.step(f"s{g}", fill("s", g, F)))
                e = (g - 4) // 2
                if g % 2 == 0 and e >= 0 and active(2 * e, F, G):
                    act.wait_ge(*down.done(f"d{2 * e + 1}", U))
                    before = earlier(2 * e, 4, t, G)
                    if before:
                        act.wait_ge(*acc.done(f"x{before[0] // 2}", before[1]))
                    if e == 0:
                        act.wait_ge(*in_dve.done("cw1", U - 1))
                    elif e == EXPERTS:
                        act.wait_ge(*in_dve.done("cw0", U))
                    for n in range(NC):
                        part = slice(n * D, (n + 1) * D)
                        w_ = cw1[:, n, e:e + 1] if e < EXPERTS else cw0[:, n, e - EXPERTS:e - EXPERTS + 1]
                        last = copy(scaled[:, e % 2, part], psDn[:, e % 2, part], scale=w_)
                    last.then_inc(*scale.step(f"c{e}", f"c{UNITS // 2 - 1}" if e == EXPERTS - 1 and not F else None))

            to = Slots(unit)
            planes = ps6.rearrange("p (n h j) -> p j n h", n=NC, h=H1)
            if M:
                to("kxdup")
                act.wait_ge(*k_pool.done("kx", K))
                copy(kx[:, :, 1, :], kx[:, :, 0, :]).then_inc(*k_act.step("kxdup"))
                to("sddup")
                act.wait_ge(*k_dve.done(f"sd{NC // 2 - 1}", K))
                copy(sd[:, :, :, 1, :], sd[:, :, :, 0, :]).then_inc(*k_act.step("sddup"))
                copy(sf[:, :, 0:OFF, :], sd[:, :, :, 0, :]).then_inc(*k_act.step("sf0"))
                act.wait_ge(*k_act.done("sddup", K))
                for n in range(NC):
                    s0 = sd[:, n, 0, 0, 0:1]
                    back = bass.AP(s0.tensor, s0.offset + (H1 - OFF) * 2 * H1 + OFF, [list(s0.ap[0]), [1 - 2 * H1, H1 - OFF], [1, H1]])
                    last = copy(sf[:, n, OFF:H1, :], back)
                last.then_inc(*k_act.step("sf1"))
            if RB:
                to("ogTa")
                act.wait_ge(*m_pe.done("ogT", t - 1))
                copy(ogT[:], ps6).then_inc(*m_act.step("ogT"))
            if F:
                to("e0")
                act.wait_ge(*in_dve.done("sub0", N2))
                copy(ex8[:], s8[:], ACT.Exp).then_inc(*in_act.step("e0", None if RB else "e1"))
            if M:
                to("exp")
                act.wait_ge(*k_dve.done("sub", K))
                copy(sf[:].rearrange("p n o h -> p (n o h)"), sf[:].rearrange("p n o h -> p (n o h)"), ACT.Exp,
                     scale=float(D1) ** -0.5).then_inc(*k_act.step("exp"))
            to("copies")
            if RA:
                if RB:
                    act.wait_ge(*m_dve.done("x3", t - 1))
                act.wait_ge(*k_act.done("x2", t))
                copy(x2_now[:], x2_next[:]).then_inc(*m_act.step("x2"))
            if M:
                act.wait_ge(*acc.done(f"x{UNITS // 2 - 1}", U - 1))
                if RA:
                    act.wait_ge(*m_act.done("x2", t))
                copy(x2_next[:], acc0[:]).then_inc(*k_act.step("x2"))

            def square_and_keep(i, name):
                to("sq" + name)
                act.wait_ge(*m_pe.done(name, t))
                if RB:
                    act.wait_ge(*m_dve.done("ss", t - 1))
                if F:
                    act.wait_ge(*in_pe.done("y", N2))
                copy(sqr[i][:], ps6, ACT.Square).then_inc(*m_act.step("sq" + name))
                dst = A[:, :, D1, :] if i == 0 else kv[:, 0:D1, :]
                copy(dst.rearrange("p j (n h) -> p j n h", n=NC), planes).then_inc(*m_act.step(name))

            if RA:
                if RB:
                    act.wait_ge(*m_pool.done(f"hv{NC - 1}", t - 1))
                square_and_keep(0, "q")
                square_and_keep(1, "k")
                to("va")
                act.wait_ge(*m_pe.done("v", t))
                copy(kv[:, D1:2 * D1, :].rearrange("p j (n h) -> p j n h", n=NC), planes).then_inc(*m_act.step("v"))
            if RB:
                to("x3Ta")
                act.wait_ge(*in_pe.done("x3T", N2))
                if G:
                    act.wait_ge(*up.done(f"b{UNITS1 - 1}", U))
                copy(x3T[:], ps7).then_inc(*in_act.step("x3T"))
            if RA:
                to("fbt")
                act.wait_ge(*m_dve.done("fb0", t))
                copy(fbt[:], fb0[:], ACT.Tanh, scale=0.5).then_inc(*m_act.step("fbt"))
                to("gT")
                act.wait_ge(*m_pe.done("g", t))
                copy(gT[:], ps6[0:D1, :]).then_inc(*m_act.step("gT"))
                to("gatea")
                act.wait_ge(*m_pe.done("gate", t))
                act.wait_ge(*m_dve.done("ssk", t))
                copy(gate[:], ps6, ACT.Tanh, scale=0.5).then_inc(*m_act.step("gate"))
            if M:
                to("y2T")
                act.wait_ge(*k_dve.done("y1", K))
                copy(y2T[:], kx0[:], ACT.Identity, bias=vecs[:, 1:2]).then_inc(*k_act.step("y2T"))
            if RB:
                to("za")
                act.wait_ge(*in_pe.done("z", N2))
                copy(z[:], ps7).then_inc(*in_act.step("z"))
                copy(zn[:], ps7, ACT.Square).then_inc(*in_act.step("zsq"))
            if RA:
                to("carry")
                act.wait_ge(*m_dve.done(f"hk{NC - 1}", t))
                for i, j in UPPER:
                    last = copy(carry[:].rearrange("p (i j) h -> p i j h", i=D1)[:, i, j], A4[:, i, j, NC - 1, :])
                last.then_inc(*m_act.step("carry_k"))
            if RB:
                to("zn")
                act.wait_ge(*in_pool.done(f"uz{ROOTS - 1}", t - 1))
                for n in range(NC):
                    last = copy(zn[:, n * D:(n + 1) * D], z[:, n * D:(n + 1) * D], scale=ms4[:, 1, n:n + 1])
                last.then_inc(*in_act.step("zn"))
                to("znTa")
                act.wait_ge(*in_pe.done("znT", N2))
                copy(x3T[:], ps7, scale=vecs[:, 5:6]).then_inc(*in_act.step("znT"))
                to("e1")
                act.wait_ge(*in_dve.done("sub1", N2))
                copy(ex8[:], s8[:], ACT.Exp).then_inc(*in_act.step("e1"))
            to.up_to(UNITS + 3)

        run(act, turn)

    @block.gpsimd
    def _(pool):
        tt = nc.gpsimd.tensor_tensor

        def root(S, of, tile, y, a):
            width = y.shape[-1]
            h, w = newton[:, 0, 0:width], newton[:, 1, 0:width]
            minus_half, three_halves = (half[:, i:i + 1].broadcast_to([P, width]) for i in (0, 1))
            tt(h, a, minus_half, ALU.mult).then_inc(*S.step(f"h{of}"))
            for i in range(ROOTS):
                pool.wait_ge(*S.done(f"u{of}{i - 1}" if i else f"h{of}", tile))
                tt(w, y, y, ALU.mult).then_inc(*S.step(f"r{of}{i}"))
                pool.wait_ge(*S.done(f"r{of}{i}", tile))
                tt(w, w, h, ALU.mult).then_inc(*S.step(f"s{of}{i}"))
                pool.wait_ge(*S.done(f"s{of}{i}", tile))
                tt(w, w, three_halves, ALU.add).then_inc(*S.step(f"t{of}{i}"))
                pool.wait_ge(*S.done(f"t{of}{i}", tile))
                tt(y, y, w, ALU.mult).then_inc(*S.step(f"u{of}{i}"))

        for dst, val in ((half[:, 0:1], -0.5), (half[:, 1:2], 1.5), (carry, 0.0), (Hv, 0.0), (cw0, 1.0 / (TOP_K + 1))):
            nc.gpsimd.memset(dst if dst.__class__ is bass.AP else dst[:], val).then_inc(zeroed, 1)
        nc.gpsimd.memset(res[:], 0.0).then_inc(res_free, 16)
        pool.wait_ge(zeroed, ZEROED)
        for i in STYLE:
            pool.wait_ge(*su_dve.done(f"gs{i}"))
            root(su_pool, f"d{i}", 0, demod[:, i, :], wsq[:, i, :])

        def turn(t, F, M, RA, RB, G):
            U, K, N2 = t + 2, t + 1, t + 2

            def unit(g):
                e = (g - 5) // 2
                if g % 2 == 1 and e >= 0 and active(2 * e, F, G):
                    pool.wait_ge(*scale.done(f"c{e}", U))
                    sum_ = res if e < EXPERTS else acc0
                    if e == 0:
                        pool.wait_ge(*in_pool.done("base", t - 2))
                    elif e == EXPERTS:
                        pool.wait_ge(x_read, (t + 3) * 16)
                        if M:
                            pool.wait_ge(*k_pe.done("x2T", K))
                            pool.wait_ge(*k_act.done("x2", K))
                    else:
                        pool.wait_ge(*acc.done(f"x{e - 1}", U))
                    upto = f"x{UNITS // 2 - 1}" if e == EXPERTS - 1 and not F else None
                    tt(sum_[:], (xs if e == EXPERTS else sum_)[:], scaled[:, e % 2, :], ALU.add).then_inc(*acc.step(f"x{e}", upto))

            to = Slots(unit)
            if RB:
                to("op")
                pool.wait_ge(*m_dve.done("bx1", t - 1))
                pool.wait_ge(*m_pool.done(f"la{LOW - 1}", t - 1))
                tt(A[:, OWN:, 0:D1, :], A[:, OWN:, D1, :].unsqueeze(2).broadcast_to([P, D1 - OWN, D1, SYS]),
                   Hv[:].rearrange("p (i j) n h -> p i j (n h)", i=D1)[:, OWN:], ALU.mult).then_inc(*m_pool.step("op"))
                to("ogsq")
                pool.wait_ge(*m_dve.done("og", t - 1))
                tt(gate[:], o1[:], o1[:], ALU.mult).then_inc(*m_pool.step("sq"))
            if M:
                to("kxadd")
                pool.wait_ge(*k_dve.done("kx0", K))
                tt(kx[:, :, 0, :], by_n(kx0[:]), bc_n(rows[:, 0, :]), ALU.add).then_inc(*k_pool.step("kx"))
            if RB:
                to("rooto")
                pool.wait_ge(*m_dve.done("yo", t - 1))
                root(m_pool, "o", t - 1, rn[:, 0, :], ssr[:, 0, :])
                to("og2")
                pool.wait_ge(*m_dve.done("ogn", t - 1))
                tt(by_n(o1[:]), by_n(o1[:]), bc_n(rows[:, 2, :]), ALU.mult).then_inc(*m_pool.step("og2"))
            if M:
                to("probs")
                pool.wait_ge(*k_dve.done("rsum", K))
                tt(sf[:], sf[:], rsh[:].unsqueeze(2).broadcast_to([P, NC, H1, H1]), ALU.mult).then_inc(*k_pool.step("probs"))
                pool.wait_ge(*k_pool.done("probs", K))
                pool.wait_ge(*k_dve.done("sd1", K))
                tt(prod[:, HP + HO * D:HP + H1 * D].rearrange("p (o h d) -> p o h d", h=H1, d=D1),
                   sf[:, NC - 1, HO:, :].unsqueeze(3).broadcast_to([P, H1 - HO, H1, D1]), head_windows(NC - 1, HO, H1),
                   ALU.mult).then_inc(*k_pool.step("hp"))
            if RA:
                to("rootq")
                pool.wait_ge(*m_dve.done("yq", t))
                root(m_pool, "q", t, rn[:].rearrange("p i s -> p (i s)"), ssr[:].rearrange("p i s -> p (i s)"))
                pT = poolT[:].rearrange("p (a h) -> p a h", h=H1)
                lT = poolT[:, 0:2 * 3 * SYS].rearrange("p (i j s) -> p i j s", i=2, j=3)

                def decayed(n):
                    tt(pT, Hv[:, :, (n - 1) % NC, :], fb[:, n, 0, :].unsqueeze(1).broadcast_to([P, D1 * D1, H1]),
                       ALU.mult).then_inc(*m_pool.step(f"mv{n}"))

                def added(n):
                    pool.wait_ge(*m_pool.done(f"mv{n}" if n else "U", t))
                    tt(Hv[:, :, n, :], Hv[:, :, n, :], pT, ALU.add).then_inc(*m_pool.step(f"hv{n}"))

                def v_state(n, before):
                    to(f"v{n}")
                    pool.wait_ge(*m_pool.done(before, t))
                    decayed(n)
                    added(n)

                to("mv0")
                pool.wait_ge(*m_dve.done("fb", t))
                decayed(0)
                pool.wait_ge(*m_pool.done("mv0", t))
                pool.wait_ge(*m_dve.done("bk", t))
                pool.wait_ge(*m_act.done("v", t))
                if RB:
                    pool.wait_ge(*m_dve.done("oprod", t - 1))
                    pool.wait_ge(*m_pool.done("op", t - 1))
                Hv5 = Hv[:].rearrange("p (i j) n h -> p i j (n h)", i=D1)
                for i, name in ((0, "Ua"), (D1 // 2, "U")):
                    to("Ub" if i else "Ua")
                    rows_ = slice(i, i + D1 // 2)
                    tt(Hv5[:, rows_], bk[:, rows_, :].unsqueeze(2).broadcast_to([P, D1 // 2, D1, SYS]),
                       kv[:, D1:, :].unsqueeze(1).broadcast_to([P, D1 // 2, D1, SYS]), ALU.mult).then_inc(*m_pool.step(name))
                to("hv0")
                added(0)

                def last_rows(k, before):
                    to(f"lr{k}")
                    pool.wait_ge(*m_dve.done(f"col{k}", t))
                    pool.wait_ge(*m_pool.done(before, t))
                    tt(lT, A[:, LOW:, k, :].unsqueeze(2).broadcast_to([P, 2, 3, SYS]),
                       A[:, k, LOW:, :].unsqueeze(1).broadcast_to([P, 2, 3, SYS]), ALU.mult).then_inc(*m_pool.step(f"lt{k}"))
                    pool.wait_ge(*m_pool.done(f"lt{k}", t))
                    tt(A[:, LOW:, LOW:, :], A[:, LOW:, LOW:, :], lT, ALU.subtract).then_inc(*m_pool.step(f"la{k}"))

                v_state(1, "hv0")
                v_state(2, "hv1")
                v_state(3, "hv2")
            if RB:
                to("rootz")
                pool.wait_ge(*in_dve.done("yz", N2))
                root(in_pool, "z", t - 1, ms4[:, 1, :], ms4[:, 0, :])
                to("base")
                pool.wait_ge(res_free, t * 16)
                tt(res[:], x3[:], z[:], ALU.add).then_inc(*in_pool.step("base"))
            if RA:
                for k in range(LOW):
                    last_rows(k, f"la{k - 1}" if k else "hv3")
            to.up_to(UNITS + 4)

        run(pool, turn)

    @block.vector
    def _(dve):
        tt, red = nc.vector.tensor_tensor, nc.vector.tensor_reduce

        def guess(y, a):
            return nc.vector.tensor_scalar(y.bitcast(I32), a.bitcast(I32), -0.5, MAGIC, ALU.mult, ALU.add)

        dve.wait_ge(loaded, LOADED)
        dve.wait_ge(loaded_early, LOADED_EARLY)
        dve.wait_ge(zeroed, ZEROED)
        dve.wait_ge(*su_pe.done("gates"))
        for i in STYLE:
            nc.vector.tensor_scalar(style[:, i, :], ps6[:, i * B:(i + 1) * B], SCALE_C if i == 0 else 1.0, vecs[:, 2 + i:3 + i],
                                    ALU.mult, ALU.add).then_inc(su_dve(f"st{i}"), 1)
        for i in STYLE:
            dve.wait_ge(*su_dve.done(f"st{i}"))
            tt(ssq[:, i, :], style[:, i, :], style[:, i, :], ALU.mult).then_inc(su_dve(f"ssq{i}"), 1)
        for i, w in enumerate((w2c, kwT, owT)):
            tt(wsq[:, i, :], w[:], w[:], ALU.mult).then_inc(su_dve(f"wsq{i}"), 1)
        dve.wait_ge(*su_pe.done("sums"))
        for i in STYLE:
            nc.vector.tensor_scalar(wsq[:, i, :], ps7[:, i * B:(i + 1) * B], 1e-8, None, ALU.add).then_inc(su_dve(f"dem{i}"), 1)
            dve.wait_ge(*su_dve.done(f"dem{i}"))
            guess(demod[:, i, :], wsq[:, i, :]).then_inc(su_dve(f"gs{i}"), 1)
        nc.vector.scalar_tensor_tensor(out=ltmp, in0=rows[:, 1, :], scalar=-1.0, in1=rows[:, 1, :], op0=ALU.mult,
                                       op1=ALU.min).then_inc(su_dve("l0"), 1)
        dve.wait_ge(*su_act.done("ln"))
        nc.vector.scalar_tensor_tensor(out=lam[:], in0=rows[:, 1, :], scalar=0.0, in1=ltmp, op0=ALU.max,
                                       op1=ALU.add).then_inc(su_dve("l1"), 1)
        dve.wait_ge(*su_dve.done("l1"))
        nc.vector.tensor_scalar(lam[:], lam[:], 0.25, None, ALU.add).then_inc(su_dve("l2"), 1)
        nc.vector.tensor_scalar(rows[:, 2, :], rows[:, 2, :], 0.5, None, ALU.mult).then_inc(su_dve("nw"), 1)
        dve.wait_ge(*su_pool.done(f"ud0{ROOTS - 1}"))

        def generated_weights():
            dve.wait_ge(*su_pool.done(f"ud2{ROOTS - 1}"))
            for g, (lo, hi) in enumerate(UG):
                dve.wait_ge(*su_u.done(f"g{g}"))
                tt(Uw[:, lo:hi, :], ps6[:, 0:(hi - lo) * B].rearrange("p (k b) -> p k b", b=B),
                   bdec[:, lo:hi].unsqueeze(2).broadcast_to([P, hi - lo, B]), ALU.add).then_inc(su_v(f"g{g}"), 1)
            dve.wait_ge(*su_pe.done("uw"))
            nc.vector.tensor_scalar(Ub[:], ps6[0:KDEC, 0:B], bdecb[:, 0:1], None, ALU.add).then_inc(su_dve("ub"), 1)

        def ranks(layer, c, vals):
            a = vals.unsqueeze(2).broadcast_to([P, NC, EXPERTS, EXPERTS])
            b = vals.unsqueeze(3).broadcast_to([P, NC, EXPERTS, EXPERTS])
            sq = lambda t: t[:].rearrange("p n (e f) -> p n e f", e=EXPERTS)
            tt(sq(ge), a, b, ALU.subtract).then_inc(*in_dve.step(f"dif{layer}"))
            dve.wait_ge(*in_dve.done(f"dif{layer}", c))
            tt(ge[:], ge[:], bc_n(ahead[:]), ALU.is_ge).then_inc(*in_dve.step(f"cmp{layer}"))
            dve.wait_ge(*in_dve.done(f"cmp{layer}", c))
            red(rank[:], sq(ge), AX, ALU.add).then_inc(*in_dve.step(f"rank{layer}"))
            dve.wait_ge(*in_dve.done(f"rank{layer}", c))

        def turn(t, F, M, RA, RB, G):
            U, K, N2 = t + 2, t + 1, t + 2

            def unit(g):
                if g < UNITS and active(g, F, G):
                    q = g % 2
                    dve.wait_ge(*silu.done(f"s{g}", U))
                    dve.wait_ge(*up.done(f"b{g}", U))
                    wait_unit(dve, down, "d", g, 2, t, G)
                    tt(hid[:, q, :], sil[:, q, :], psU[:, 2 * q + 1, :], ALU.mult).then_inc(*mul.step(f"h{g}", fill("h", g, F)))

            to = Slots(unit)

            def mul_n(out_, in_, per_batch):
                return tt(by_n(out_[:]), by_n(in_), bc_n(per_batch), ALU.mult)

            window = kx[:].rearrange("p n t d -> p n (t d)")

            def shifted(n, count):
                w = window[:, n, 0:D]
                return bass.AP(w.tensor, w.offset, [list(w.ap[0]), [D1, count], [1, D]])

            def score_products(m):
                pr4 = prod[:, 0:2 * OFF * D].rearrange("p (n o x) -> p n o x", n=2, o=OFF)
                for n in range(2):
                    last = tt(pr4[:, n, :, :], window[:, 2 * m + n, 0:D].unsqueeze(1).broadcast_to([P, OFF, D]),
                              shifted(2 * m + n, OFF), ALU.mult)
                last.then_inc(*k_dve.step(f"prod{m}"))

            def score_sums(m):
                dve.wait_ge(*k_dve.done(f"prod{m}", K))
                red(sd[:, 2 * m:2 * m + 2, :, 0, :].rearrange("p n o h -> p (n o) h"),
                    prod[:, 0:2 * OFF * D].rearrange("p (a h d) -> p a h d", h=H1, d=D1), AX, ALU.add).then_inc(*k_dve.step(f"sd{m}"))

            def head_products(n):
                at, count = (HP, HO) if n == NC - 1 else (0, H1)
                tt(prod[:, at:at + count * D].rearrange("p (o h d) -> p o h d", h=H1, d=D1),
                   sf[:, n, 0:count, :].unsqueeze(3).broadcast_to([P, count, H1, D1]), head_windows(n, 0, count), ALU.mult).then_inc(*k_dve.step(f"ap{n}"))

            def head_sums(n):
                dve.wait_ge(*k_dve.done(f"ap{n}", K))
                at = HP if n == NC - 1 else 0
                red(mixed[:, n * D:(n + 1) * D], prod[:, at:at + H1 * D].rearrange("p (o x) -> p x o", o=H1),
                    AX, ALU.add).then_inc(*k_dve.step(f"av{n}"))

            A00 = A[:, 0, 0, 0:1]
            diagonal = bass.AP(A00.tensor, A00.offset, [list(A00.ap[0]), [(D1 + 2) * SYS, D1], [1, SYS]])

            def head_round(n):
                to(f"av{n}")
                if n == NC - 1:
                    dve.wait_ge(*k_pool.done("hp", K))
                head_sums(n)
                if n + 1 < NC:
                    dve.wait_ge(*k_dve.done(f"av{n}", K))
                    head_products(n + 1)

            def eliminate(k):
                to(f"el{k}")
                if k == 0:
                    prev = "diag"
                else:
                    prev = f"a{k - 1}" if k < LOW else f"col{k - 1}"
                dve.wait_ge(*m_dve.done(prev, t))
                if k == LOW:
                    dve.wait_ge(*m_pool.done(f"la{LOW - 1}", t))
                nc.vector.reciprocal(A[:, k, k, :], A[:, k, k, :]).then_inc(*m_dve.step(f"ri{k}"))
                dve.wait_ge(*m_dve.done(f"ri{k}", t))
                tt(A[:, k + 1:, k, :], A[:, k, k + 1:D1, :], A[:, k, k:k + 1, :].broadcast_to([P, D1 - 1 - k, SYS]),
                   ALU.mult).then_inc(*m_dve.step(f"col{k}"))
                if k == LOW or k < LOW - 1:
                    dve.wait_ge(*m_dve.done(f"col{k}", t))
                    at, parts = 0, []
                    for i in range(k + 1, D1 if k == LOW else LOW):
                        w = D1 + 1 - i
                        parts.append((i, T[:, at:at + w, :]))
                        at += w
                        last = tt(parts[-1][1], A[:, k, i:, :], A[:, i, k:k + 1, :].broadcast_to([P, w, SYS]), ALU.mult)
                    last.then_inc(*m_dve.step(f"t{k}"))
                    dve.wait_ge(*m_dve.done(f"t{k}", t))
                    for i, part in parts:
                        last = tt(A[:, i, i:, :], A[:, i, i:, :], part, ALU.subtract)
                    last.then_inc(*m_dve.step(f"a{k}"))

            T4 = prod[:, 0:D1 * D1 * H1].rearrange("p (i j h) -> p i j h", i=D1, h=H1)
            carry4 = carry[:].rearrange("p (i j) h -> p i j h", i=D1)

            def k_state(n):
                to(f"hk{n}")
                dve.wait_ge(*m_dve.done(f"hk{n - 1}" if n else "Uk", t))
                for i, j in UPPER:
                    rows_, cols = i.stop - i.start, j.stop - j.start
                    last = tt(T4[:, i, j], carry4[:, i, j] if n == 0 else A4[:, i, j, n - 1, :],
                              fb[:, n, 0, :].unsqueeze(1).unsqueeze(1).broadcast_to([P, rows_, cols, H1]), ALU.mult)
                last.then_inc(*m_dve.step(f"mk{n}"))
                dve.wait_ge(*m_dve.done(f"mk{n}", t))
                for i, j in UPPER:
                    last = tt(A4[:, i, j, n, :], A4[:, i, j, n, :], T4[:, i, j], ALU.add)
                last.then_inc(*m_dve.step(f"hk{n}"))

            if RB:
                to("back")
                prev = "rhs"
                for k in range(D1 - 1, 0, -1):
                    dve.wait_ge(*m_dve.done(prev, t - 1))
                    tt(T[:, 0:k, :], A[:, k, 0:k, :], A[:, k, D1:D1 + 1, :].broadcast_to([P, k, SYS]), ALU.mult).then_inc(*m_dve.step(f"bt{k}"))
                    dve.wait_ge(*m_dve.done(f"bt{k}", t - 1))
                    tt(A[:, 0:k, D1, :], A[:, 0:k, D1, :], T[:, 0:k, :], ALU.subtract).then_inc(*m_dve.step(f"bx{k}"))
                    prev = f"bx{k}"
            if F:
                to("xm")
                dve.wait_ge(*in_pe.done("x1", N2))
                mul_n(xm, ps7, style[:, 0, :]).then_inc(*in_dve.step("xm"))
            if M:
                to("xk")
                dve.wait_ge(*k_pe.done("x2T", K))
                mul_n(xk, ps6, style[:, 1, :]).then_inc(*k_dve.step("xk"))
            if RB:
                to("oprod")
                dve.wait_ge(*m_dve.done("bx1", t - 1))
                dve.wait_ge(*m_pool.done(f"hv{NC - 1}", t - 1))
                tt(A[:, 0:OWN, 0:D1, :], A[:, 0:OWN, D1, :].unsqueeze(2).broadcast_to([P, OWN, D1, SYS]),
                   Hv[:].rearrange("p (i j) n h -> p i j (n h)", i=D1)[:, 0:OWN], ALU.mult).then_inc(*m_dve.step("oprod"))
            if F:
                to("dm")
                dve.wait_ge(*in_pe.done("y", N2))
                wait_if(dve, up, f"b{UNITS - 1}", U - 1)
                mul_n(yT, ps7, demod[:, 0, :]).then_inc(*in_dve.step("dm"))
                dve.wait_ge(*in_dve.done("dm", N2))
                nc.vector.tensor_scalar(yT[:], yT[:], vecs[:, 0:1], 256.0, ALU.add, ALU.min).then_inc(*in_dve.step("bias"))
                dve.wait_ge(*in_dve.done("bias", N2))
                nc.vector.tensor_scalar(yT[:], yT[:], -256.0, None, ALU.max).then_inc(*in_dve.step("yT"))
            if M:
                to("kx0")
                dve.wait_ge(*k_pe.done("kx", K))
                mul_n(kx0, ps6, demod[:, 1, :]).then_inc(*k_dve.step("kx0"))
            if RB:
                to("o1")
                dve.wait_ge(*m_dve.done("oprod", t - 1))
                dve.wait_ge(*m_pool.done("op", t - 1))
                red(o1[:].rearrange("p (s j) -> p j s", j=D1), A[:, :, 0:D1, :].rearrange("p i j s -> p j s i"), AX, ALU.add).then_inc(*m_dve.step("o1"))
                to("og")
                dve.wait_ge(*m_dve.done("o1", t - 1))
                dve.wait_ge(*m_act.done("gate", t - 1))
                nc.vector.scalar_tensor_tensor(out=o1[:], in0=gate[:], scalar=1.0, in1=o1[:], op0=ALU.add, op1=ALU.mult).then_inc(*m_dve.step("og"))
            if F:
                to("sub0")
                dve.wait_ge(*in_pe.done("r0", N2))
                r = ps7[:, 0:NC * EXPERTS].rearrange("p (n e) -> p n e", n=NC)
                red(m4[:], r, AX, ALU.max).then_inc(*in_dve.step("max0"))
                dve.wait_ge(*in_dve.done("max0", N2))
                tt(s8[:], r, m4[:].unsqueeze(2).broadcast_to([P, NC, EXPERTS]), ALU.subtract).then_inc(*in_dve.step("sub0"))
            if RB:
                to("ss")
                dve.wait_ge(*m_pool.done("sq", t - 1))
                red(ssr[:, 0, :], gate[:].rearrange("p (s j) -> p s j", j=D1), AX, ALU.add).then_inc(*m_dve.step("ss"))
                dve.wait_ge(*m_dve.done("ss", t - 1))
                nc.vector.tensor_scalar(ssr[:, 0, :], ssr[:, 0, :], 1.0 / (4 * D1), 1e-5, ALU.mult, ALU.add).then_inc(*m_dve.step("ao"))
                dve.wait_ge(*m_dve.done("ao", t - 1))
                guess(rn[:, 0, :], ssr[:, 0, :]).then_inc(*m_dve.step("yo"))
            if M:
                to("prod0")
                dve.wait_ge(*k_act.done("kxdup", K))
                score_products(0)
                to("sd0")
                score_sums(0)
            if RB:
                to("ogn")
                dve.wait_ge(*m_pool.done(f"uo{ROOTS - 1}", t - 1))
                o13 = o1[:].rearrange("p (s j) -> p s j", j=D1)
                tt(o13, o13, rn[:, 0, :].unsqueeze(2).broadcast_to([P, SYS, D1]), ALU.mult).then_inc(*m_dve.step("ogn"))
            if M:
                to("prod1")
                dve.wait_ge(*k_dve.done("sd0", K))
                score_products(1)
                to("sd1")
                score_sums(1)
                to("sf1")
                dve.wait_ge(*k_act.done("sf1", K))
                red(mxh[:], sf[:].rearrange("p n o h -> p n h o"), AX, ALU.max).then_inc(*k_dve.step("max"))
                to("sub")
                dve.wait_ge(*k_dve.done("max", K))
                tt(sf[:], sf[:], mxh[:].unsqueeze(2).broadcast_to([P, NC, H1, H1]), ALU.subtract).then_inc(*k_dve.step("sub"))
            if RB:
                to("x3")
                dve.wait_ge(*m_pe.done("x3", t - 1))
                dve.wait_ge(*m_act.done("x2", t - 1))
                if G:
                    dve.wait_ge(*in_pool.done("base", t - 2))
                tt(x3[:], ps6, x2_now[:], ALU.add).then_inc(*m_dve.step("x3"))
            if M:
                to("sum")
                dve.wait_ge(*k_act.done("exp", K))
                red(smh[:], sf[:].rearrange("p n o h -> p n h o"), AX, ALU.add).then_inc(*k_dve.step("sum"))
                dve.wait_ge(*k_dve.done("sum", K))
                nc.vector.reciprocal(rsh[:], smh[:]).then_inc(*k_dve.step("rsum"))
            if F:
                to("probs0")
                dve.wait_ge(*in_act.done("e0", N2))
                red(m4[:], ex8[:], AX, ALU.add).then_inc(*in_dve.step("sum0"))
                dve.wait_ge(*in_dve.done("sum0", N2))
                nc.vector.reciprocal(m4[:], m4[:]).then_inc(*in_dve.step("rsum0"))
                dve.wait_ge(*in_dve.done("rsum0", N2))
                tt(p8[:], ex8[:], m4[:].unsqueeze(2).broadcast_to([P, NC, EXPERTS]), ALU.mult).then_inc(*in_dve.step("probs"))
            if F:
                to("ranks0")
                dve.wait_ge(*in_dve.done("probs", N2))
                ranks(0, N2, p8[:])
                nc.vector.tensor_scalar(rank[:], rank[:], float(TOP_K), TOP_K / (TOP_K + 1.0), ALU.is_lt, ALU.mult).then_inc(*in_dve.step("rk2"))
                dve.wait_ge(*in_dve.done("rk2", N2))
                wait_if(dve, acc, f"x{UNITS // 2 - 1}", U - 1)
                tt(cw0[:, :, 0:EXPERTS], rank[:], p8[:], ALU.mult).then_inc(*in_dve.step("cw0", None if RB else "cw1"))
            if M:
                to("ap0")
                dve.wait_ge(*k_pool.done("probs", K))
                head_products(0)
                head_round(0)
                head_round(1)
            if RA:
                to("ssq")
                for i, name in enumerate("qk"):
                    dve.wait_ge(*m_act.done("sq" + name, t))
                    red(ssr[:, i, :], sqr[i][:].rearrange("p (s j) -> p s j", j=D1), AX, ALU.add).then_inc(*m_dve.step("ss" + name))
                dve.wait_ge(*m_dve.done("ssk", t))
                nc.vector.tensor_scalar(ssr[:], ssr[:], 1e-6, None, ALU.add).then_inc(*m_dve.step("aq"))
                dve.wait_ge(*m_dve.done("aq", t))
                guess(rn[:], ssr[:]).then_inc(*m_dve.step("yq"))
            if M:
                head_round(2)
            if RA:
                to("fb0")
                dve.wait_ge(*m_pe.done("fb", t))
                tt(fb0[:], ps6[:, 0:NC * 2 * H1].rearrange("p (n t h) -> p n t h", n=NC, t=2), bc_n(fbias[:]).rearrange("p n (t h) -> p n t h", t=2),
                   ALU.add).then_inc(*m_dve.step("fb0"))
            if M:
                head_round(3)
            if RA:
                to("fb1")
                dve.wait_ge(*m_act.done("fbt", t))
                nc.vector.tensor_scalar(fb[:], fbt[:], 0.5, 0.5, ALU.mult, ALU.add).then_inc(*m_dve.step("fb"))
                to("qk")
                dve.wait_ge(*m_pool.done(f"uq{ROOTS - 1}", t))
                for i, name in enumerate("qk"):
                    dve.wait_ge(*m_act.done(name, t))
                    dst = A[:, :, D1, :] if i == 0 else kv[:, 0:D1, :]
                    tt(dst, dst, rn[:, i, :].unsqueeze(1).broadcast_to([P, D1, SYS]), ALU.mult).then_inc(*m_dve.step(name))
                dve.wait_ge(*m_dve.done("k", t))
                dve.wait_ge(*m_dve.done("fb", t))
                tt(bk[:].rearrange("p j (n h) -> p j n h", n=NC), kv[:, 0:D1, :].rearrange("p j (n h) -> p j n h", n=NC),
                   fb[:, :, 1, :].unsqueeze(1).broadcast_to([P, D1, NC, H1]), ALU.mult).then_inc(*m_dve.step("bk"))
                to("Uk")
                dve.wait_ge(*m_dve.done("bk", t))
                if RB:
                    dve.wait_ge(*m_act.done("carry_k", t - 1))
                if M:
                    dve.wait_ge(*k_dve.done(f"av{NC - 1}", K))
                for i, j in UPPER:
                    shape = [P, i.stop - i.start, j.stop - j.start, SYS]
                    last = tt(A[:, i, j, :], bk[:, i, :].unsqueeze(2).broadcast_to(shape), kv[:, j, :].unsqueeze(1).broadcast_to(shape), ALU.mult)
                last.then_inc(*m_dve.step("Uk"))
                k_state(0)
            if M:
                to("xo")
                dve.wait_ge(*k_pe.done("oT", K))
                mul_n(xk, ps6, style[:, 2, :]).then_inc(*k_dve.step("xo"))
            if RA:
                k_state(1)
            if RB:
                to("t")
                dve.wait_ge(*in_pe.done(f"t{TG - 1}", N2))
                tt(tK[:].rearrange("k n b -> k b n"), ps7[0:KDEC, :].rearrange("k (b n) -> k b n", n=NC),
                   Ub[:].unsqueeze(2).broadcast_to([KDEC, B, NC]), ALU.add).then_inc(*in_dve.step("t"))
            if RA:
                k_state(2)
            if M:
                to("y1")
                dve.wait_ge(*k_pe.done("y", K))
                mul_n(kx0, ps6, demod[:, 2, :]).then_inc(*k_dve.step("y1"))
            if RA:
                k_state(3)
                to("diag")
                dve.wait_ge(*m_act.done("carry_k", t))
                diag4 = diagonal.rearrange("p i (n h) -> p i n h", n=NC)
                tt(diag4, diag4, lam[:].rearrange("p (h i) -> p i h", h=H1).unsqueeze(2).broadcast_to([P, D1, NC, H1]), ALU.add).then_inc(*m_dve.step("diag"))
                eliminate(0)
            if RB:
                to("ms")
                dve.wait_ge(*in_act.done("zsq", N2))
                red(ms4[:, 0, :], by_n(zn[:]), AX, ALU.add).then_inc(*in_dve.step("ms"))
                dve.wait_ge(*in_dve.done("ms", N2))
                nc.vector.tensor_scalar(ms4[:, 0, :], ms4[:, 0, :], 1.0 / D, 1e-6, ALU.mult, ALU.add).then_inc(*in_dve.step("me"))
                dve.wait_ge(*in_dve.done("me", N2))
                guess(ms4[:, 1, :], ms4[:, 0, :]).then_inc(*in_dve.step("yz"))
            if RA:
                eliminate(1)
                eliminate(2)
                eliminate(3)
                eliminate(4)
            if RB:
                to("sub1")
                dve.wait_ge(*in_pe.done("r1", N2))
                r = ps7[:, 0:NC * EXPERTS].rearrange("p (n e) -> p n e", n=NC)
                red(m4[:], r, AX, ALU.max).then_inc(*in_dve.step("max1"))
                dve.wait_ge(*in_dve.done("max1", N2))
                tt(s8[:], r, m4[:].unsqueeze(2).broadcast_to([P, NC, EXPERTS]), ALU.subtract).then_inc(*in_dve.step("sub1"))
                dve.wait_ge(*in_dve.done("sub1", N2))
                nc.vector.tensor_copy(p8[:], r).then_inc(*in_dve.step("raw"))
            if RA:
                eliminate(5)
            if RB:
                to("ranks1")
                dve.wait_ge(*in_dve.done("raw", N2))
                ranks(1, N2, p8[:])
                to("cw1")
                dve.wait_ge(*in_act.done("e1", N2))
                nc.vector.scalar_tensor_tensor(out=cw1[:], in0=rank[:], scalar=float(TOP_K), in1=ex8[:], op0=ALU.is_lt,
                                               op1=ALU.mult).then_inc(*in_dve.step("em"))
                dve.wait_ge(*in_dve.done("em", N2))
                red(m4[:], cw1[:], AX, ALU.add).then_inc(*in_dve.step("sum1"))
                dve.wait_ge(*in_dve.done("sum1", N2))
                nc.vector.reciprocal(m4[:], m4[:]).then_inc(*in_dve.step("rsum1"))
                dve.wait_ge(*in_dve.done("rsum1", N2))
                tt(cw1[:], cw1[:], m4[:].unsqueeze(2).broadcast_to([P, NC, EXPERTS]), ALU.mult).then_inc(*in_dve.step("cw1"))
            if RA:
                eliminate(6)
                dve.wait_ge(*m_dve.done("a6", t))
                k = D1 - 1
                nc.vector.reciprocal(A[:, k, k, :], A[:, k, k, :]).then_inc(*m_dve.step(f"ri{k}"))
                to("rhs")
                dve.wait_ge(*m_dve.done(f"ri{k}", t))
                tt(A[:, :, D1, :], A[:, :, D1, :], diagonal, ALU.mult).then_inc(*m_dve.step("rhs"))
            to.up_to(UNITS + 2)

        run(dve, turn, generated_weights)


def layouts(inp):
    f = lambda k: np.asarray(inp[k])
    a = {}
    x = f("x")
    inv = 1.0 / 10000.0 ** (np.arange(0, HD, 2, dtype=np.float32) / HD)
    ang = np.tile(np.arange(N, dtype=np.float32)[:, None] * inv[None, :], (GB, 1))
    a["cos"] = np.concatenate([np.cos(ang)] * 2, 1)
    a["sin"] = np.concatenate([-np.sin(ang), np.sin(ang)], 1)
    a["fold"] = np.tile(np.eye(AH, dtype=np.float32), (2, 1))
    a["ident"] = np.eye(P, dtype=np.float32)
    e = np.arange(EXPERTS)
    limits = np.finfo(np.float32)
    lead = np.where(e[None, :] < e[:, None], 0.0, np.where(e[None, :] > e[:, None], limits.tiny, limits.max))
    a["ahead"] = np.tile(lead.astype(np.float32).reshape(1, -1), (P, 1))
    a["xT"] = x.reshape(TOK, D).T
    a["condT"] = f("cond_512").T
    a["dgb"] = np.concatenate([f("L0_cond_down_gamma"), f("L0_cond_down_beta")], 1)
    a["ugb"] = np.stack([f("L0_cond_up_gamma"), f("L0_cond_up_beta")], 1)
    a["down"], a["up"] = f("L0_cond_down_project"), f("L0_cond_up_project")
    a["ln_gb"] = np.stack([f("L0_attn_ln_gamma"), f("L0_attn_ln_beta")], 1)
    a["b_out"] = np.tile(f("L0_attn_b_out")[None], (P, 1))
    a["x"] = x.reshape(TOK, D)
    a["w_qkv"] = f("L0_attn_w_qkv")
    a["w_out"] = f("L0_attn_w_out").reshape(PAIRS, P, D).transpose(1, 0, 2)
    a["w2c"] = f("L0_cond2_weight").T
    a["vecs"] = np.stack([f("L0_cond2_bias"), f("L1_cond_o_b"), f("L0_cond2_affine_b"), f("L1_cond_k_aff_b"),
                          f("L1_cond_o_aff_b"), f("L1_ffn_norm_scale")], 1)
    a["w_r0"], a["w_r1"] = f("L0_ffn_w_router"), f("L1_ffn_w_router").T
    w1 = np.concatenate([f("L0_ffn_w1"), f("L0_ffn_ws1")[None]])
    w3 = np.concatenate([f("L0_ffn_w3"), f("L0_ffn_ws3")[None]])
    w2 = np.concatenate([f("L0_ffn_w2"), f("L0_ffn_ws2")[None]])
    a["w13"] = np.stack([w1, w3], 2).transpose(1, 0, 2, 3)
    a["w2"] = w2.reshape(EX0, 2, P, D).transpose(2, 0, 1, 3)
    a["aff"] = np.stack([f("L0_cond2_affine_w").T, f("L1_cond_k_aff_w").T, f("L1_cond_o_aff_w").T], 1)
    a["kwT"], a["owT"] = f("L1_cond_k_w").T, f("L1_cond_o_w").T
    a["wqkv1"] = np.stack([f("L1_attn_Wq"), f("L1_attn_Wk"), f("L1_attn_Wv")], 1)
    a["wfb"] = np.concatenate([f("L1_attn_Wf"), f("L1_attn_Wbet")], 1)
    a["wo1"], a["g1"], a["g2"] = f("L1_attn_Wo"), f("L1_attn_gate_w1"), f("L1_attn_gate_w2")
    a["rows"] = np.tile(np.stack([f("L1_cond_k_b"), f("L1_attn_lamb_params"), f("L1_attn_norm_weight")])[None], (P, 1, 1))
    a["fbias"] = np.tile(np.concatenate([f("L1_attn_delta"), np.zeros(H1, np.float32)])[None], (P, 1))
    a["wdec"] = f("L1_cond2_W_dec")
    b = f("L1_cond2_b_dec").reshape(D + 1, KDEC)
    a["bdec"], a["bdecb"] = b[:D], b[D][:, None]
    a["vmat"] = f("L1_cond2_V")
    a["w_up1"] = f("L1_ffn_w_up").transpose(2, 0, 1)
    a["w_dn1"] = f("L1_ffn_w_down").transpose(0, 2, 1).reshape(EXPERTS, 2, P, D).transpose(2, 0, 1, 3)
    return {k: np.ascontiguousarray(v) for k, v in a.items()}


def block_pair(nc, dram, x1, out):
    with ExitStack() as both:
        loaded = both.enter_context(nc.semaphore("mixing_weights"))
        w = weight_tiles(nc, both)

        def load_weights(sp):
            for name, tile in w.items():
                sp.dma_start(tile[:], dram[name]).then_inc(loaded, 16)

        with ExitStack() as ctx:
            attention_phase(nc, ctx, dram, x1, load_weights)
        with ExitStack() as ctx:
            mixing_phase(nc, ctx, dram, w, loaded, x1.rearrange("(b n) d -> b (n d)", b=B), out)


def kernel(**inputs):
    import concourse.bacc as bacc
    from concourse.bass_utils import run_bass_kernel_spmd

    nc = bacc.Bacc("TRN2", target_bir_lowering=False, num_devices=1)
    arrays = layouts(inputs)
    dram = {name: nc.dram_tensor(name, a.shape, F32, kind="ExternalInput").ap() for name, a in arrays.items()}
    x1 = nc.dram_tensor("x1", (TOK, D), F32, kind="Internal").ap()
    out = nc.dram_tensor("out", (B, N * D), F32, kind="ExternalOutput").ap()
    block_pair(nc, dram, x1, out)
    r = run_bass_kernel_spmd(nc, [arrays], core_ids=[0])
    return np.asarray(r.results[0]["out"]).reshape(B, N, D)
```
